# Optimizing a Trainium2 kernel written in Bass

```python
import numpy as np
import jax
import jax.numpy as jnp

def _softmax(x, axis=-1):
    return jax.nn.softmax(x, axis=axis)

def _gelu(x):
    return jax.nn.gelu(x, approximate=True)

def _silu(x):
    return jax.nn.silu(x)

def _sigmoid(x):
    return jax.nn.sigmoid(x)

def _layernorm(x, axis=-1, eps=1e-05):
    m = jnp.mean(x, axis=axis, keepdims=True)
    v = jnp.var(x, axis=axis, keepdims=True)
    return (x - m) / jnp.sqrt(v + eps)

def _scatter_add(tgt, idx, src, axis=0):
    return tgt.at[idx].add(src)

def _segment_sum(src, seg, n):
    return jax.ops.segment_sum(src, seg, n)
kernel_name = 'mk_prb_d2_jaxref_r8_28e499'

def setup_inputs(seed: int=0):
    np.random.seed(seed)
    _w = jnp.asarray

    def _L0_attn_setup():
        import jax, jax.numpy as jnp
        import numpy as np
        EPS = 1e-05

        def rmsnorm(x, w):
            var = jnp.mean(x * x, axis=-1, keepdims=True)
            return x * jax.lax.rsqrt(var + EPS) * w

        def _mamba_block(x, rms_w, in_proj, conv_w, conv_b, x_proj, dt_w, dt_b, A_log, D, out_proj):
            B, L, dim = x.shape
            d_inner, K = conv_w.shape
            d_state = A_log.shape[1]
            dt_rank = dt_w.shape[0]
            xn = rmsnorm(x, rms_w)
            xz = xn @ in_proj
            xi, z = jnp.split(xz, 2, axis=-1)
            xc = jax.lax.conv_general_dilated(xi.transpose(0, 2, 1), conv_w[:, None, :], window_strides=(1,), padding=[(K - 1, 0)], feature_group_count=d_inner).transpose(0, 2, 1) + conv_b
            xi = jax.nn.silu(xc)
            dbc = xi @ x_proj
            dt, Bm, Cm = jnp.split(dbc, [dt_rank, dt_rank + d_state], axis=-1)
            delta = jax.nn.softplus(dt @ dt_w + dt_b)
            A = -jnp.exp(A_log)

            def step(h, inputs):
                d_t, x_t, B_t, C_t = inputs
                dA = jnp.exp(d_t[..., None] * A)
                h = dA * h + (d_t * x_t)[..., None] * B_t[:, None, :]
                y = jnp.einsum('bds,bs->bd', h, C_t)
                return (h, y)
            h0 = jnp.zeros((B, d_inner, d_state), x.dtype)
            xs = (delta.transpose(1, 0, 2), xi.transpose(1, 0, 2), Bm.transpose(1, 0, 2), Cm.transpose(1, 0, 2))
            _, ys = jax.lax.scan(step, h0, xs)
            y = ys.transpose(1, 0, 2) + xi * D
            y = y * jax.nn.silu(z)
            return x + y @ out_proj
        key = jax.random.key(seed)
        B, L, dim = (4, 256, 128)
        d_inner, d_state, d_conv, dt_rank = (2 * dim, 16, 4, dim // 16)
        ks = jax.random.split(key, 8)
        g = lambda k, shape, scale: jax.random.normal(k, shape, jnp.float32) * scale
        return {'x': g(ks[0], (B, L, dim), 1.0), 'rms_w': jnp.ones((dim,), jnp.float32), 'in_proj': g(ks[1], (dim, 2 * d_inner), dim ** (-0.5)), 'conv_w': g(ks[2], (d_inner, d_conv), 0.25), 'conv_b': jnp.zeros((d_inner,), jnp.float32), 'x_proj': g(ks[3], (d_inner, dt_rank + 2 * d_state), d_inner ** (-0.5)), 'dt_w': g(ks[4], (dt_rank, d_inner), dt_rank ** (-0.5)), 'dt_b': jnp.full((d_inner,), float(np.log(np.expm1(0.01))), jnp.float32), 'A_log': jnp.log(jnp.broadcast_to(jnp.arange(1, d_state + 1, dtype=jnp.float32), (d_inner, d_state))).copy(), 'D': jnp.ones((d_inner,), jnp.float32), 'out_proj': g(ks[5], (d_inner, dim), d_inner ** (-0.5))}
    _L0_attn_in = _L0_attn_setup()

    def _L0_ffn_setup():
        import jax, jax.numpy as jnp
        import numpy as np
        TOP_P = 0.8
        B, T, H, F, E = (2, 256, 128, 512, 8)
        key = jax.random.key(seed)
        k0, k1, k2, k3 = jax.random.split(key, 4)
        x = jax.random.normal(k0, (B, T, H), jnp.float32)
        Wr = jax.random.normal(k1, (H, E), jnp.float32) * 0.02
        br = jnp.zeros((E,), jnp.float32)
        W1 = jax.random.normal(k2, (E, H, F), jnp.float32) * 0.02
        b1 = jnp.zeros((E, F), jnp.float32)
        W2 = jax.random.normal(k3, (E, F, H), jnp.float32) * 0.02
        b2 = jnp.zeros((E, H), jnp.float32)
        return {'x': x, 'Wr': Wr, 'br': br, 'W1': W1, 'b1': b1, 'W2': W2, 'b2': b2}
    _L0_ffn_in = _L0_ffn_setup()

    def _L1_attn_setup():
        import jax, jax.numpy as jnp
        import numpy as np
        import math
        B, T, C = (2, 256, 128)
        H, L = (16, 64)
        DH = C // H
        DHE = DH // 2
        THETA = 10000.0

        def _rope_cache(t, dim):
            inv_freq = 1.0 / THETA ** (jnp.arange(0, dim, 2, dtype=jnp.float32) / dim)
            freqs = jnp.arange(t, dtype=jnp.float32)[:, None] * inv_freq[None, :]
            emb = jnp.concatenate((freqs, freqs), axis=-1)
            return (jnp.cos(emb), jnp.sin(emb))

        def _apply_rope(x, cos, sin):
            x1 = x[..., 0::2]
            x2 = x[..., 1::2]
            rot = jnp.stack((-x2, x1), axis=-1).reshape(x.shape)
            return x * cos[None, None] + rot * sin[None, None]
        key = jax.random.key(seed)
        ks = jax.random.split(key, 10)
        s = 0.02
        return {'x': jax.random.normal(ks[0], (B, T, C), jnp.float32), 'Wq_down': jax.random.normal(ks[1], (C, H * L), jnp.float32) * s, 'Wk_down': jax.random.normal(ks[2], (C, H * L), jnp.float32) * s, 'Wv_down': jax.random.normal(ks[3], (C, H * L), jnp.float32) * s, 'Wq_up_c': jax.random.normal(ks[4], (L, DHE), jnp.float32) * s, 'Wq_up_e': jax.random.normal(ks[5], (L, DHE), jnp.float32) * s, 'Wk_up_c': jax.random.normal(ks[6], (L, DHE), jnp.float32) * s, 'Wk_up_e': jax.random.normal(ks[7], (L, DHE), jnp.float32) * s, 'Wv_up': jax.random.normal(ks[8], (L, DH), jnp.float32) * s, 'Wc': jax.random.normal(ks[9], (C, C), jnp.float32) * s}
    _L1_attn_in = _L1_attn_setup()

    def _L1_ffn_setup():
        import jax, jax.numpy as jnp
        import numpy as np
        E = 128
        D = 128
        C = 32
        key = jax.random.key(seed)
        kx, kg, ke = jax.random.split(key, 3)
        x = jax.random.normal(kx, (4, 256, D), dtype=jnp.float32)
        wg = jax.random.normal(kg, (D, E), dtype=jnp.float32) * 0.02
        we = jax.random.normal(ke, (E, D, D), dtype=jnp.float32) * 0.02
        return {'x': x, 'wg': wg, 'we': we}
    _L1_ffn_in = _L1_ffn_setup()
    _d = {'L0_attn_x': _L0_attn_in['x'], 'L0_attn_rms_w': _L0_attn_in['rms_w'], 'L0_attn_in_proj': _L0_attn_in['in_proj'], 'L0_attn_conv_w': _L0_attn_in['conv_w'], 'L0_attn_conv_b': _L0_attn_in['conv_b'], 'L0_attn_x_proj': _L0_attn_in['x_proj'], 'L0_attn_dt_w': _L0_attn_in['dt_w'], 'L0_attn_dt_b': _L0_attn_in['dt_b'], 'L0_attn_A_log': _L0_attn_in['A_log'], 'L0_attn_D': _L0_attn_in['D'], 'L0_attn_out_proj': _L0_attn_in['out_proj'], 'L0_ffn_Wr': _L0_ffn_in['Wr'], 'L0_ffn_br': _L0_ffn_in['br'], 'L0_ffn_W1': _L0_ffn_in['W1'], 'L0_ffn_b1': _L0_ffn_in['b1'], 'L0_ffn_W2': _L0_ffn_in['W2'], 'L0_ffn_b2': _L0_ffn_in['b2'], 'L1_attn_Wq_down': _L1_attn_in['Wq_down'], 'L1_attn_Wk_down': _L1_attn_in['Wk_down'], 'L1_attn_Wv_down': _L1_attn_in['Wv_down'], 'L1_attn_Wq_up_c': _L1_attn_in['Wq_up_c'], 'L1_attn_Wq_up_e': _L1_attn_in['Wq_up_e'], 'L1_attn_Wk_up_c': _L1_attn_in['Wk_up_c'], 'L1_attn_Wk_up_e': _L1_attn_in['Wk_up_e'], 'L1_attn_Wv_up': _L1_attn_in['Wv_up'], 'L1_attn_Wc': _L1_attn_in['Wc'], 'L1_ffn_wg': _L1_ffn_in['wg'], 'L1_ffn_we': _L1_ffn_in['we']}
    _x0 = _d['L0_attn_x']
    _d['L0_attn_x'] = jax.random.normal(jax.random.fold_in(jax.random.key(seed), 1), (32, 256, 128), dtype=_x0.dtype)
    del _x0
    return _d

def reference(L0_attn_x, L0_attn_rms_w, L0_attn_in_proj, L0_attn_conv_w, L0_attn_conv_b, L0_attn_x_proj, L0_attn_dt_w, L0_attn_dt_b, L0_attn_A_log, L0_attn_D, L0_attn_out_proj, L0_ffn_Wr, L0_ffn_br, L0_ffn_W1, L0_ffn_b1, L0_ffn_W2, L0_ffn_b2, L1_attn_Wq_down, L1_attn_Wk_down, L1_attn_Wv_down, L1_attn_Wq_up_c, L1_attn_Wq_up_e, L1_attn_Wk_up_c, L1_attn_Wk_up_e, L1_attn_Wv_up, L1_attn_Wc, L1_ffn_wg, L1_ffn_we):

    def _L0_attn_ref(x, rms_w, in_proj, conv_w, conv_b, x_proj, dt_w, dt_b, A_log, D, out_proj):
        import jax, jax.numpy as jnp
        import numpy as np
        EPS = 1e-05

        def rmsnorm(x, w):
            var = jnp.mean(x * x, axis=-1, keepdims=True)
            return x * jax.lax.rsqrt(var + EPS) * w

        def _mamba_block(x, rms_w, in_proj, conv_w, conv_b, x_proj, dt_w, dt_b, A_log, D, out_proj):
            B, L, dim = x.shape
            d_inner, K = conv_w.shape
            d_state = A_log.shape[1]
            dt_rank = dt_w.shape[0]
            xn = rmsnorm(x, rms_w)
            xz = xn @ in_proj
            xi, z = jnp.split(xz, 2, axis=-1)
            xc = jax.lax.conv_general_dilated(xi.transpose(0, 2, 1), conv_w[:, None, :], window_strides=(1,), padding=[(K - 1, 0)], feature_group_count=d_inner).transpose(0, 2, 1) + conv_b
            xi = jax.nn.silu(xc)
            dbc = xi @ x_proj
            dt, Bm, Cm = jnp.split(dbc, [dt_rank, dt_rank + d_state], axis=-1)
            delta = jax.nn.softplus(dt @ dt_w + dt_b)
            A = -jnp.exp(A_log)

            def step(h, inputs):
                d_t, x_t, B_t, C_t = inputs
                dA = jnp.exp(d_t[..., None] * A)
                h = dA * h + (d_t * x_t)[..., None] * B_t[:, None, :]
                y = jnp.einsum('bds,bs->bd', h, C_t)
                return (h, y)
            h0 = jnp.zeros((B, d_inner, d_state), x.dtype)
            xs = (delta.transpose(1, 0, 2), xi.transpose(1, 0, 2), Bm.transpose(1, 0, 2), Cm.transpose(1, 0, 2))
            _, ys = jax.lax.scan(step, h0, xs)
            y = ys.transpose(1, 0, 2) + xi * D
            y = y * jax.nn.silu(z)
            return x + y @ out_proj
        return _mamba_block(x, rms_w, in_proj, conv_w, conv_b, x_proj, dt_w, dt_b, A_log, D, out_proj)

    def _L0_ffn_ref(x, Wr, br, W1, b1, W2, b2):
        import jax, jax.numpy as jnp
        import numpy as np
        TOP_P = 0.8
        B, T, H, F, E = (2, 256, 128, 512, 8)
        probs = jax.nn.softmax(x @ Wr + br, axis=-1)
        sorted_idx = jnp.argsort(-probs, axis=-1)
        sorted_probs = jnp.take_along_axis(probs, sorted_idx, axis=-1)
        cum = jnp.cumsum(sorted_probs, axis=-1)
        mask = cum < TOP_P
        mask = mask.at[..., 0].set(True)
        inv = jnp.argsort(sorted_idx, axis=-1)
        keep = jnp.take_along_axis(mask, inv, axis=-1)
        gate = probs * keep
        h = jax.nn.relu(jnp.einsum('bth,ehf->betf', x, W1) + b1[None, :, None, :])
        y = jnp.einsum('betf,efh->beth', h, W2) + b2[None, :, None, :]
        return jnp.einsum('bte,beth->bth', gate, y)

    def _L1_attn_ref(x, Wq_down, Wk_down, Wv_down, Wq_up_c, Wq_up_e, Wk_up_c, Wk_up_e, Wv_up, Wc):
        import jax, jax.numpy as jnp
        import numpy as np
        import math
        B, T, C = (2, 256, 128)
        H, L = (16, 64)
        DH = C // H
        DHE = DH // 2
        THETA = 10000.0

        def _rope_cache(t, dim):
            inv_freq = 1.0 / THETA ** (jnp.arange(0, dim, 2, dtype=jnp.float32) / dim)
            freqs = jnp.arange(t, dtype=jnp.float32)[:, None] * inv_freq[None, :]
            emb = jnp.concatenate((freqs, freqs), axis=-1)
            return (jnp.cos(emb), jnp.sin(emb))

        def _apply_rope(x, cos, sin):
            x1 = x[..., 0::2]
            x2 = x[..., 1::2]
            rot = jnp.stack((-x2, x1), axis=-1).reshape(x.shape)
            return x * cos[None, None] + rot * sin[None, None]
        b, t, c = x.shape
        q_lat = (x @ Wq_down).reshape(b, t, H, L)
        k_lat = (x @ Wk_down).reshape(b, t, H, L)
        v_lat = (x @ Wv_down).reshape(b, t, H, L)
        q_c = jnp.einsum('bthl,ld->bhtd', q_lat, Wq_up_c)
        q_e = jnp.einsum('bthl,ld->bhtd', q_lat, Wq_up_e)
        k_c = jnp.einsum('bthl,ld->bhtd', k_lat, Wk_up_c)
        k_e = jnp.einsum('bthl,ld->bhtd', k_lat, Wk_up_e)
        v = jnp.einsum('bthl,ld->bhtd', v_lat, Wv_up)
        cos, sin = _rope_cache(t, DHE)
        q = jnp.concatenate([q_c, _apply_rope(q_e, cos, sin)], axis=-1)
        k = jnp.concatenate([k_c, _apply_rope(k_e, cos, sin)], axis=-1)
        scale = 1.0 / math.sqrt(DH)
        scores = jnp.einsum('bhqd,bhkd->bhqk', q, k) * scale
        causal = jnp.tril(jnp.ones((t, t), dtype=bool))
        scores = jnp.where(causal[None, None], scores, -jnp.inf)
        att = jax.nn.softmax(scores, axis=-1)
        y = jnp.einsum('bhqk,bhkd->bhqd', att, v)
        y = y.transpose(0, 2, 1, 3).reshape(b, t, c)
        return y @ Wc

    def _L1_ffn_ref(x, wg, we):
        import jax, jax.numpy as jnp
        import numpy as np
        E = 128
        D = 128
        C = 32
        B, S, d = x.shape
        xt = x.reshape(-1, d)
        T = xt.shape[0]
        logits = xt @ wg
        gates = jax.nn.softmax(logits, axis=-1)
        e1 = jnp.argmax(gates, axis=-1)
        mask1 = jax.nn.one_hot(e1, E, dtype=logits.dtype)
        logits2 = jnp.where(mask1 > 0, -jnp.inf, logits)
        e2 = jnp.argmax(logits2, axis=-1)
        mask2 = jax.nn.one_hot(e2, E, dtype=logits.dtype)
        g1 = jnp.take_along_axis(gates, e1[:, None], 1)[:, 0]
        g2 = jnp.take_along_axis(gates, e2[:, None], 1)[:, 0]
        denom = jnp.maximum(g1 + g2, jnp.finfo(gates.dtype).eps)
        g1, g2 = (g1 / denom, g2 / denom)
        loc1 = jnp.take_along_axis(jnp.cumsum(mask1, axis=0), e1[:, None], 1)[:, 0].astype(jnp.int32) - 1
        counts1 = mask1.sum(axis=0)
        loc2 = (jnp.take_along_axis(jnp.cumsum(mask2, axis=0), e2[:, None], 1)[:, 0] + counts1[e2]).astype(jnp.int32) - 1
        v1 = (loc1 < C).astype(xt.dtype)
        v2 = (loc2 < C).astype(xt.dtype)
        idx1 = e1.astype(jnp.int32) * C + jnp.minimum(loc1, C - 1)
        idx2 = e2.astype(jnp.int32) * C + jnp.minimum(loc2, C - 1)
        buf = jnp.zeros((E * C, d), dtype=xt.dtype)
        buf = buf.at[idx1].add(xt * v1[:, None])
        buf = buf.at[idx2].add(xt * v2[:, None])
        yb = jnp.einsum('ecd,edf->ecf', buf.reshape(E, C, d), we).reshape(E * C, d)
        y = (g1 * v1)[:, None] * yb[idx1] + (g2 * v2)[:, None] * yb[idx2]
        return y.reshape(B, S, d)
    x = L0_attn_x
    xn = _layernorm(x, axis=-1)
    x = x + _L0_attn_ref(xn, L0_attn_rms_w, L0_attn_in_proj, L0_attn_conv_w, L0_attn_conv_b, L0_attn_x_proj, L0_attn_dt_w, L0_attn_dt_b, L0_attn_A_log, L0_attn_D, L0_attn_out_proj) + _L0_ffn_ref(xn, L0_ffn_Wr, L0_ffn_br, L0_ffn_W1, L0_ffn_b1, L0_ffn_W2, L0_ffn_b2)
    xn = _layernorm(x, axis=-1)
    x = x + _L1_attn_ref(xn, L1_attn_Wq_down, L1_attn_Wk_down, L1_attn_Wv_down, L1_attn_Wq_up_c, L1_attn_Wq_up_e, L1_attn_Wk_up_c, L1_attn_Wk_up_e, L1_attn_Wv_up, L1_attn_Wc) + _L1_ffn_ref(xn, L1_ffn_wg, L1_ffn_we)
    return x

_drawn_inputs = setup_inputs


def setup_inputs(seed=0):
    import zlib

    import numpy as np

    out = dict(_drawn_inputs(seed))
    spreads = {'L0_attn_rms_w': (1.0, 0.2),
     'L0_attn_conv_b': (0.0, 0.367),
     'L0_attn_dt_b': (-4.600165843963623, 0.6),
     'L0_attn_D': (1.0, 0.6),
     'L0_ffn_br': (0.0, 2.0),
     'L0_ffn_b1': (0.0, 2.0),
     'L0_ffn_b2': (0.0, 2.0)}
    factors = {'L0_attn_x_proj': 8.0,
     'L0_attn_dt_w': 8.0,
     'L0_attn_A_log': 8.0,
     'L0_ffn_Wr': 33.712,
     'L0_ffn_W1': 36.256,
     'L0_ffn_W2': 25.022,
     'L1_attn_Wq_down': 8.0,
     'L1_attn_Wk_down': 8.0,
     'L1_attn_Wv_down': 8.0,
     'L1_attn_Wq_up_c': 22.096,
     'L1_attn_Wq_up_e': 21.637,
     'L1_attn_Wk_up_c': 21.974,
     'L1_attn_Wk_up_e': 8.0,
     'L1_attn_Wv_up': 8.0,
     'L1_attn_Wc': 8.0,
     'L1_ffn_wg': 64.0,
     'L1_ffn_we': 64.0}
    for name, (base, spread) in spreads.items():
        noise = np.random.default_rng([zlib.crc32(name.encode()), seed]).standard_normal(out[name].shape)
        drawn = base * np.exp(spread * noise) if base else spread * noise
        out[name] = jnp.asarray(drawn.astype(out[name].dtype))
    for name, factor in factors.items():
        out[name] = (out[name] * factor).astype(out[name].dtype)
    return out
```

```python
from contextlib import ExitStack

import numpy as np

import concourse.bass as bass
from concourse import mybir

F32 = mybir.dt.float32
BF16 = mybir.dt.bfloat16
ALU = mybir.AluOpType
ACT = mybir.ActivationFunctionType
AX = mybir.AxisListType

P = 128
NTOK = 32 * 256
NT = NTOK // P
D = 128
L = 256
EPS = 1e-5

T0 = 512
J0 = T0 // P
IT0 = NTOK // T0
HALF = 2
S = 16
RANK = 8
E0 = 8
FB = 4
TOP_P = 0.8


class Signal:

    def __init__(self, sem, per):
        self.sem, self.per = sem, per

    def at(self, c, k):
        return c * self.per + (2 * self.per + k)


def layer0(nc, ctx, t, dram):
    def sb(name, shape, dt=F32):
        return ctx.enter_context(nc.sbuf_tensor(name, shape, dt))

    def signal(name, per):
        return Signal(ctx.enter_context(nc.semaphore(name)), per)

    def sem(name):
        return ctx.enter_context(nc.semaphore(name))

    X = t["X"]
    ident, identb = t["ident"], t["identb"]
    inproj = sb("inproj", [P, 4 * P]); rmsw = sb("rmsw", [P, 1])
    convw = sb("convw", [P, HALF, 4]); convb = sb("convb", [P, HALF])
    xproj = sb("xproj", [P, HALF, 104]); dtw = sb("dtw", [P, HALF * P]); dtb = sb("dtb", [P, HALF])
    A = sb("A", [P, HALF, S]); Dp = sb("Dp", [P, HALF]); outproj = sb("outproj", [P, HALF, D])
    Wr = sb("Wr", [P, E0]); br = sb("br", [P, E0]); W1 = sb("W1", [P, E0, FB * P]); b1 = sb("b1", [P, E0, FB])
    W2 = sb("W2", [P, E0, FB, D]); b2 = sb("b2", [J0 * E0, J0, D])
    sel = sb("sel", [96, 2 * S, P], BF16); tri8 = sb("tri8", [P, E0 * E0]); split = sb("split", [P, 2])
    stats = sb("stats", [P, NT, 6]); mean = sb("mean", [P, NT]); rstd = sb("rstd", [P, NT]); rrms = sb("rrms", [P, NT])
    q1 = sb("q1", [P, NT]); q2 = sb("q2", [P, NT])
    XN = sb("XN", [P, J0, D]); XR = sb("XR", [P, J0, D]); xrT = sb("xrT", [P, T0])
    xch = sb("xch", [P, HALF, T0]); xi = sb("xi", [P, HALF, T0]); th = sb("th", [P, HALF, T0]); tz = sb("tz", [P, HALF, T0])
    hi = sb("hi", [96, T0], BF16); rest = sb("rest", [96, T0]); mid = sb("mid", [96, T0], BF16); dtT = sb("dtT", [P, T0])
    soft = sb("soft", [P, HALF, T0])
    u, lnw, one_w = xch, th, tz
    lg = sb("lg", [P, J0, E0]); pe_ = sb("pe_", [P, J0, E0]); pr = sb("pr", [P, J0, E0]); g4 = sb("g4", [P, 3, J0])
    gt = sb("gt", [P, J0, E0, E0]); eq = sb("eq", [P, J0, E0, E0]); cnt = sb("cnt", [P, J0, E0]); cum = sb("cum", [P, J0, E0])
    xnT = sb("xnT", [P, 2, T0]); zs = sb("zs", [P, 2, HALF, T0]); BC = sb("BC", [96, 2, T0], BF16)
    delta = sb("delta", [P, 2, HALF, T0]); dx = sb("dx", [P, 2, HALF, T0])
    y = sb("y", [P, 2, HALF, T0]); FF = sb("FF", [P, 2, J0, D])
    gate = sb("gate", [P, 2, J0, E0]); gT = sb("gT", [J0 * E0, 2, P])
    Bs = sb("Bs", [P, 2, T0]); dBx = sb("dBx", [P, 2, HALF, T0]); H = sb("H", [P, 2, HALF, T0])
    hT = sb("hT", [P, 2, FB, T0])
    dA = ctx.enter_context(nc.psum_tensor("dA", [P, HALF, T0], F32))
    UP = [ctx.enter_context(nc.psum_tensor(f"UP{i}", [P, 512], F32)) for i in range(2)]
    DN = ctx.enter_context(nc.psum_tensor("DN", [P, 512], F32))
    Bp = ctx.enter_context(nc.psum_tensor("Bp", [P, 512], F32))
    Cp = ctx.enter_context(nc.psum_tensor("Cp", [P, 512], F32))
    FRO = ctx.enter_context(nc.psum_tensor("FRO", [P, 512], F32))

    front = signal("front", 11)
    upf = signal("upf", E0 * FB); downf = signal("downf", E0)
    bready = signal("bready", S); cready = signal("cready", S); outf = signal("outf", 1)
    xT_copied = signal("xT_copied", 2); tanh_z = signal("tanh_z", 2); tanh_x = signal("tanh_x", 1)
    gexp = signal("gexp", 1); gT_copied = signal("gT_copied", 1); dt_copied = signal("dt_copied", 1)
    hi_done = signal("hi_done", 1); mid_done = signal("mid_done", 1); sp_done = signal("sp_done", 3)
    relu_done = signal("relu_done", E0 * FB); b_copied = signal("b_copied", S); da_ready = signal("da_ready", 2 * S)
    conv_step = signal("conv_step", 8); gate_step = signal("gate_step", 15); z_done = signal("z_done", 2)
    xi_done = signal("xi_done", 1); rest_done = signal("rest_done", 1); bc_done = signal("bc_done", 1)
    u_done = signal("u_done", 2); log_step = signal("log_step", 4); delta_done = signal("delta_done", 1)
    dx_done = signal("dx_done", 1); scan_done = signal("scan_done", S); prod_done = signal("prod_done", S)
    add_done = signal("add_done", S); acc_done = signal("acc_done", E0); yz_done = signal("yz_done", 1)
    x_done = signal("x_done", 1)
    xn_ready = signal("xn_ready", 4); dbx_ready = signal("dbx_ready", S); y_init = signal("y_init", 1)
    loaded = sem("loaded"); xloaded = sem("xloaded"); zeroed = sem("zeroed"); stat_step = sem("stat_step")
    root_done = sem("root_done"); prep = sem("prep"); aexp = sem("aexp"); paced = sem("paced0")

    block = ctx.enter_context(nc.Block())

    loads = [
        (rmsw[:], dram["L0_attn_rms_w"].rearrange("(p a) -> p a", a=1)),
        (inproj[:], dram["L0_attn_in_proj"]),
        (ident[:], dram["c_ident"]), (identb[:], dram["c_identb"]), (sel[:].rearrange("p a b -> p (a b)"), dram["c_sel"]),
        (tri8[:], dram["c_tri8"]), (split[:], dram["c_split"]),
        (convw[:], dram["L0_attn_conv_w"].rearrange("(h p) k -> p h k", p=P)),
        (convb[:], dram["L0_attn_conv_b"].rearrange("(h p) -> p h", p=P)),
        (dtb[:], dram["L0_attn_dt_b"].rearrange("(h p) -> p h", p=P)),
        (dtw[96:104, :], dram["L0_attn_dt_w"]),
        (A[:], dram["L0_attn_A_log"].rearrange("(h p) s -> p h s", p=P)),
        (Dp[:], dram["L0_attn_D"].rearrange("(h p) -> p h", p=P)),
        (outproj[:], dram["L0_attn_out_proj"].rearrange("(h p) n -> p h n", p=P)),
        (Wr[:], dram["L0_ffn_Wr"]),
        (br[:], dram["L0_ffn_br"].rearrange("(a e) -> a e", a=1).to_broadcast([P, E0])),
        (W1[:], dram["L0_ffn_W1"].rearrange("e p f -> p e f")),
        (b1[:], dram["L0_ffn_b1"].rearrange("e (b p) -> p e b", p=P)),
        (W2[:].rearrange("p e b n -> p (e b) n"), dram["L0_ffn_W2"].rearrange("e (b p) n -> p (e b) n", p=P)),
    ]
    xp = dram["L0_attn_x_proj"].rearrange("(h p) n -> p h n", p=P)
    for r in range(3):
        loads.append((xproj[:, :, 32 * r:32 * r + 32], xp[:, :, RANK:RANK + 32]))
    loads.append((xproj[:, :, 96:104], xp[:, :, 0:RANK]))

    def pipeline(fore, start, slot, end, eng):
        for s in range(S):
            fore(s, 0, 0)
        start()
        for s in range(S):
            slot(s, 0, 0, first=True)
            fore(s, 1, 1)
        with eng.Fori(0, IT0 // 2 - 1) as i:
            for k in range(2):
                it, par = i * 2 + (1 + k), 1 - k
                for s in range(S):
                    slot(s, it, par)
                    fore(s, it + 1, 1 - par)
        for s in range(S):
            slot(s, IT0 - 1, 1, final=True)
        end(IT0 - 1, 1)

    @block.sync
    def _(sp):
        xd = dram["L0_attn_x"].rearrange("b (j p) d -> p (b j) d", p=P)
        for g in range(8):
            sp.dma_start(X[:, 8 * g:8 * g + 8, :], xd[:, 8 * g:8 * g + 8, :]).then_inc(xloaded, 16)
        for dst, src in loads:
            sp.dma_start(dst, src, allow_slow_non_contiguous=True).then_inc(loaded, 16)
        sp.wait_ge(zeroed, 1)
        for j in range(J0):
            sp.dma_start(b2[E0 * j:E0 * j + E0, j, :], dram["L0_ffn_b2"]).then_inc(loaded, 16)

    LOADED = 16 * (len(loads) + J0)

    @block.tensor
    def _(pe):
        for s in (front, upf, downf, bready, cready, outf):
            pe.sem_inc(s.sem, 2 * s.per)
        pe.wait_ge(loaded, LOADED)
        pe.wait_ge(prep, 1)

        def up(e, it, par, blocks):
            q = par if e < E0 else 1 - par
            if e == E0 and blocks[0] == 0:
                pe.wait_ge(xT_copied.sem, xT_copied.at(it + 1, 1))
            for f in blocks:
                k = e * FB + f
                pe.wait_ge(relu_done.sem, relu_done.at(it, k - 1))
                nc.tensor.matmul(UP[k % 2][:], W1[:, e % E0, f * P:(f + 1) * P], xnT[:, q, :], start=True, stop=True).then_inc(upf.sem, 1)

        def down(e, it, tiles):
            if tiles[0] == 0:
                pe.wait_ge(relu_done.sem, relu_done.at(it, (e + 1) * FB))
                pe.wait_ge(acc_done.sem, acc_done.at(it, e))
            for j in tiles:
                for f in range(FB):
                    last = nc.tensor.matmul(DN[:, j * P:(j + 1) * P], hT[:, e % 2, f, j * P:(j + 1) * P], W2[:, e, f, :],
                                            start=(f == 0), stop=(f == FB - 1))
            if tiles[-1] == J0 - 1:
                last.then_inc(downf.sem, 1)

        def output(it, par, last_one=False):
            if not last_one:
                pe.wait_ge(gT_copied.sem, gT_copied.at(it + 1, 1))
            pe.wait_ge(yz_done.sem, yz_done.at(it, 1))
            for j in range(J0):
                nc.tensor.matmul(FRO[:, j * P:(j + 1) * P], gT[:, par, :], b2[:, j, :], start=True, stop=False)
                for h in range(HALF):
                    last = nc.tensor.matmul(FRO[:, j * P:(j + 1) * P], y[:, par, h, j * P:(j + 1) * P], outproj[:, h, :],
                                            start=False, stop=(h == 1))
            last.then_inc(outf.sem, 1)

        def make_b(s, it, par):
            q = par if s < S else 1 - par
            if s == S:
                pe.wait_ge(bc_done.sem, bc_done.at(it + 1, 1))
            pe.wait_ge(b_copied.sem, b_copied.at(it, s))
            nc.tensor.matmul(Bp[:], sel[:, s % S, :], BC[:, q, :], start=True, stop=True).then_inc(bready.sem, 1)

        def start():
            up(E0, -1, 1, range(FB))
            make_b(S, -1, 1)
            make_b(S + 1, -1, 1)

        def slot(s, it, par, first=False, final=False):
            more_up = not (final and s == S - 2)
            if s % 2 == 1:
                down(s // 2, it, range(0, 1))
            elif more_up:
                up(s // 2 + 1, it, par, range(0, 2))
            pe.wait_ge(prod_done.sem, prod_done.at(it, s))
            nc.tensor.matmul(Cp[:], sel[:, S + s, :], BC[:, par, :], start=True, stop=True).then_inc(cready.sem, 1)
            if not (final and s + 2 >= S):
                make_b(s + 2, it, par)
            if s % 2 == 1:
                down(s // 2, it, range(1, J0))
            elif more_up:
                up(s // 2 + 1, it, par, range(2, FB))
            if s == 0 and not first:
                output(it - 1, 1 - par)

        def fore(s, n, q):
            if s == 1:
                pe.wait_ge(xn_ready.sem, xn_ready.at(n, 2))
                pe.wait_ge(gT_copied.sem, gT_copied.at(n - 1, 1))
                pe.wait_ge(x_done.sem, x_done.at(n - 2, 1))
                for j in range(J0):
                    last = nc.tensor.transpose(FRO[:, j * P:(j + 1) * P], XN[:, j, :], ident[:])
                last.then_inc(front.sem, 1)
            elif s == 2:
                pe.wait_ge(xn_ready.sem, xn_ready.at(n, 3))
                pe.wait_ge(xT_copied.sem, xT_copied.at(n, 1))
                for j in range(J0):
                    last = nc.tensor.transpose(FRO[:, j * P:(j + 1) * P], XR[:, j, :], ident[:])
                last.then_inc(front.sem, 1)
            elif 3 <= s < 7:
                k = s - 3
                b = (0, 2, 1, 3)[k]
                if k == 0:
                    pe.wait_ge(xT_copied.sem, xT_copied.at(n, 2))
                elif k == 2:
                    pe.wait_ge(z_done.sem, z_done.at(n, 1))
                else:
                    pe.wait_ge(conv_step.sem, conv_step.at(n, 4 * (b - 1)))
                nc.tensor.matmul(FRO[:], inproj[:, b * P:(b + 1) * P], xrT[:], start=True, stop=True).then_inc(front.sem, 1)
            elif s == 7:
                pe.wait_ge(z_done.sem, z_done.at(n, 2))
                for j in range(J0):
                    last = nc.tensor.matmul(FRO[:, j * E0:(j + 1) * E0], xnT[:, q, j * P:(j + 1) * P], Wr[:], start=True, stop=True)
                last.then_inc(front.sem, 1)
            elif s == 8:
                pe.wait_ge(xi_done.sem, xi_done.at(n, 1))
                pe.wait_ge(gate_step.sem, gate_step.at(n, 1))
                for h in range(HALF):
                    last = nc.tensor.matmul(FRO[0:104, :], xproj[:, h, :], xi[:, h, :], start=(h == 0), stop=(h == 1))
                last.then_inc(front.sem, 1)
            elif s == 9 or s == 10:
                h = s - 9
                if h == 0:
                    pe.wait_ge(dt_copied.sem, dt_copied.at(n, 1))
                    pe.wait_ge(rest_done.sem, rest_done.at(n, 1))
                else:
                    pe.wait_ge(u_done.sem, u_done.at(n, 1))
                nc.tensor.matmul(FRO[:], dtw[96:104, h * P:(h + 1) * P], dtT[96:104, :], start=True, stop=True).then_inc(front.sem, 1)
            elif s == 11:
                pe.wait_ge(gate_step.sem, gate_step.at(n, 15))
                pe.wait_ge(u_done.sem, u_done.at(n, 2))
                nc.tensor.transpose(FRO[0:J0 * E0, 0:P], gate[:, q].rearrange("p j e -> p (j e)"), ident[:]).then_inc(front.sem, 1)

        pipeline(fore, start, slot, lambda it, par: output(it, par, last_one=True), pe)

    @block.scalar
    def _(act):
        for s in (xT_copied, tanh_z, tanh_x, gexp, gT_copied, dt_copied, hi_done, mid_done, sp_done, relu_done, b_copied, da_ready):
            act.sem_inc(s.sem, 2 * s.per)
        act.wait_ge(loaded, LOADED)
        nc.scalar.activation(A[:], A[:], ACT.Exp).then_inc(aexp, 1)
        act.wait_ge(stat_step, 7)
        nc.scalar.activation(stats[:, :, 0], q1[:], ACT.Sqrt).then_inc(root_done, 1)
        act.wait_ge(stat_step, 15)
        nc.scalar.activation(stats[:, :, 0], q2[:], ACT.Sqrt).then_inc(root_done, 1)
        act.wait_ge(prep, 1)

        def copy_b(s, it):
            act.wait_ge(bready.sem, bready.at(it, s + 1))
            act.wait_ge(dbx_ready.sem, dbx_ready.at(it, s - 1))
            nc.scalar.copy(Bs[:, s % 2, :], Bp[:]).then_inc(b_copied.sem, 1)

        def make_da(s, it, par):
            q = par if s < S else 1 - par
            if s == S:
                act.wait_ge(delta_done.sem, delta_done.at(it + 1, 1))
            act.wait_ge(scan_done.sem, scan_done.at(it, s))
            for h in range(HALF):
                nc.scalar.activation(dA[:, h, :].rearrange("p (b l) -> p b l", l=L)[:, :, 1:L],
                                     delta[:, q, h, :].rearrange("p (b l) -> p b l", l=L)[:, :, 1:L],
                                     ACT.Exp, scale=A[:, h, s % S:s % S + 1]).then_inc(da_ready.sem, 1)

        def relus(e, it, blocks):
            for f in blocks:
                k = e * FB + f
                act.wait_ge(upf.sem, upf.at(it, k + 1))
                if f == 0:
                    act.wait_ge(downf.sem, downf.at(it, e - 1))
                nc.scalar.activation(hT[:, e % 2, f, :], UP[k % 2][:], ACT.Relu, bias=b1[:, e % E0, f:f + 1]).then_inc(relu_done.sem, 1)

        def start():
            relus(E0, -1, range(FB))
            copy_b(S, -1)
            copy_b(S + 1, -1)
            make_da(S, -1, 1)

        def slot(s, it, par, first=False, final=False):
            ups = s % 2 == 0 and not (final and s == S - 2)
            if ups:
                relus(s // 2 + 1, it, range(0, 2))
            if not (final and s + 2 >= S):
                copy_b(s + 2, it)
            if not (final and s + 1 >= S):
                make_da(s + 1, it, par)
            if ups:
                relus(s // 2 + 1, it, range(2, FB))

        def fore(s, n, q):
            if s == 2:
                act.wait_ge(upf.sem, upf.at(n - 2, E0 * FB))
                act.wait_ge(front.sem, front.at(n, 1))
                nc.scalar.copy(xnT[:, q, :], FRO[:]).then_inc(xT_copied.sem, 1)
            elif s == 3:
                act.wait_ge(front.sem, front.at(n, 2))
                nc.scalar.copy(xrT[:], FRO[:]).then_inc(xT_copied.sem, 1)
            elif s == 5 or s == 7:
                b = (s - 5) // 2
                if b == 0:
                    act.wait_ge(delta_done.sem, delta_done.at(n - 1, 1))
                act.wait_ge(front.sem, front.at(n, 4 + 2 * b))
                nc.scalar.activation(tz[:, b, :], FRO[:], ACT.Tanh, scale=0.5).then_inc(tanh_z.sem, 1)
                if b == 1:
                    act.wait_ge(conv_step.sem, conv_step.at(n, 8))
                    nc.scalar.activation(th[:], xch[:], ACT.Tanh).then_inc(tanh_x.sem, 1)
            elif s == 8:
                act.wait_ge(gate_step.sem, gate_step.at(n, 3))
                nc.scalar.activation(pe_[:], lg[:], ACT.Exp).then_inc(gexp.sem, 1)
            elif s == 9:
                act.wait_ge(front.sem, front.at(n, 8))
                nc.scalar.copy(dtT[96:104, :], FRO[96:104, :]).then_inc(dt_copied.sem, 1)
                nc.scalar.copy(hi[:], FRO[0:96, :]).then_inc(hi_done.sem, 1)
            elif s == 10:
                act.wait_ge(rest_done.sem, rest_done.at(n, 1))
                act.wait_ge(bc_done.sem, bc_done.at(n - 1, 1))
                nc.scalar.copy(mid[:], rest[:]).then_inc(mid_done.sem, 1)
            elif s == 12:
                act.wait_ge(outf.sem, outf.at(n - 2, 1))
                act.wait_ge(front.sem, front.at(n, 11))
                nc.scalar.copy(gT[:, q, :], FRO[0:J0 * E0, 0:P]).then_inc(gT_copied.sem, 1)
                act.wait_ge(u_done.sem, u_done.at(n, 2))
                nc.scalar.activation(soft[:], u[:], ACT.Abs).then_inc(sp_done.sem, 1)
                act.wait_ge(sp_done.sem, sp_done.at(n, 1))
                nc.scalar.activation(soft[:], soft[:], ACT.Exp, scale=-1.0).then_inc(sp_done.sem, 1)
            elif s == 13:
                act.wait_ge(log_step.sem, log_step.at(n, 2))
                nc.scalar.activation(lnw[:], one_w[:], ACT.Ln).then_inc(sp_done.sem, 1)

        pipeline(fore, start, slot, lambda it, par: None, act)

    @block.gpsimd
    def _(pool):
        for s in (xn_ready, dbx_ready, y_init):
            pool.sem_inc(s.sem, 2 * s.per)
        nc.gpsimd.memset(b2[:], 0.0).then_inc(zeroed, 1)
        pool.wait_ge(stat_step, 20)
        pool.wait_ge(prep, 1)

        def make_dbx(s, it, par):
            q = par if s < S else 1 - par
            if s == S:
                pool.wait_ge(dx_done.sem, dx_done.at(it + 1, 1))
            pool.wait_ge(b_copied.sem, b_copied.at(it, s + 1))
            pool.wait_ge(scan_done.sem, scan_done.at(it, s - 1))
            nc.gpsimd.tensor_tensor(dBx[:, s % 2], dx[:, q], Bs[:, s % 2, :].unsqueeze(1).to_broadcast([P, HALF, T0]),
                                    ALU.mult).then_inc(dbx_ready.sem, 1)

        def slot(s, it, par, first=False, final=False):
            if not (final and s + 1 >= S):
                make_dbx(s + 1, it, par)

        def fore(s, n, q):
            def wide(v):
                return v[:, bass.ds(n * J0, J0)].unsqueeze(2).to_broadcast([P, J0, D])

            xs = X[:, bass.ds(n * J0, J0), :]
            if s == 0:
                pool.wait_ge(front.sem, front.at(n - 1, 2))
                pool.sem_inc(paced, 1)
                nc.gpsimd.tensor_tensor(XR[:], xs, wide(mean), ALU.subtract).then_inc(xn_ready.sem, 1)
                pool.wait_ge(xn_ready.sem, xn_ready.at(n, 1))
                nc.gpsimd.tensor_tensor(XN[:], XR[:], wide(rstd), ALU.mult).then_inc(xn_ready.sem, 1)
            elif s == 1:
                pool.wait_ge(xn_ready.sem, xn_ready.at(n, 2))
                nc.gpsimd.tensor_tensor(XR[:], XN[:], wide(rrms), ALU.mult).then_inc(xn_ready.sem, 1)
            elif s == 2:
                pool.wait_ge(x_done.sem, x_done.at(n - 2, 1))
                pool.sem_inc(paced, 1)
                nc.gpsimd.tensor_tensor(FF[:, q], XN[:], xs, ALU.add).then_inc(xn_ready.sem, 1)
            elif s == 9:
                pool.wait_ge(xi_done.sem, xi_done.at(n, 1))
                pool.wait_ge(outf.sem, outf.at(n - 2, 1))
                nc.gpsimd.tensor_tensor(y[:, q], xi[:], Dp[:].unsqueeze(2).to_broadcast([P, HALF, T0]), ALU.mult).then_inc(y_init.sem, 1)

        pipeline(fore, lambda: make_dbx(S, -1, 1), slot, lambda it, par: None, pool)

    @block.vector
    def _(dve):
        for s in (conv_step, gate_step, z_done, xi_done, rest_done, bc_done, u_done, log_step, delta_done, dx_done,
                  scan_done, prod_done, add_done, acc_done, yz_done, x_done):
            dve.sem_inc(s.sem, 2 * s.per)
        nc.vector.memset(dA[:].rearrange("p h (b l) -> p h b l", l=L)[:, :, :, 0:1], 0.0)
        dve.wait_ge(xloaded, 16 * 8)
        token_stats(nc, dve, X, stats, mean, rstd, q1, q2, stat_step, root_done)
        dve.wait_ge(stat_step, 12)
        nc.vector.tensor_tensor(q2[:], q2[:], rstd[:], ALU.mult).then_inc(stat_step, 1)
        dve.wait_ge(stat_step, 13)
        nc.vector.tensor_tensor(q2[:], q2[:], rstd[:], ALU.mult).then_inc(stat_step, 1)
        dve.wait_ge(stat_step, 14)
        nc.vector.tensor_scalar(q2[:], q2[:], EPS, None, ALU.add).then_inc(stat_step, 1)
        inverse_root(nc, dve, rrms, q2, stats, stat_step, root_done, 15, 2)
        dve.wait_ge(loaded, LOADED)
        nc.vector.tensor_scalar(inproj[:], inproj[:], rmsw[:], None, ALU.mult)
        nc.vector.tensor_scalar(convw[:], convw[:], 0.5, None, ALU.mult)
        nc.vector.tensor_scalar(convb[:], convb[:], 0.5, None, ALU.mult)
        nc.vector.tensor_scalar(outproj[:], outproj[:], 0.5, None, ALU.mult)
        dve.wait_ge(aexp, 1)
        nc.vector.tensor_scalar(A[:], A[:], -1.0, None, ALU.mult).then_inc(prep, 1)
        dve.wait_ge(prep, 1)

        def add(s, it, par):
            if s == 0:
                dve.wait_ge(y_init.sem, y_init.at(it, 1))
            dve.wait_ge(prod_done.sem, prod_done.at(it, s + 1))
            dve.wait_ge(add_done.sem, add_done.at(it, s))
            nc.vector.tensor_tensor(y[:, par], y[:, par], H[:, s % 2], ALU.add).then_inc(add_done.sem, 1)

        def close(it, par):
            add(S - 1, it, par)
            dve.wait_ge(add_done.sem, add_done.at(it, S))
            nc.vector.tensor_tensor(y[:, par], y[:, par], zs[:, par], ALU.mult).then_inc(yz_done.sem, 1)

        def store(it, par):
            dve.wait_ge(outf.sem, outf.at(it, 1))
            dve.wait_ge(acc_done.sem, acc_done.at(it, E0))
            nc.vector.tensor_tensor(X[:, bass.ds(it * J0, J0), :], FRO[:].rearrange("p (j d) -> p j d", d=D), FF[:, par],
                                    ALU.add).then_inc(x_done.sem, 1)

        def accumulate(e, it, par):
            dve.wait_ge(downf.sem, downf.at(it, e + 1))
            dve.wait_ge(acc_done.sem, acc_done.at(it, e))
            if e == 0:
                dve.wait_ge(xn_ready.sem, xn_ready.at(it, 4))
            for j in range(J0):
                last = nc.vector.scalar_tensor_tensor(FF[:, par, j, :], DN[:, j * P:(j + 1) * P], gate[:, par, j, e:e + 1],
                                                      FF[:, par, j, :], ALU.mult, ALU.add)
            last.then_inc(acc_done.sem, 1)

        def slot(s, it, par, first=False, final=False):
            dve.wait_ge(da_ready.sem, da_ready.at(it, 2 * s + 2))
            dve.wait_ge(dbx_ready.sem, dbx_ready.at(it, s + 1))
            dve.wait_ge(add_done.sem, add_done.at(it, s - 1))
            nc.vector.tensor_tensor_scan(H[:, s % 2].rearrange("p h t -> p (h t)"), dA[:].rearrange("p h t -> p (h t)"),
                                         dBx[:, s % 2].rearrange("p h t -> p (h t)"), 0.0, ALU.mult, ALU.add).then_inc(scan_done.sem, 1)
            if s == 0 and not first:
                close(it - 1, 1 - par)
                accumulate(E0 - 1, it - 1, 1 - par)
            if s == 1 and not first:
                store(it - 1, 1 - par)
            if s > 0:
                if s % 2 == 0:
                    accumulate(s // 2 - 1, it, par)
                add(s - 1, it, par)
            dve.wait_ge(scan_done.sem, scan_done.at(it, s + 1))
            dve.wait_ge(cready.sem, cready.at(it, s + 1))
            nc.vector.tensor_tensor(H[:, s % 2], H[:, s % 2], Cp[:].unsqueeze(1).to_broadcast([P, HALF, T0]), ALU.mult).then_inc(prod_done.sem, 1)

        def end(it, par):
            accumulate(E0 - 1, it, par)
            close(it, par)
            store(it, par)

        def seqs(ap):
            return ap.rearrange("p (b l) -> p b l", l=L)

        def over(v, n=E0):
            return v.unsqueeze(2).to_broadcast([P, J0, n])

        def delta_input(h, n):
            dve.wait_ge(front.sem, front.at(n, 9 + h))
            nc.vector.tensor_scalar(u[:, h, :], FRO[:], dtb[:, h:h + 1], None, ALU.add).then_inc(u_done.sem, 1)

        def fore(s, n, q):
            def gstep(ins, k):
                ins.then_inc(gate_step.sem, 1)
                dve.wait_ge(gate_step.sem, gate_step.at(n, k))

            other = pr[:].unsqueeze(2).to_broadcast([P, J0, E0, E0])
            this = pr[:].unsqueeze(3).to_broadcast([P, J0, E0, E0])
            if s == 4 or s == 6:
                b = (s - 4) // 2
                dve.wait_ge(front.sem, front.at(n, 3 + 2 * b))
                src, dst = seqs(FRO[:]), seqs(xch[:, b, :])
                nc.vector.tensor_scalar(xch[:, b, :], FRO[:], convw[:, b, 3:4], convb[:, b:b + 1],
                                        ALU.mult, ALU.add).then_inc(conv_step.sem, 1)
                for k in range(1, 4):
                    dve.wait_ge(conv_step.sem, conv_step.at(n, 4 * b + k))
                    nc.vector.scalar_tensor_tensor(dst[:, :, k:], src[:, :, :L - k], convw[:, b, 3 - k:4 - k], dst[:, :, k:],
                                                   ALU.mult, ALU.add).then_inc(conv_step.sem, 1)
            elif s == 5:
                dve.wait_ge(tanh_z.sem, tanh_z.at(n, 1))
                nc.vector.scalar_tensor_tensor(zs[:, q, 0, :], tz[:, 0, :], 1.0, FRO[:], ALU.add, ALU.mult).then_inc(z_done.sem, 1)
            elif s == 7:
                dve.wait_ge(tanh_x.sem, tanh_x.at(n, 1))
                dve.wait_ge(y_init.sem, y_init.at(n - 1, 1))
                nc.vector.scalar_tensor_tensor(xi[:], th[:], 1.0, xch[:], ALU.add, ALU.mult).then_inc(xi_done.sem, 1)
                dve.wait_ge(tanh_z.sem, tanh_z.at(n, 2))
                nc.vector.scalar_tensor_tensor(zs[:, q, 1, :], tz[:, 1, :], 1.0, FRO[:], ALU.add, ALU.mult).then_inc(z_done.sem, 1)
            elif s == 8:
                dve.wait_ge(front.sem, front.at(n, 7))
                gstep(nc.vector.tensor_tensor(lg[:], FRO[:, 0:J0 * E0].rearrange("p (j e) -> p j e", e=E0),
                                              br[:].unsqueeze(1).to_broadcast([P, J0, E0]), ALU.add), 1)
                gstep(nc.vector.tensor_reduce(g4[:, 0, :], lg[:], AX.X, ALU.max), 2)
                nc.vector.tensor_tensor(lg[:], lg[:], over(g4[:, 0, :]), ALU.subtract).then_inc(gate_step.sem, 1)
            elif s == 9:
                dve.wait_ge(hi_done.sem, hi_done.at(n, 1))
                nc.vector.scalar_tensor_tensor(rest[:], hi[:], split[0:96, 0:1], FRO[0:96, :], ALU.mult, ALU.add).then_inc(rest_done.sem, 1)
                dve.wait_ge(gexp.sem, gexp.at(n, 1))
                gstep(nc.vector.tensor_reduce(g4[:, 1, :], pe_[:], AX.X, ALU.add), 4)
                gstep(nc.vector.reciprocal(g4[:, 2, :], g4[:, 1, :]), 5)
                gstep(nc.vector.tensor_tensor(pr[:], pe_[:], over(g4[:, 2, :]), ALU.mult), 6)
                gstep(nc.vector.tensor_tensor(gt[:], other, this, ALU.is_gt), 7)
                gstep(nc.vector.tensor_tensor(eq[:], other, this, ALU.is_equal), 8)
                tri = tri8[:].rearrange("p (e o) -> p e o", o=E0).unsqueeze(1).to_broadcast([P, J0, E0, E0])
                gstep(nc.vector.tensor_tensor(eq[:], eq[:], tri, ALU.mult), 9)
            elif s == 10:
                delta_input(0, n)
                gstep(nc.vector.tensor_tensor(gt[:], gt[:], eq[:], ALU.add), 10)
                nc.vector.tensor_reduce(cnt[:], gt[:], AX.X, ALU.add)
                gstep(nc.vector.tensor_tensor(eq[:], gt[:], other, ALU.mult), 11)
                gstep(nc.vector.tensor_reduce(cum[:], eq[:], AX.X, ALU.add), 12)
                gstep(nc.vector.tensor_scalar(cum[:], cum[:], TOP_P, None, ALU.is_lt), 13)
                gstep(nc.vector.scalar_tensor_tensor(cum[:], cnt[:], 1.5, cum[:], ALU.is_lt, ALU.max), 14)
                nc.vector.tensor_tensor(gate[:, q], pr[:], cum[:], ALU.mult).then_inc(gate_step.sem, 1)
            elif s == 11:
                delta_input(1, n)
                dve.wait_ge(mid_done.sem, mid_done.at(n, 1))
                dve.wait_ge(cready.sem, cready.at(n - 2, S))
                nc.vector.scalar_tensor_tensor(BC[:, q, :], mid[:], split[0:96, 1:2], rest[:], ALU.mult, ALU.add).then_inc(bc_done.sem, 1)
            elif s == 12:
                dve.wait_ge(sp_done.sem, sp_done.at(n, 2))
                nc.vector.tensor_scalar(one_w[:], soft[:], 1.0, None, ALU.add).then_inc(log_step.sem, 1)
                dve.wait_ge(log_step.sem, log_step.at(n, 1))
                nc.vector.scalar_tensor_tensor(soft[:], one_w[:], -1.0, soft[:], ALU.add, ALU.subtract).then_inc(log_step.sem, 1)
                dve.wait_ge(log_step.sem, log_step.at(n, 2))
                nc.vector.scalar_tensor_tensor(u[:], u[:], 0.0, soft[:], ALU.max, ALU.subtract).then_inc(log_step.sem, 1)
            elif s == 13:
                dve.wait_ge(sp_done.sem, sp_done.at(n, 3))
                nc.vector.scalar_tensor_tensor(lnw[:], one_w[:], 1.0, lnw[:], ALU.is_gt, ALU.mult).then_inc(log_step.sem, 1)
                dve.wait_ge(log_step.sem, log_step.at(n, 4))
                dve.wait_ge(da_ready.sem, da_ready.at(n - 2, 2 * S))
                nc.vector.tensor_tensor(delta[:, q], u[:], lnw[:], ALU.add).then_inc(delta_done.sem, 1)
                dve.wait_ge(delta_done.sem, delta_done.at(n, 1))
                nc.vector.tensor_tensor(dx[:, q], delta[:, q], xi[:], ALU.mult).then_inc(dx_done.sem, 1)

        pipeline(fore, lambda: None, slot, end, dve)
        dve.wait_ge(x_done.sem, x_done.at(IT0 - 1, 1))




J1 = L // P
NSEQ = NTOK // L
HEADS, LAT, DH = 16, 64, 8
GROUPS = 4
HG = HEADS // GROUPS
TERMS = ((0, 0), (0, 1), (0, 2), (1, 0), (1, 1), (2, 0))
KQ = len(TERMS) * DH
SCALE = 1.0 / float(np.sqrt(DH))
E1, CAP = 128, 32
NSLOT = E1 * CAP


def token_stats(nc, dve, X, stats, mean, rstd, q1, q2, stat_step, root_done):
    for i in range(NT):
        last = nc.vector.bn_stats(stats[:, i, :], X[:, i, :])
    last.then_inc(stat_step, 1)
    dve.wait_ge(stat_step, 1)
    me, mo = stats[:, :, 1], stats[:, :, 4]
    nc.vector.tensor_tensor(q1[:], me, mo, ALU.subtract).then_inc(stat_step, 1)
    nc.vector.tensor_tensor(mean[:], me, mo, ALU.add)
    nc.vector.tensor_tensor(rstd[:], stats[:, :, 2], stats[:, :, 5], ALU.add).then_inc(stat_step, 1)
    dve.wait_ge(stat_step, 3)
    nc.vector.tensor_tensor(q2[:], q1[:], q1[:], ALU.mult)
    nc.vector.tensor_scalar(mean[:], mean[:], 0.5, None, ALU.mult).then_inc(stat_step, 1)
    dve.wait_ge(stat_step, 4)
    nc.vector.tensor_scalar(q2[:], q2[:], 0.25, None, ALU.mult).then_inc(stat_step, 1)
    dve.wait_ge(stat_step, 5)
    nc.vector.scalar_tensor_tensor(q2[:], rstd[:], 1.0 / D, q2[:], ALU.mult, ALU.add).then_inc(stat_step, 1)
    dve.wait_ge(stat_step, 6)
    nc.vector.tensor_scalar(q1[:], q2[:], EPS, None, ALU.add).then_inc(stat_step, 1)
    inverse_root(nc, dve, rstd, q1, stats, stat_step, root_done, 7, 1)


def inverse_root(nc, dve, out, v, root, stat_step, root_done, k, r):
    dve.wait_ge(root_done, r)
    nc.vector.reciprocal(out[:], root[:, :, 0]).then_inc(stat_step, 1)
    dve.wait_ge(stat_step, k + 1)
    nc.vector.tensor_tensor(root[:, :, 0], out[:], out[:], ALU.mult).then_inc(stat_step, 1)
    dve.wait_ge(stat_step, k + 2)
    nc.vector.tensor_tensor(root[:, :, 0], root[:, :, 0], v[:], ALU.mult).then_inc(stat_step, 1)
    dve.wait_ge(stat_step, k + 3)
    nc.vector.tensor_scalar(root[:, :, 0], root[:, :, 0], -0.5, 1.5, ALU.mult, ALU.add).then_inc(stat_step, 1)
    dve.wait_ge(stat_step, k + 4)
    nc.vector.tensor_tensor(out[:], out[:], root[:, :, 0], ALU.mult).then_inc(stat_step, 1)


def layer1(nc, ctx, t, dram, scratch):
    def sb(name, shape, dt=F32):
        return ctx.enter_context(nc.sbuf_tensor(name, shape, dt))

    def signal(name, per):
        return Signal(ctx.enter_context(nc.semaphore(name)), per)

    def sem(name):
        return ctx.enter_context(nc.semaphore(name))

    X, ident, identb, WE, carry = t["X"], t["ident"], t["identb"], t["WE"], t["carry"]
    EF, EU, LG, LOC, iota = t["EF"], t["EU"], t["LG"], t["LOC"], t["iota"]
    stats = sb("stats1", [P, NT, 6]); mean = sb("mean1", [P, NT]); rstd = sb("rstd1", [P, NT])
    q1 = sb("q11", [P, NT]); q2 = sb("q21", [P, NT])
    wq = sb("wq", [P, P]); wk = sb("wk", [P, P]); wqr = sb("wqr", [P, P]); wkr = sb("wkr", [P, P])
    wvg = sb("wvg", [P, 2 * P]); wc = sb("wc", [P, D])
    cos = sb("cos", [P, L]); sin = sb("sin", [P, L])
    maskq = sb("maskq", [P, HG, P], BF16); maskk = sb("maskk", [P, HG, P], BF16); mask2 = sb("mask2", [P, 2, 512], BF16)
    tri = sb("tri", [P, P], BF16); ones = sb("ones", [P, P], BF16)
    XN = sb("XN2", [P, 2, J1, D]); XM = sb("XM2", [P, J1, D]); xnT = sb("xnT2", [P, L])
    t1 = sb("t1", [P, 2, L]); t2 = sb("t2", [P, 2, L]); QK = sb("QK", [P, 2, L]); R1 = sb("R1", [P, 2, L])
    SPL = sb("SPL", [P, 3, 2, L], BF16)
    QS = [sb(f"QS{i}", [64, HEADS, L], BF16) for i in range(2)]
    KS = [sb(f"KS{i}", [64, HEADS, L], BF16) for i in range(2)]
    V = [sb(f"V{i}", [P, J1, HEADS, DH + 1]) for i in range(2)]
    PT = sb("PT", [P, 2, 1536])
    OSB = sb("OSB", [P, GROUPS, L]); rec = sb("rec", [P, HEADS]); YN = sb("YN", [P, J1, HEADS, DH]); yT = sb("yT", [P, L])
    NM = sb("NM", [P, J1, HEADS]); NR = sb("NR", [P, J1, HEADS]); NMS = sb("NMS", [P, J1, P // HEADS, HEADS], BF16)
    NMT = sb("NMT", [3 * HEADS, L], BF16)
    mx = sb("mx", [P, J1, 8]); ix = sb("ix", [P, J1, 8], mybir.dt.uint32); ef = sb("ef", [P, J1, 2])
    MK = sb("MK", [P, J1, 2, P], BF16); cs = sb("cs", [P, 2, P]); loc = sb("loc", [P, J1, 2])
    zeros = sb("zeros", [P, 2048])
    SS = [ctx.enter_context(nc.psum_tensor(f"SS{i}", [P, 1536], F32)) for i in range(2)]
    FR = ctx.enter_context(nc.psum_tensor("FR", [P, 512], F32))
    OT = ctx.enter_context(nc.psum_tensor("OT", [P, 2, L], F32))
    FRb = FR[:].bitcast(BF16)

    fr_x = signal("fr_x", 1); fr_vg = signal("fr_vg", 1); fr_qk = signal("fr_qk", 1); fr_rot = signal("fr_rot", 1)
    fr_route = signal("fr_route", 2); fr_nm = signal("fr_nm", 1); fr_o = signal("fr_o", 2); fr_y = signal("fr_y", 1)
    fr_wc = signal("fr_wc", 1); p1 = signal("p1", GROUPS); p2 = signal("p2", GROUPS); pv = signal("pv", GROUPS)
    xT_done = signal("xT_done", 1); v_done = signal("v_done", 1); part_done = signal("part_done", 2)
    nm_copied = signal("nm_copied", 1); exp_done = signal("exp_done", GROUPS); ot_copied = signal("ot_copied", 2)
    yT_done = signal("yT_done", 1)
    top = signal("top", 4); rope = signal("rope", 2); route = signal("route", 13); max_done = signal("max_done", 8)
    nm_step = signal("nm_step", 4); epi = signal("epi", 4); x_upd = signal("x_upd", 1)
    xn_ready = signal("xn_ready1", 2); rest = signal("rest1", 3)
    xn_stored = signal("xn_stored", 16); parts_out = signal("parts_out", 16); parts_in = signal("parts_in", 16 * 12)
    nm_out = signal("nm_out", 16); nm_in = signal("nm_in", 16)
    loaded = sem("loaded1"); stat_step = sem("stat_step1"); root_done = sem("root_done1"); we_loaded = sem("we_loaded")
    wT = sem("wT"); wTc = sem("wTc"); wE = sem("wE"); cleared = sem("cleared"); yzero = sem("yzero")
    poolset = sem("poolset"); paced = sem("paced")

    down = {n: dram[f"L1_attn_W{n}_down"] for n in "qkv"}
    WD = sb("WD", [P, 3, HEADS * LAT]); BD = sb("BD", [P, 3, 2, 2, DH])
    WDT = PT[:, 0, 0:8 * P]

    block = ctx.enter_context(nc.Block())
    loads = [(WD[:, n, :], down[k]) for n, k in enumerate("qkv")]
    for hh in range(2):
        rows = slice(LAT * hh, LAT * hh + LAT)
        for n, k in enumerate("qk"):
            c_, e_ = dram[f"L1_attn_W{k}_up_c"], dram[f"L1_attn_W{k}_up_e"]
            loads += [(BD[rows, n, 0, hh, 0:4], c_), (BD[rows, n, 0, hh, 4:8], e_)]
            pair = e_.rearrange("l (i two) -> l i two", two=2)
            dst = BD[rows, n, 1, hh, 4:8].rearrange("p (i two) -> p i two", two=2)
            loads += [(dst[:, :, 0:1], pair[:, :, 1:2]), (dst[:, :, 1:2], pair[:, :, 0:1])]
        loads += [(BD[rows, 2, 0, hh, :], dram["L1_attn_Wv_up"])]
    loads += [(wvg[:, P:], dram["L1_ffn_wg"]), (wc[:], dram["L1_attn_Wc"]), (cos[:], dram["c_cos"]), (sin[:], dram["c_sin"]),
              (maskq[:].rearrange("p a b -> p (a b)"), dram["c_maskq"]), (maskk[:].rearrange("p a b -> p (a b)"), dram["c_maskk"]),
              (mask2[:].rearrange("p a b -> p (a b)"), dram["c_mask2"]), (tri[:], dram["c_tri"]), (iota[:], dram["c_iota"])]
    LOADED = 16 * len(loads)

    parts_d, nm_d, xn_d, y_d = scratch["parts"], scratch["nm"], scratch["xn"], scratch["y"]

    def schedule(eng, front, pass1, pass2, epilogue):
        front(0, 0)
        pass1(0, 0)
        front(1, 1)
        with eng.Fori(0, NSEQ // 2 - 1) as i:
            for par in range(2):
                c = i * 2 + par
                pass2(c, par)
                pass1(c + 1, 1 - par)
                epilogue(c, par)
                front(c + 2, par)
        pass2(NSEQ - 2, 0)
        pass1(NSEQ - 1, 1)
        epilogue(NSEQ - 2, 0)
        pass2(NSEQ - 1, 1)
        epilogue(NSEQ - 1, 1)

    def nothing(c, par):
        pass

    @block.sync
    def _(sp):
        sp.wait_ge(cleared, 1)
        for dst, src in loads:
            sp.dma_start(dst, src, allow_slow_non_contiguous=True).then_inc(loaded, 16)
        sp.wait_ge(poolset, 2)
        sp.wait_ge(stat_step, 1)
        sp.sem_inc(xn_stored.sem, 32)
        sp.sem_inc(parts_out.sem, 32)
        sp.sem_inc(parts_in.sem, 2 * 16 * 12)
        sp.sem_inc(nm_out.sem, 32)
        sp.sem_inc(nm_in.sem, 32)

        def front(c, par):
            if isinstance(c, int) and c == 1:
                for g in range(8):
                    sp.dma_start(WE[:, 16 * g:16 * g + 16, :], dram["L1_ffn_we"][16 * g:16 * g + 16].rearrange("e d f -> d e f")).then_inc(we_loaded, 16)
                for g in range(8):
                    sp.dma_start(y_d[2048 * g:2048 * g + 2048, :].rearrange("(p r) d -> p (r d)", p=P), zeros[:]).then_inc(yzero, 16)
            sp.wait_ge(xn_ready.sem, xn_ready.at(c, 2))
            sp.dma_start(xn_d.rearrange("(i p) d -> p i d", p=P)[:, bass.ds(c * J1, J1), :], XN[:, par]).then_inc(xn_stored.sem, 16)
            sp.wait_ge(rest.sem, rest.at(c, 3))
            sp.wait_ge(parts_in.sem, parts_in.at(c - 1, 16 * 12))
            sp.dma_start(parts_d[par], SPL[:].rearrange("p r q t -> p (r q t)")).then_inc(parts_out.sem, 16)
            sp.wait_ge(parts_out.sem, parts_out.at(c, 16))
            sp.wait_ge(p2.sem, p2.at(c - 2, GROUPS))
            src = parts_d[par].rearrange("(h d) (r q t) -> d r q h t", d=DH, r=3, q=2)
            for n, term in enumerate(TERMS):
                for q, dst in enumerate((QS, KS)):
                    sp.dma_start(dst[par][DH * n:DH * n + DH, :, :], src[:, term[q], q, :, :]).then_inc(parts_in.sem, 16)

        def pass1(c, par):
            sp.wait_ge(nm_copied.sem, nm_copied.at(c, 1))
            sp.wait_ge(nm_in.sem, nm_in.at(c - 1, 16))
            sp.dma_start(nm_d[par], NMT[:]).then_inc(nm_out.sem, 16)
            sp.wait_ge(nm_out.sem, nm_out.at(c, 16))
            sp.dma_start(QS[par][KQ:KQ + 3, :, :], nm_d[par].rearrange("(r h) t -> r h t", r=3)).then_inc(nm_in.sem, 16)

        schedule(sp, front, pass1, nothing, nothing)
        sp.wait_ge(xn_stored.sem, xn_stored.at(NSEQ - 1, 16))
        sp.wait_ge(nm_in.sem, nm_in.at(NSEQ - 1, 16))
        sp.wait_ge(we_loaded, 16 * 8)
        sp.wait_ge(yzero, 16 * 8)

    @block.tensor
    def _(pe):
        for s in (fr_x, fr_vg, fr_qk, fr_rot, fr_route, fr_nm, fr_o, fr_y, fr_wc, p1, p2, pv):
            pe.sem_inc(s.sem, 2 * s.per)
        pe.wait_ge(loaded, LOADED)
        for n in range(3):
            if n:
                pe.wait_ge(wTc, 2 * n)
            for b in range(8):
                last = nc.tensor.transpose(SS[0][:, b * P:(b + 1) * P], WD[:, n, b * P:(b + 1) * P], ident[:])
            last.then_inc(wT, 1)
            pe.wait_ge(wTc, 2 * n + 1)
            for b in range(8):
                last = nc.tensor.matmul(SS[1][:, b * 32:b * 32 + 32], WDT[:, b * P:(b + 1) * P],
                                        BD[:, n, :, :, :].rearrange("p r h d -> p (r h d)"), start=True, stop=True)
            last.then_inc(wE, 1)
        pe.wait_ge(wTc, 6)
        pe.wait_ge(poolset, 2)
        pe.wait_ge(stat_step, 1)

        def front(c, par):
            pe.wait_ge(nm_copied.sem, nm_copied.at(c - 1, 1))
            pe.wait_ge(x_upd.sem, x_upd.at(c - 2, 1))
            pe.wait_ge(xn_ready.sem, xn_ready.at(c, 2))
            for j in range(J1):
                last = nc.tensor.transpose(FR[:, j * P:(j + 1) * P], XN[:, par, j, :], ident[:])
            last.then_inc(fr_x.sem, 1)
            pe.wait_ge(xT_done.sem, xT_done.at(c, 1))
            for j in range(J1):
                last = nc.tensor.matmul(FR[:, 2 * j * P:2 * (j + 1) * P], xnT[:, j * P:(j + 1) * P], wvg[:], start=True, stop=True)
            last.then_inc(fr_vg.sem, 1)
            pe.wait_ge(top.sem, top.at(c, 4))
            for q, w in enumerate((wq, wk)):
                last = nc.tensor.matmul(FR[:, q * L:(q + 1) * L], w[:], xnT[:], start=True, stop=True)
            last.then_inc(fr_qk.sem, 1)
            pe.wait_ge(rope.sem, rope.at(c, 1))
            for q, w in enumerate((wqr, wkr)):
                last = nc.tensor.matmul(FR[:, q * L:(q + 1) * L], w[:], xnT[:], start=True, stop=True)
            last.then_inc(fr_rot.sem, 1)
            for j in range(J1):
                if j == 0:
                    pe.wait_ge(rope.sem, rope.at(c, 2))
                    pe.wait_ge(route.sem, route.at(c, 4))
                else:
                    pe.wait_ge(route.sem, route.at(c, 6))
                rhs = MK[:, j, :, :].rearrange("p c e -> p (c e)")
                nc.tensor.matmul(FR[:, 0:2 * P], tri[:], rhs, start=True, stop=True)
                nc.tensor.matmul(FR[:, 2 * P:4 * P], ones[:], rhs, start=True, stop=True).then_inc(fr_route.sem, 1)

        def pass1(c, par):
            pe.wait_ge(parts_in.sem, parts_in.at(c, 16 * 12))
            for g in range(GROUPS):
                S_ = SS[g % 2]
                if g < 2:
                    pe.wait_ge(exp_done.sem, exp_done.at(c - 1, g + 3))
                else:
                    pe.wait_ge(max_done.sem, max_done.at(c, 2 * (g - 1)))
                nc.tensor.matmul(S_[:, 0:512], identb[:], maskq[:].rearrange("p a b -> p (a b)"), start=True, stop=False)
                for j in range(HG):
                    h = HG * g + j
                    nc.tensor.matmul(S_[:, j * P:(j + 1) * P], QS[par][0:KQ, h, 0:P], KS[par][0:KQ, h, 0:P], start=False, stop=(j == HG - 1))
                for b in range(2):
                    bank = S_[:, 512 * (b + 1):512 * (b + 2)]
                    nc.tensor.matmul(bank, identb[:], mask2[:, 0, :], start=True, stop=False)
                    for j in range(2):
                        h = HG * g + 2 * b + j
                        last = nc.tensor.matmul(bank[:, j * L:(j + 1) * L], QS[par][0:KQ, h, P:L], KS[par][0:KQ, h, :], start=False, stop=(j == 1))
                last.then_inc(p1.sem, 1)
            pe.wait_ge(nm_step.sem, nm_step.at(c, 4))
            pe.wait_ge(route.sem, route.at(c, 13))
            for j in range(J1):
                last = nc.tensor.transpose(FRb[:, j * P:(j + 1) * P], NMS[:, j, :, :].rearrange("p r h -> p (r h)"), identb[:])
            last.then_inc(fr_nm.sem, 1)

        def values(c, par, g):
            pe.wait_ge(exp_done.sem, exp_done.at(c, g + 1))
            if g == 0:
                pe.wait_ge(ot_copied.sem, ot_copied.at(c - 1, 2))
            if g == 2:
                pe.wait_ge(ot_copied.sem, ot_copied.at(c, 1))
            for j in range(HG):
                h, rows = HG * g + j, slice(32 * j, 32 * j + DH + 1)
                nc.tensor.matmul(OT[rows, g % 2, :], V[par][:, 0, h, :], PT[:, g % 2, j * L:(j + 1) * L],
                                 start=True, stop=False, tile_position=(0, 32 * j))
                last = nc.tensor.matmul(OT[rows, g % 2, P:L], V[par][:, 1, h, :], PT[:, g % 2, 1024 + j * P:1024 + (j + 1) * P],
                                        start=False, stop=True, tile_position=(0, 32 * j))
            last.then_inc(pv.sem, 1)

        def pass2(c, par):
            pe.wait_ge(nm_in.sem, nm_in.at(c, 16))
            for g in range(GROUPS):
                S_ = SS[g % 2]
                if g < 2:
                    pe.wait_ge(max_done.sem, max_done.at(c, 2 * (g + 3)))
                else:
                    pe.wait_ge(exp_done.sem, exp_done.at(c, g - 1))
                for b in range(2):
                    bank = S_[:, 512 * b:512 * (b + 1)]
                    nc.tensor.matmul(bank, identb[:], mask2[:, 1, :], start=True, stop=False)
                    for j in range(2):
                        h = HG * g + 2 * b + j
                        nc.tensor.matmul(bank[:, j * L:(j + 1) * L], KS[par][0:KQ + 3, h, 0:P], QS[par][0:KQ + 3, h, :], start=False, stop=(j == 1))
                nc.tensor.matmul(S_[:, 1024:1536], identb[:], maskk[:].rearrange("p a b -> p (a b)"), start=True, stop=False)
                for j in range(HG):
                    h = HG * g + j
                    last = nc.tensor.matmul(S_[:, 1024 + j * P:1024 + (j + 1) * P], KS[par][0:KQ + 3, h, P:L], QS[par][0:KQ + 3, h, P:L],
                                            start=False, stop=(j == HG - 1))
                last.then_inc(p2.sem, 1)
                if g:
                    values(c, par, g - 1)
            values(c, par, GROUPS - 1)

        def epilogue(c, par):
            pe.wait_ge(ot_copied.sem, ot_copied.at(c, 2))
            if not (isinstance(c, int) and c == NSEQ - 1):
                pe.wait_ge(nm_copied.sem, nm_copied.at(c + 1, 1))
            else:
                pe.wait_ge(x_upd.sem, x_upd.at(c - 1, 1))
            for j in range(J1):
                if j:
                    pe.wait_ge(epi.sem, epi.at(c, 2))
                for g in range(GROUPS):
                    last = nc.tensor.transpose(FR[:, g * P:(g + 1) * P], OSB[:, g, j * P:(j + 1) * P], ident[:])
                last.then_inc(fr_o.sem, 1)
            pe.wait_ge(epi.sem, epi.at(c, 4))
            for j in range(J1):
                last = nc.tensor.transpose(FR[:, j * P:(j + 1) * P], YN[:, j, :, :].rearrange("p h d -> p (h d)"), ident[:])
            last.then_inc(fr_y.sem, 1)
            pe.wait_ge(yT_done.sem, yT_done.at(c, 1))
            for j in range(J1):
                last = nc.tensor.matmul(FR[:, j * P:(j + 1) * P], yT[:, j * P:(j + 1) * P], wc[:], start=True, stop=True)
            last.then_inc(fr_wc.sem, 1)

        schedule(pe, front, pass1, pass2, epilogue)

    @block.scalar
    def _(act):
        for s in (xT_done, v_done, part_done, nm_copied, exp_done, ot_copied, yT_done):
            act.sem_inc(s.sem, 2 * s.per)
        for n in range(3):
            act.wait_ge(wT, n + 1)
            nc.scalar.copy(WDT, SS[0][:, 0:1024]).then_inc(wTc, 1)
            act.wait_ge(wE, n + 1)
            e = SS[1][:, 0:256].rearrange("p (b r d) -> p b r d", r=2, d=2 * DH)
            if n == 2:
                nc.scalar.copy(wvg[:, 0:P].rearrange("p (b d) -> p b d", b=8), e[:, :, 0, :]).then_inc(wTc, 1)
            else:
                nc.scalar.copy((wq, wk)[n][:].rearrange("p (b d) -> p b d", b=8), e[:, :, 0, :])
                nc.scalar.copy((wqr, wkr)[n][:].rearrange("p (b d) -> p b d", b=8), e[:, :, 1, :]).then_inc(wTc, 1)
        act.wait_ge(poolset, 2)
        act.wait_ge(stat_step, 7)
        nc.scalar.activation(stats[:, :, 0], q1[:], ACT.Sqrt).then_inc(root_done, 1)

        def front(c, par):
            act.wait_ge(fr_x.sem, fr_x.at(c, 1))
            nc.scalar.copy(xnT[:], FR[:, 0:L]).then_inc(xT_done.sem, 1)
            act.wait_ge(fr_vg.sem, fr_vg.at(c, 1))
            act.wait_ge(pv.sem, pv.at(c - 2, GROUPS))
            vg = FR[:].rearrange("p (j v h d) -> p j v h d", j=J1, v=2, d=DH)
            for j in range(J1):
                last = nc.scalar.copy(V[par][:, j, :, 0:DH], vg[:, j, 0, :, :])
            last.then_inc(v_done.sem, 1)
            act.wait_ge(rest.sem, rest.at(c, 1))
            act.wait_ge(parts_out.sem, parts_out.at(c - 1, 16))
            nc.scalar.copy(SPL[:, 0], QK[:]).then_inc(part_done.sem, 1)
            act.wait_ge(rest.sem, rest.at(c, 2))
            nc.scalar.copy(SPL[:, 1], R1[:]).then_inc(part_done.sem, 1)

        def pass1(c, par):
            act.wait_ge(fr_nm.sem, fr_nm.at(c, 1))
            act.wait_ge(nm_out.sem, nm_out.at(c - 1, 16))
            nc.scalar.copy(NMT[:], FRb[0:3 * HEADS, 0:L]).then_inc(nm_copied.sem, 1)

        def pass2(c, par):
            def out_copy(k):
                act.wait_ge(pv.sem, pv.at(c, 2 * k + 2))
                act.wait_ge(fr_o.sem, fr_o.at(c - 1, 2))
                nc.scalar.copy(OSB[:, 2 * k:2 * k + 2, :], OT[:]).then_inc(ot_copied.sem, 1)

            for g in range(GROUPS):
                act.wait_ge(p2.sem, p2.at(c, g + 1))
                act.wait_ge(pv.sem, pv.at(c, g - 1))
                nc.scalar.activation(PT[:, g % 2, :], SS[g % 2][:], ACT.Exp, scale=SCALE).then_inc(exp_done.sem, 1)
                if g == 2:
                    out_copy(0)
            out_copy(1)

        def epilogue(c, par):
            act.wait_ge(fr_y.sem, fr_y.at(c, 1))
            act.wait_ge(fr_wc.sem, fr_wc.at(c - 1, 1))
            nc.scalar.copy(yT[:], FR[:, 0:L]).then_inc(yT_done.sem, 1)

        schedule(act, front, pass1, pass2, epilogue)

    @block.gpsimd
    def _(pool):
        pool.sem_inc(xn_ready.sem, 2 * xn_ready.per)
        pool.sem_inc(rest.sem, 2 * rest.per)
        nc.gpsimd.memset(BD[:], 0.0).then_inc(cleared, 1)
        nc.gpsimd.memset(zeros[:], 0.0)
        nc.gpsimd.memset(ones[:], 1.0)
        nc.gpsimd.memset(carry[:], 0.0)
        for i in range(2):
            nc.gpsimd.memset(V[i][:], 1.0).then_inc(poolset, 1)
        pool.wait_ge(stat_step, 12)

        def front(c, par):
            def wide(v):
                return v[:, bass.ds(c * J1, J1)].unsqueeze(2).to_broadcast([P, J1, D])

            pool.wait_ge(fr_x.sem, fr_x.at(c - 2, 1))
            pool.wait_ge(xn_stored.sem, xn_stored.at(c - 2, 16))
            nc.gpsimd.tensor_tensor(XM[:], X[:, bass.ds(c * J1, J1), :], wide(mean), ALU.subtract).then_inc(xn_ready.sem, 1)
            pool.wait_ge(xn_ready.sem, xn_ready.at(c, 1))
            nc.gpsimd.tensor_tensor(XN[:, par], XM[:], wide(rstd), ALU.mult).then_inc(xn_ready.sem, 1)
            pool.wait_ge(rope.sem, rope.at(c, 2))
            nc.gpsimd.tensor_tensor(QK[:], t1[:], t2[:], ALU.add).then_inc(rest.sem, 1)
            pool.wait_ge(part_done.sem, part_done.at(c, 1))
            nc.gpsimd.tensor_tensor(R1[:], QK[:], SPL[:, 0], ALU.subtract).then_inc(rest.sem, 1)
            pool.wait_ge(part_done.sem, part_done.at(c, 2))
            nc.gpsimd.tensor_tensor(SPL[:, 2], R1[:], SPL[:, 1], ALU.subtract).then_inc(rest.sem, 1)

        schedule(pool, front, nothing, nothing, nothing)

    @block.vector
    def _(dve):
        for s in (top, rope, route, max_done, nm_step, epi, x_upd):
            dve.sem_inc(s.sem, 2 * s.per)
        nc.vector.memset(OT[:], 0.0)
        nc.vector.memset(NMS[:], 0.0)
        for i in range(2):
            nc.vector.memset(KS[i][32:64], 1.0)
        token_stats(nc, dve, X, stats, mean, rstd, q1, q2, stat_step, root_done)
        dve.wait_ge(poolset, 2)

        def front(c, par):
            dve.wait_ge(v_done.sem, v_done.at(c, 1))
            dve.sem_inc(paced, 1)
            for j in range(J1):
                nc.vector.max(mx[:, j, :], FR[:, (2 * j + 1) * P:(2 * j + 2) * P]).then_inc(top.sem, 1)
            dve.wait_ge(top.sem, top.at(c, J1))
            dve.sem_inc(paced, 1)
            for j in range(J1):
                nc.vector.max_index(ix[:, j, :], mx[:, j, :], FR[:, (2 * j + 1) * P:(2 * j + 2) * P]).then_inc(top.sem, 1)
            dve.wait_ge(fr_qk.sem, fr_qk.at(c, 1))
            dve.wait_ge(rest.sem, rest.at(c - 1, 1))
            wide = lambda v: v[:].unsqueeze(1).to_broadcast([P, 2, L])
            fr = FR[:].rearrange("p (q t) -> p q t", q=2)
            nc.vector.tensor_tensor(t1[:], fr, wide(cos), ALU.mult).then_inc(rope.sem, 1)
            dve.wait_ge(fr_rot.sem, fr_rot.at(c, 1))
            nc.vector.tensor_tensor(t2[:], fr, wide(sin), ALU.mult).then_inc(rope.sem, 1)

            def step(ins, k):
                ins.then_inc(route.sem, 1)
                dve.wait_ge(route.sem, route.at(c, k))

            step(nc.vector.tensor_copy(ef[:], ix[:, :, 0:2]), 1)
            tiles = bass.ds(c * J1, J1)
            step(nc.vector.tensor_copy(EF[:, tiles, :], ef[:]), 2)
            step(nc.vector.tensor_copy(EU[:, tiles, :], ix[:, :, 0:2]), 3)
            step(nc.vector.tensor_tensor(MK[:], iota[:].unsqueeze(1).unsqueeze(1).to_broadcast([P, J1, 2, P]),
                                         ef[:].unsqueeze(3).to_broadcast([P, J1, 2, P]), ALU.is_equal), 4)
            for j in range(J1):
                dve.wait_ge(fr_route.sem, fr_route.at(c, j + 1))
                fv = FR[:].rearrange("p (s e) -> p s e", e=P)
                k = 4 + 4 * j
                step(nc.vector.tensor_tensor(cs[:], fv[:, 0:2, :], carry[:], ALU.add), k + 1)
                step(nc.vector.tensor_tensor(carry[:], fv[:, 2:4, :], carry[:], ALU.add), k + 2)
                step(nc.vector.tensor_tensor(cs[:], cs[:], MK[:, j, :, :], ALU.mult), k + 3)
                step(nc.vector.tensor_reduce(loc[:, j, :], cs[:], AX.X, ALU.add), k + 4)
            nc.vector.tensor_copy(LG[:, tiles, :], mx[:, :, 0:2])
            nc.vector.tensor_copy(LOC[:, tiles, :], loc[:]).then_inc(route.sem, 1)

        def pass1(c, par):
            for g in range(GROUPS):
                dve.wait_ge(p1.sem, p1.at(c, g + 1))
                if g == 0:
                    dve.wait_ge(nm_step.sem, nm_step.at(c - 1, 4))
                nc.vector.tensor_reduce(NM[:, 0, HG * g:HG * g + HG], SS[g % 2][:, 0:512].rearrange("p (h k) -> p h k", h=HG),
                                        AX.X, ALU.max, negate=True).then_inc(max_done.sem, 1)
                nc.vector.tensor_reduce(NM[:, 1, HG * g:HG * g + HG], SS[g % 2][:, 512:1536].rearrange("p (h k) -> p h k", h=HG),
                                        AX.X, ALU.max, negate=True).then_inc(max_done.sem, 1)
            dve.wait_ge(max_done.sem, max_done.at(c, 8))
            dve.wait_ge(fr_nm.sem, fr_nm.at(c - 1, 1))
            nc.vector.tensor_copy(NMS[:, :, 0, :], NM[:]).then_inc(nm_step.sem, 1)
            dve.wait_ge(nm_step.sem, nm_step.at(c, 1))
            nc.vector.tensor_tensor(NR[:], NM[:], NMS[:, :, 0, :], ALU.subtract).then_inc(nm_step.sem, 1)
            dve.wait_ge(nm_step.sem, nm_step.at(c, 2))
            nc.vector.tensor_copy(NMS[:, :, 1, :], NR[:]).then_inc(nm_step.sem, 1)
            dve.wait_ge(nm_step.sem, nm_step.at(c, 3))
            nc.vector.tensor_tensor(NMS[:, :, 2, :], NR[:], NMS[:, :, 1, :], ALU.subtract).then_inc(nm_step.sem, 1)

        def epilogue(c, par):
            for j in range(J1):
                dve.wait_ge(fr_o.sem, fr_o.at(c, j + 1))
                if j == 0:
                    dve.wait_ge(fr_y.sem, fr_y.at(c - 1, 1))
                else:
                    dve.wait_ge(epi.sem, epi.at(c, 2))
                o = FR[:].rearrange("p (h w) -> p h w", w=32)
                nc.vector.reciprocal(rec[:], o[:, :, DH]).then_inc(epi.sem, 1)
                dve.wait_ge(epi.sem, epi.at(c, 2 * j + 1))
                nc.vector.tensor_tensor(YN[:, j, :, :], o[:, :, 0:DH], rec[:].unsqueeze(2).to_broadcast([P, HEADS, DH]),
                                        ALU.mult).then_inc(epi.sem, 1)
            dve.wait_ge(fr_wc.sem, fr_wc.at(c, 1))
            xs = X[:, bass.ds(c * J1, J1), :]
            nc.vector.tensor_tensor(xs, FR[:, 0:L].rearrange("p (j d) -> p j d", j=J1), xs, ALU.add).then_inc(x_upd.sem, 1)

        schedule(dve, front, pass1, nothing, epilogue)


def experts1(nc, ctx, t, dram, scratch, out):
    def sb(name, shape, dt=F32):
        return ctx.enter_context(nc.sbuf_tensor(name, shape, dt))

    def sem(name):
        return ctx.enter_context(nc.semaphore(name))

    X, ident, WE, carry, iota = t["X"], t["ident"], t["WE"], t["carry"], t["iota"]
    EF, EU, LG, LOC = t["EF"], t["EU"], t["LG"], t["LOC"]
    xn_d, y_d = scratch["xn"], scratch["y"]
    U32 = mybir.dt.uint32
    NG = NSLOT // P
    NV = 5
    FAR = float(1 << 20)
    off = sb("off", [P, NT]); junk = sb("junk", [P, 2, P])
    W = sb("W", [P, NT, 2]); wd = sb("wd", [P, NT]); wr = sb("wr", [P, NT, 2])
    VAL = sb("VAL", [P, NT, 2, NV], BF16)
    lo_u = sb("lo_u", [P, NT, 2], U32); hi_u = sb("hi_u", [P, NT, 2], U32)
    lo_e = sb("lo_e", [P, NT, 2]); hi_e = sb("hi_e", [P, NT, 2]); ok = sb("ok", [P, NT, 2])
    A = sb("A1", [P, 2, 2, 2, P], BF16); G = sb("G1", [P, 2, 4, NG], BF16); R = sb("R1c", [P, 2, 4, NV, NG], BF16)
    mhi = sb("mhi", [P, NG]); mlo = sb("mlo", [P, NG]); mw = sb("mw", [P, NG]); m1 = sb("m1", [P, NG]); m2 = sb("m2", [P, NG])
    gi = sb("gi", [P, NG], U32); si = sb("si", [P, NG], U32)
    XG = sb("XG", [P, NG, D]); XGT = sb("XGT", [P, 2, 4, P]); YB = sb("YB", [P, 2, 4, D])
    YC = sb("YC", [P, 2, 2, 8, D])
    MAP = ctx.enter_context(nc.psum_tensor("MAP", [P, 512], F32))
    TR = [ctx.enter_context(nc.psum_tensor(f"TR{i}", [P, 512], F32)) for i in range(2)]
    EO = [ctx.enter_context(nc.psum_tensor(f"EO{i}", [P, 512], F32)) for i in range(2)]

    val_loaded = sem("val_loaded"); offs = sem("offs"); bulk = sem("bulk"); gexp = sem("gexp1"); onehot = sem("onehot")
    told = sem("told"); mapped = sem("mapped"); decoded = sem("decoded"); gathered = [sem(f"gathered{i}") for i in range(8)]
    blank = sem("blank"); transposed = sem("transposed"); tr_copied = sem("tr_copied"); applied = sem("applied"); weighted = sem("weighted")
    scattered = [sem(f"scattered{i}") for i in range(2)]; y_loaded = [sem(f"y_loaded{i}") for i in range(2)]; half_added = sem("half_added"); added = sem("added")
    stored = sem("stored")

    block = ctx.enter_context(nc.Block())

    @block.sync
    def _(sp):
        sp.dma_start(VAL[:, :, :, 0:2], dram["c_rowval"].rearrange("p (i c v) -> p i c v", c=2, v=2), allow_slow_non_contiguous=True).then_inc(val_loaded, 16)
        yv, ov = y_d.rearrange("(c i p) d -> p c i d", c=2, p=P), out.rearrange("(i p) d -> p i d", p=P)
        for i in range(2):
            sp.wait_ge(scattered[i], 16 * NG // 2)
        for g in range(8):
            if g >= 2:
                sp.wait_ge(added, g - 1)
            for c in range(2):
                sp.dma_start(YC[:, g % 2, c, :, :], yv[:, c, 8 * g:8 * g + 8, :]).then_inc(y_loaded[g % 2], 16)
            if g:
                sp.wait_ge(added, g)
                sp.dma_start(ov[:, 8 * g - 8:8 * g, :], X[:, 8 * g - 8:8 * g, :]).then_inc(stored, 16)
        sp.wait_ge(added, 8)
        sp.dma_start(ov[:, 56:64, :], X[:, 56:64, :]).then_inc(stored, 16)
        sp.wait_ge(stored, 16 * 8)

    @block.tensor
    def _(pe):
        for i in range(NT // 2):
            pe.wait_ge(told, i + 1)
            for k in range(4):
                last = nc.tensor.matmul(MAP[:, 0:NV * NG], A[:, i % 2, k // 2, k % 2, :], R[:, i % 2, k, :, :].rearrange("p v g -> p (v g)"),
                                        start=(i == 0 and k == 0), stop=(i == NT // 2 - 1 and k == 3))
            last.then_inc(mapped, 1)
        for b in range(8):
            pe.wait_ge(gathered[b], 64)
            if b >= 2:
                pe.wait_ge(tr_copied, b - 1)
            for k in range(4):
                last = nc.tensor.transpose(TR[b % 2][:, k * P:(k + 1) * P], XG[:, 4 * b + k, :], ident[:])
            last.then_inc(transposed, 1)
            pe.wait_ge(tr_copied, b + 1)
            if b >= 2:
                pe.wait_ge(weighted, b - 1)
            for k in range(4):
                for j in range(4):
                    e = 4 * (4 * b + k) + j
                    last = nc.tensor.matmul(EO[b % 2][32 * j:32 * j + 32, k * P:(k + 1) * P], XGT[:, b % 2, k, 32 * j:32 * j + 32], WE[:, e, :],
                                            start=True, stop=True, tile_position=(0, 32 * j))
            last.then_inc(applied, 1)

    @block.scalar
    def _(act):
        act.wait_ge(bulk, 1)
        nc.scalar.activation(wd[:], wd[:], ACT.Exp).then_inc(gexp, 1)
        for b in range(8):
            act.wait_ge(transposed, b + 1)
            if b >= 2:
                act.wait_ge(applied, b - 1)
            nc.scalar.copy(XGT[:, b % 2].rearrange("p k q -> p (k q)"), TR[b % 2][:]).then_inc(tr_copied, 1)

    @block.gpsimd
    def _(pool):
        nc.gpsimd.memset(XG[:], 0.0).then_inc(blank, 1)
        for i in range(NT // 2):
            pool.wait_ge(onehot, 2 * i + 2)
            if i >= 2:
                pool.wait_ge(mapped, i - 1)
            val = VAL[:, 2 * i:2 * i + 2, :, :].rearrange("p i c v -> p (i c) v")
            nc.gpsimd.tensor_tensor(R[:, i % 2], G[:, i % 2].unsqueeze(2).to_broadcast([P, 4, NV, NG]),
                                    val.unsqueeze(3).to_broadcast([P, 4, NV, NG]), ALU.mult).then_inc(told, 1)
        pool.wait_ge(decoded, 11)
        pool.wait_ge(blank, 1)
        for b in range(8):
            for k in range(4):
                g = 4 * b + k
                nc.gpsimd.indirect_dma_start(out=XG[:, g, :], out_offset=None, in_=xn_d, in_offset=bass.IndirectOffsetOnAxis(ap=gi[:, g:g + 1], axis=0),
                                             bounds_check=NTOK - 1, oob_is_err=False).then_inc(gathered[b], 16)
        for b in range(8):
            pool.wait_ge(weighted, b + 1)
            for k in range(4):
                g = 4 * b + k
                nc.gpsimd.indirect_dma_start(out=y_d, out_offset=bass.IndirectOffsetOnAxis(ap=si[:, g:g + 1], axis=0), in_=YB[:, b % 2, k, :], in_offset=None,
                                             bounds_check=2 * NTOK - 1, oob_is_err=False).then_inc(scattered[b % 2], 16)

    @block.vector
    def _(dve):
        nc.vector.tensor_tensor(wd[:], LG[:, :, 1], LG[:, :, 0], ALU.subtract).then_inc(bulk, 1)
        for i in range(NT):
            if i >= 2:
                dve.wait_ge(offs, i - 1)
            nc.vector.scalar_tensor_tensor(junk[:, i % 2, :], iota[:], EF[:, i, 1:2], carry[:, 0, :], ALU.is_equal, ALU.mult,
                                           accum_out=off[:, i:i + 1]).then_inc(offs, 1)
        n = [1]

        def step(ins):
            ins.then_inc(bulk, 1)
            n[0] += 1
            dve.wait_ge(bulk, n[0])

        dve.wait_ge(gexp, 1)
        dve.wait_ge(offs, NT)
        step(nc.vector.tensor_scalar(W[:, :, 0], wd[:], 1.0, None, ALU.add))
        step(nc.vector.reciprocal(W[:, :, 0], W[:, :, 0]))
        step(nc.vector.tensor_tensor(W[:, :, 1], wd[:], W[:, :, 0], ALU.mult))
        dve.wait_ge(val_loaded, 16)
        for r in range(3):
            step(nc.vector.tensor_copy(VAL[:, :, :, 2 + r], W[:]))
            if r < 2:
                step(nc.vector.tensor_tensor(W[:], W[:], VAL[:, :, :, 2 + r], ALU.subtract))
        step(nc.vector.tensor_tensor(LOC[:, :, 1], LOC[:, :, 1], off[:], ALU.add))
        step(nc.vector.tensor_scalar(ok[:], LOC[:], float(CAP) + 0.5, None, ALU.is_lt))
        step(nc.vector.tensor_single_scalar(lo_u[:], EU[:], 3, ALU.bitwise_and))
        step(nc.vector.tensor_single_scalar(hi_u[:], EU[:], 2, ALU.logical_shift_right))
        step(nc.vector.tensor_copy(lo_e[:], lo_u[:]))
        step(nc.vector.tensor_copy(hi_e[:], hi_u[:]))
        step(nc.vector.scalar_tensor_tensor(lo_e[:], lo_e[:], float(CAP), LOC[:], ALU.mult, ALU.add))
        step(nc.vector.tensor_tensor(lo_e[:], lo_e[:], ok[:], ALU.mult))
        step(nc.vector.tensor_scalar(lo_e[:], lo_e[:], -1.0, None, ALU.add))
        for i in range(NT // 2):
            if i >= 2:
                dve.wait_ge(mapped, i - 1)
                dve.wait_ge(told, i - 1)
            def wide(v, m):
                return v[:, 2 * i:2 * i + 2, :].rearrange("p i c -> p (i c)").unsqueeze(2).to_broadcast([P, 4, m])
            nc.vector.tensor_tensor(A[:, i % 2].rearrange("p i c q -> p (i c) q"), iota[:].unsqueeze(1).to_broadcast([P, 4, P]), wide(lo_e, P),
                                    ALU.is_equal).then_inc(onehot, 1)
            nc.vector.tensor_tensor(G[:, i % 2], iota[:, 0:NG].unsqueeze(1).to_broadcast([P, 4, NG]), wide(hi_e, NG), ALU.is_equal).then_inc(onehot, 1)
        dve.wait_ge(mapped, NT // 2)
        m = [0]

        def dstep(ins):
            ins.then_inc(decoded, 1)
            m[0] += 1
            dve.wait_ge(decoded, m[0])

        mv = MAP[:, 0:NV * NG].rearrange("p (v g) -> p v g", v=NV)
        dstep(nc.vector.tensor_scalar(mhi[:], mv[:, 0, :], -1.0, float(P), ALU.add, ALU.mult))
        dstep(nc.vector.tensor_tensor(mlo[:], mhi[:], mv[:, 1, :], ALU.add))
        dstep(nc.vector.tensor_scalar(m1[:], mv[:, 0, :], 0.5, FAR, ALU.is_lt, ALU.mult))
        dstep(nc.vector.tensor_tensor(mlo[:], mlo[:], m1[:], ALU.add))
        dstep(nc.vector.tensor_copy(si[:], mlo[:]))
        dstep(nc.vector.tensor_scalar(m2[:], mv[:, 0, :], NT + 0.5, -float(NTOK), ALU.is_gt, ALU.mult))
        dstep(nc.vector.tensor_tensor(mlo[:], mlo[:], m2[:], ALU.add))
        dstep(nc.vector.tensor_copy(gi[:], mlo[:]))
        dstep(nc.vector.tensor_copy(mw[:], mv[:, 2, :]))
        dstep(nc.vector.tensor_tensor(mw[:], mw[:], mv[:, 3, :], ALU.add))
        dstep(nc.vector.tensor_tensor(mw[:], mw[:], mv[:, 4, :], ALU.add))
        for b in range(8):
            dve.wait_ge(applied, b + 1)
            if b >= 2:
                dve.wait_ge(scattered[b % 2], 64 * (b // 2))
            nc.vector.tensor_tensor(YB[:, b % 2], EO[b % 2][:].rearrange("p (k d) -> p k d", k=4),
                                    mw[:, 4 * b:4 * b + 4].unsqueeze(2).to_broadcast([P, 4, D]), ALU.mult).then_inc(weighted, 1)
        for g in range(8):
            dve.wait_ge(y_loaded[g % 2], 32 * (g // 2 + 1))
            xs = X[:, 8 * g:8 * g + 8, :]
            nc.vector.tensor_tensor(xs, xs, YC[:, g % 2, 0], ALU.add).then_inc(half_added, 1)
            dve.wait_ge(half_added, g + 1)
            nc.vector.tensor_tensor(xs, xs, YC[:, g % 2, 1], ALU.add).then_inc(added, 1)


def constants():
    bf16 = np.dtype("bfloat16")
    c = {}
    c["c_ident"] = np.eye(P, dtype=np.float32)
    c["c_identb"] = np.eye(P).astype(bf16)
    sel = np.zeros((96, 2 * S, P), np.float32)
    for r in range(3):
        for n in range(2 * S):
            sel[32 * r + n, n, :] = 1
    c["c_sel"] = sel.reshape(96, -1).astype(bf16)
    c["c_tri8"] = np.tile(np.tril(np.ones((E0, E0), np.float32)).reshape(1, -1), (P, 1))
    split = np.zeros((P, 2), np.float32)
    split[32:96, 0] = -1
    split[64:96, 1] = -1
    c["c_split"] = split
    dim = DH // 2
    inv = (1.0 / np.float32(10000.0) ** (np.arange(0, dim, 2, dtype=np.float32) / np.float32(dim))).astype(np.float32)
    freqs = np.arange(L, dtype=np.float32)[:, None] * inv[None, :]
    emb = np.concatenate((freqs, freqs), axis=-1)
    cos, sin = np.ones((HEADS, DH, L), np.float32), np.zeros((HEADS, DH, L), np.float32)
    cos[:, dim:, :] = np.cos(emb).T
    sin[:, dim:, :] = (np.sin(emb) * np.array([-1, 1] * (dim // 2), np.float32)).T
    c["c_cos"], c["c_sin"] = cos.reshape(P, L), sin.reshape(P, L)
    q = np.where(np.arange(P)[None, :] <= np.arange(P)[:, None], 0, -1e30).astype(np.float32)
    none = np.zeros((P, P), np.float32)
    c["c_maskq"], c["c_maskk"] = np.tile(q, (1, HG)).astype(bf16), np.tile(q.T, (1, HG)).astype(bf16)
    c["c_mask2"] = np.concatenate([none, q, none, q, q.T, none, q.T, none], 1).astype(bf16)
    c["c_tri"] = np.triu(np.ones((P, P), np.float32)).astype(bf16)
    c["c_iota"] = np.tile(np.arange(P, dtype=np.float32), (P, 1))
    row = np.zeros((P, NT, 2, 2), np.float32)
    row[:, :, :, 0] = np.arange(NT)[None, :, None] + NT * np.arange(2)[None, None, :] + 1
    row[:, :, :, 1] = np.arange(P)[:, None, None]
    c["c_rowval"] = row.reshape(P, -1).astype(bf16)
    return c


def build(nc, dram, out):
    def scr(name, shape, dt):
        return nc.dram_tensor(name, shape, dt, kind="Internal").ap()

    scratch = {
        "xn": scr("s_xn", [NTOK, D], F32), "y": scr("s_y", [2 * NTOK, D], F32),
        "parts": [scr(f"s_parts{i}", [P, 3 * 2 * L], BF16) for i in range(2)],
        "nm": [scr(f"s_nm{i}", [3 * HEADS, L], BF16) for i in range(2)],
    }
    with ExitStack() as ctx:
        def sb(name, shape, dt=F32):
            return ctx.enter_context(nc.sbuf_tensor(name, shape, dt))

        U32 = mybir.dt.uint32
        t = {"X": sb("X", [P, NT, D]), "ident": sb("ident", [P, P]), "identb": sb("identb", [P, P], BF16)}
        with ExitStack() as c0:
            layer0(nc, c0, t, dram)
        t.update(WE=sb("WE", [P, E1, D]), carry=sb("carry", [P, 2, P]), EF=sb("EF", [P, NT, 2]), EU=sb("EU", [P, NT, 2], U32),
                 LG=sb("LG", [P, NT, 2]), LOC=sb("LOC", [P, NT, 2]), iota=sb("iota", [P, P]))
        with ExitStack() as c1:
            layer1(nc, c1, t, dram, scratch)
        with ExitStack() as c2:
            experts1(nc, c2, t, dram, scratch, out)


_INS = ['L0_attn_x', 'L0_attn_rms_w', 'L0_attn_in_proj', 'L0_attn_conv_w', 'L0_attn_conv_b', 'L0_attn_x_proj', 'L0_attn_dt_w',
        'L0_attn_dt_b', 'L0_attn_A_log', 'L0_attn_D', 'L0_attn_out_proj', 'L0_ffn_Wr', 'L0_ffn_br', 'L0_ffn_W1', 'L0_ffn_b1',
        'L0_ffn_W2', 'L0_ffn_b2', 'L1_attn_Wq_down', 'L1_attn_Wk_down', 'L1_attn_Wv_down', 'L1_attn_Wq_up_c', 'L1_attn_Wq_up_e',
        'L1_attn_Wk_up_c', 'L1_attn_Wk_up_e', 'L1_attn_Wv_up', 'L1_attn_Wc', 'L1_ffn_wg', 'L1_ffn_we']


def kernel(**inputs):
    import concourse.bacc as bacc
    from concourse.bass_utils import run_bass_kernel_spmd

    nc = bacc.Bacc("TRN2", target_bir_lowering=False, num_devices=1)
    given = {name: np.ascontiguousarray(inputs[name]) for name in _INS}
    given.update(constants())
    arrays, dram = {}, {}
    for name, a in given.items():
        arrays[f"in_{name}"] = a
        dram[name] = nc.dram_tensor(f"in_{name}", a.shape, mybir.dt.from_np(a.dtype), kind="ExternalInput").ap()
    out = nc.dram_tensor("out_0", (NTOK, D), F32, kind="ExternalOutput").ap()
    build(nc, dram, out)
    r = run_bass_kernel_spmd(nc, [arrays], core_ids=[0])
    return r.results[0]["out_0"].reshape(NTOK // L, L, D)
```

```python
from contextlib import ExitStack

import numpy as np

import concourse.bass as bass
from concourse import mybir

F32 = mybir.dt.float32
BF16 = mybir.dt.bfloat16
ALU = mybir.AluOpType
ACT = mybir.ActivationFunctionType
AX = mybir.AxisListType

P = 128
NTOK = 32 * 256
NT = NTOK // P
D = 128
L = 256
EPS = 1e-5

T0 = 512
J0 = T0 // P
IT0 = NTOK // T0
HALF = 2
S = 16
RANK = 8
E0 = 8
FB = 4
TOP_P = 0.8
B_AT, DT_AT = 64, 96


class Signal:

    def __init__(self, sem, per):
        self.sem, self.per = sem, per

    def at(self, c, k):
        return c * self.per + (2 * self.per + k)


def layer0(nc, ctx, t, dram, b_d):
    def sb(name, shape, dt=F32):
        return ctx.enter_context(nc.sbuf_tensor(name, shape, dt))

    def signal(name, per):
        return Signal(ctx.enter_context(nc.semaphore(name)), per)

    def sem(name):
        return ctx.enter_context(nc.semaphore(name))

    X = t["X"]
    ident, identb = t["ident"], t["identb"]
    inproj = sb("inproj", [P, 4 * P]); rmsw = sb("rmsw", [P, 1])
    convw = sb("convw", [P, HALF, 4]); convb = sb("convb", [P, HALF])
    xproj = sb("xproj", [P, HALF, 104]); dtw = sb("dtw", [P, HALF * P]); dtb = sb("dtb", [P, HALF])
    A = sb("A", [P, HALF, S]); Dp = sb("Dp", [P, HALF]); outproj = sb("outproj", [P, HALF, D])
    Wr = sb("Wr", [P, E0]); br = sb("br", [P, E0]); W1 = sb("W1", [P, E0, FB * P]); b1 = sb("b1", [P, E0, FB])
    W2 = sb("W2", [P, E0, FB, D]); b2 = sb("b2", [J0 * E0, J0, D])
    sel = sb("sel", [3 * S, S, P], BF16); tri8 = sb("tri8", [P, E0 * E0]); split = sb("split", [P, 2])
    stats = sb("stats", [P, NT, 6]); mean = sb("mean", [P, NT]); rstd = sb("rstd", [P, NT]); rrms = sb("rrms", [P, NT])
    q1 = sb("q1", [P, NT]); q2 = sb("q2", [P, NT])
    XN = sb("XN", [P, J0, D]); XR = sb("XR", [P, J0, D]); xrT = sb("xrT", [P, T0])
    xch = sb("xch", [P, HALF, T0]); xi = sb("xi", [P, HALF, T0]); th = sb("th", [P, HALF, T0]); tz = sb("tz", [P, HALF, T0])
    hi = sb("hi", [3 * S, T0], BF16); rest = sb("rest", [3 * S, T0]); mid = sb("mid", [3 * S, T0], BF16)
    dtB = sb("dtB", [P, T0])
    soft = sb("soft", [P, HALF, T0])
    u, lnw, one_w = xch, th, tz
    lg = sb("lg", [P, J0, E0]); pe_ = sb("pe_", [P, J0, E0]); pr = sb("pr", [P, J0, E0]); g4 = sb("g4", [P, 3, J0])
    gt = sb("gt", [P, J0, E0, E0]); eq = sb("eq", [P, J0, E0, E0]); cnt = sb("cnt", [P, J0, E0]); cum = sb("cum", [P, J0, E0])
    xnT = sb("xnT", [P, 2, T0]); zs = sb("zs", [P, 2, HALF, T0]); CC = sb("CC", [3 * S, 2, T0], BF16)
    delta = sb("delta", [P, 2, HALF, T0]); dx = sb("dx", [P, 2, HALF, T0])
    y = sb("y", [P, 2, HALF, T0]); FF = sb("FF", [P, 2, J0, D])
    gate = sb("gate", [P, 2, J0, E0]); gT = sb("gT", [J0 * E0, 2, P])
    Bs = sb("Bs", [P, 2, 2, T0]); dBx = sb("dBx", [P, 2, HALF, T0]); H = sb("H", [P, 2, HALF, T0])
    hT = sb("hT", [P, 2, FB, T0])
    dA = ctx.enter_context(nc.psum_tensor("dA", [P, HALF, T0], F32))
    UP = [ctx.enter_context(nc.psum_tensor(f"UP{i}", [P, 512], F32)) for i in range(2)]
    DN = ctx.enter_context(nc.psum_tensor("DN", [P, 512], F32))
    Cp = [ctx.enter_context(nc.psum_tensor(f"Cp{i}", [P, 512], F32)) for i in range(2)]
    FRO = ctx.enter_context(nc.psum_tensor("FRO", [P, 512], F32))

    front = signal("front", 11)
    upf = signal("upf", E0 * FB); downf = signal("downf", E0)
    cready = signal("cready", S); outf = signal("outf", 1)
    xT_copied = signal("xT_copied", 2); tanh_z = signal("tanh_z", 2); tanh_x = signal("tanh_x", 1)
    gexp = signal("gexp", 1); gT_copied = signal("gT_copied", 1); dt_copied = signal("dt_copied", 1)
    hi_done = signal("hi_done", 1); mid_done = signal("mid_done", 1); sp_done = signal("sp_done", 3)
    relu_done = signal("relu_done", E0 * FB); da_ready = signal("da_ready", 2 * S)
    conv_step = signal("conv_step", 8); gate_step = signal("gate_step", 15); z_done = signal("z_done", 2)
    xi_done = signal("xi_done", 1); rest_done = signal("rest_done", 1); cc_done = signal("cc_done", 1)
    u_done = signal("u_done", 2); log_step = signal("log_step", 4); delta_done = signal("delta_done", 1)
    scan_done = signal("scan_done", S); prod_done = signal("prod_done", S)
    add_done = signal("add_done", S); acc_done = signal("acc_done", E0); yz_done = signal("yz_done", 1)
    x_done = signal("x_done", 1)
    xn_ready = signal("xn_ready", 4); dbx_ready = signal("dbx_ready", S); y_init = signal("y_init", 1)
    dx_done = signal("dx_done", 1)
    b_stored = signal("b_stored", 16); b_loaded = [signal(f"b_loaded{i}", 16 * S // 4) for i in range(2)]
    loaded = sem("loaded"); xloaded = sem("xloaded"); zeroed = sem("zeroed"); stat_step = sem("stat_step")
    root_done = sem("root_done"); prep = sem("prep"); aexp = sem("aexp"); paced = sem("paced0"); sp_paced = sem("sp_paced")

    block = ctx.enter_context(nc.Block())

    loads = [
        (rmsw[:], dram["L0_attn_rms_w"].rearrange("(p a) -> p a", a=1)),
        (inproj[:], dram["L0_attn_in_proj"]),
        (ident[:], dram["c_ident"]), (identb[:], dram["c_identb"]), (sel[:].rearrange("p a b -> p (a b)"), dram["c_sel"]),
        (tri8[:], dram["c_tri8"]), (split[:], dram["c_split"]),
        (convw[:], dram["L0_attn_conv_w"].rearrange("(h p) k -> p h k", p=P)),
        (convb[:], dram["L0_attn_conv_b"].rearrange("(h p) -> p h", p=P)),
        (dtb[:], dram["L0_attn_dt_b"].rearrange("(h p) -> p h", p=P)),
        (dtw[DT_AT:DT_AT + RANK, :], dram["L0_attn_dt_w"]),
        (A[:], dram["L0_attn_A_log"].rearrange("(h p) s -> p h s", p=P)),
        (Dp[:], dram["L0_attn_D"].rearrange("(h p) -> p h", p=P)),
        (outproj[:], dram["L0_attn_out_proj"].rearrange("(h p) n -> p h n", p=P)),
        (Wr[:], dram["L0_ffn_Wr"]),
        (br[:], dram["L0_ffn_br"].rearrange("(a e) -> a e", a=1).to_broadcast([P, E0])),
        (W1[:], dram["L0_ffn_W1"].rearrange("e p f -> p e f")),
        (b1[:], dram["L0_ffn_b1"].rearrange("e (b p) -> p e b", p=P)),
        (W2[:].rearrange("p e b n -> p (e b) n"), dram["L0_ffn_W2"].rearrange("e (b p) n -> p (e b) n", p=P)),
    ]
    xp = dram["L0_attn_x_proj"].rearrange("(h p) n -> p h n", p=P)
    for r in range(3):
        loads.append((xproj[:, :, S * r:S * r + S], xp[:, :, RANK + S:RANK + 2 * S]))
    loads.append((xproj[:, :, B_AT:B_AT + S], xp[:, :, RANK:RANK + S]))
    loads.append((xproj[:, :, DT_AT:DT_AT + RANK], xp[:, :, 0:RANK]))

    def pipeline(fore, start, slot, end, eng):
        for s in range(S):
            fore(s, 0, 0)
        start()
        for s in range(S):
            slot(s, 0, 0, first=True)
            fore(s, 1, 1)
        with eng.Fori(0, IT0 // 2 - 1) as i:
            for k in range(2):
                it, par = i * 2 + (1 + k), 1 - k
                for s in range(S):
                    slot(s, it, par)
                    fore(s, it + 1, 1 - par)
        for s in range(S):
            slot(s, IT0 - 1, 1, final=True)
        end(IT0 - 1, 1)

    @block.sync
    def _(sp):
        xd = dram["L0_attn_x"].rearrange("b (j p) d -> p (b j) d", p=P)
        for g in range(8):
            sp.dma_start(X[:, 8 * g:8 * g + 8, :], xd[:, 8 * g:8 * g + 8, :]).then_inc(xloaded, 16)
        sp.wait_ge(zeroed, 1)
        for dst, src in loads:
            sp.dma_start(dst, src, allow_slow_non_contiguous=True).then_inc(loaded, 16)
        for j in range(J0):
            sp.dma_start(b2[E0 * j:E0 * j + E0, j, :], dram["L0_ffn_b2"]).then_inc(loaded, 16)
        for s in (b_stored, *b_loaded):
            sp.sem_inc(s.sem, 2 * s.per)

        def load_b(k, it, par):
            src = b_d[par if k < S // 2 else 1 - par]
            if k == S // 2:
                sp.wait_ge(b_stored.sem, b_stored.at(it + 1, 16))
                sp.sem_inc(sp_paced, 1)
            sp.wait_ge(dbx_ready.sem, dbx_ready.at(it, 2 * k - 2))
            pair = 2 * k % S
            sp.dma_start(Bs[:, k % 2], src[pair:pair + 2, :].unsqueeze(0).to_broadcast([P, 2, T0])).then_inc(b_loaded[k % 2].sem, 16)

        def slot(s, it, par, first=False, final=False):
            if s % 2 == 1 and not (final and s + 3 >= S):
                load_b((s + 3) // 2, it, par)

        def fore(s, n, q):
            if s == 9:
                sp.wait_ge(dt_copied.sem, dt_copied.at(n, 1))
                sp.dma_start(b_d[q], dtB[B_AT:B_AT + S, :]).then_inc(b_stored.sem, 16)

        def start():
            load_b(S // 2, -1, 1)
            load_b(S // 2 + 1, -1, 1)

        pipeline(fore, start, slot, lambda it, par: None, sp)

    LOADED = 16 * (len(loads) + J0)

    @block.tensor
    def _(pe):
        for s in (front, upf, downf, cready, outf):
            pe.sem_inc(s.sem, 2 * s.per)
        pe.wait_ge(loaded, LOADED)
        pe.wait_ge(prep, 1)

        def up(e, it, par, blocks):
            q = par if e < E0 else 1 - par
            if e == E0 and blocks[0] == 0:
                pe.wait_ge(xT_copied.sem, xT_copied.at(it + 1, 1))
            for f in blocks:
                k = e * FB + f
                pe.wait_ge(relu_done.sem, relu_done.at(it, k - 1))
                nc.tensor.matmul(UP[k % 2][:], W1[:, e % E0, f * P:(f + 1) * P], xnT[:, q, :], start=True, stop=True).then_inc(upf.sem, 1)

        def down(e, it, tiles):
            if tiles[0] == 0:
                pe.wait_ge(relu_done.sem, relu_done.at(it, (e + 1) * FB))
                pe.wait_ge(acc_done.sem, acc_done.at(it, e))
            for j in tiles:
                for f in range(FB):
                    last = nc.tensor.matmul(DN[:, j * P:(j + 1) * P], hT[:, e % 2, f, j * P:(j + 1) * P], W2[:, e, f, :],
                                            start=(f == 0), stop=(f == FB - 1))
            if tiles[-1] == J0 - 1:
                last.then_inc(downf.sem, 1)

        def output(it, par, last_one=False):
            if not last_one:
                pe.wait_ge(gT_copied.sem, gT_copied.at(it + 1, 1))
            pe.wait_ge(yz_done.sem, yz_done.at(it, 1))
            for j in range(J0):
                nc.tensor.matmul(FRO[:, j * P:(j + 1) * P], gT[:, par, :], b2[:, j, :], start=True, stop=False)
                for h in range(HALF):
                    last = nc.tensor.matmul(FRO[:, j * P:(j + 1) * P], y[:, par, h, j * P:(j + 1) * P], outproj[:, h, :],
                                            start=False, stop=(h == 1))
            last.then_inc(outf.sem, 1)

        def make_c(s, it, par):
            q = par if s < S else 1 - par
            if s == S:
                pe.wait_ge(cc_done.sem, cc_done.at(it + 1, 1))
            pe.wait_ge(prod_done.sem, prod_done.at(it, s - 1))
            nc.tensor.matmul(Cp[s % 2][:], sel[:, s % S, :], CC[:, q, :], start=True, stop=True).then_inc(cready.sem, 1)

        def start():
            up(E0, -1, 1, range(FB))
            make_c(S, -1, 1)

        def slot(s, it, par, first=False, final=False):
            more_up = not (final and s == S - 2)
            if s % 2 == 1:
                down(s // 2, it, range(0, 2))
            elif more_up:
                up(s // 2 + 1, it, par, range(0, 2))
            if not (final and s + 1 >= S):
                make_c(s + 1, it, par)
            if s % 2 == 1:
                down(s // 2, it, range(2, J0))
            elif more_up:
                up(s // 2 + 1, it, par, range(2, FB))
            if s == 0 and not first:
                output(it - 1, 1 - par)

        def fore(s, n, q):
            if s == 1:
                pe.wait_ge(xn_ready.sem, xn_ready.at(n, 2))
                pe.wait_ge(gT_copied.sem, gT_copied.at(n - 1, 1))
                pe.wait_ge(x_done.sem, x_done.at(n - 2, 1))
                for j in range(J0):
                    last = nc.tensor.transpose(FRO[:, j * P:(j + 1) * P], XN[:, j, :], ident[:])
                last.then_inc(front.sem, 1)
            elif s == 2:
                pe.wait_ge(xn_ready.sem, xn_ready.at(n, 3))
                pe.wait_ge(xT_copied.sem, xT_copied.at(n, 1))
                for j in range(J0):
                    last = nc.tensor.transpose(FRO[:, j * P:(j + 1) * P], XR[:, j, :], ident[:])
                last.then_inc(front.sem, 1)
            elif 3 <= s < 7:
                k = s - 3
                b = (0, 2, 1, 3)[k]
                if k == 0:
                    pe.wait_ge(xT_copied.sem, xT_copied.at(n, 2))
                elif k == 2:
                    pe.wait_ge(z_done.sem, z_done.at(n, 1))
                else:
                    pe.wait_ge(conv_step.sem, conv_step.at(n, 4 * (b - 1)))
                nc.tensor.matmul(FRO[:], inproj[:, b * P:(b + 1) * P], xrT[:], start=True, stop=True).then_inc(front.sem, 1)
            elif s == 7:
                pe.wait_ge(z_done.sem, z_done.at(n, 2))
                for j in range(J0):
                    last = nc.tensor.matmul(FRO[:, j * E0:(j + 1) * E0], xnT[:, q, j * P:(j + 1) * P], Wr[:], start=True, stop=True)
                last.then_inc(front.sem, 1)
            elif s == 8:
                pe.wait_ge(xi_done.sem, xi_done.at(n, 1))
                pe.wait_ge(gate_step.sem, gate_step.at(n, 1))
                for h in range(HALF):
                    last = nc.tensor.matmul(FRO[0:DT_AT + RANK, :], xproj[:, h, :], xi[:, h, :], start=(h == 0), stop=(h == 1))
                last.then_inc(front.sem, 1)
            elif s == 9 or s == 10:
                h = s - 9
                if h == 0:
                    pe.wait_ge(dt_copied.sem, dt_copied.at(n, 1))
                    pe.wait_ge(rest_done.sem, rest_done.at(n, 1))
                else:
                    pe.wait_ge(u_done.sem, u_done.at(n, 1))
                nc.tensor.matmul(FRO[:], dtw[DT_AT:DT_AT + RANK, h * P:(h + 1) * P], dtB[DT_AT:DT_AT + RANK, :], start=True, stop=True).then_inc(front.sem, 1)
            elif s == 11:
                pe.wait_ge(gate_step.sem, gate_step.at(n, 15))
                pe.wait_ge(u_done.sem, u_done.at(n, 2))
                nc.tensor.transpose(FRO[0:J0 * E0, 0:P], gate[:, q].rearrange("p j e -> p (j e)"), ident[:]).then_inc(front.sem, 1)

        pipeline(fore, start, slot, lambda it, par: output(it, par, last_one=True), pe)

    @block.scalar
    def _(act):
        for s in (xT_copied, tanh_z, tanh_x, gexp, gT_copied, dt_copied, hi_done, mid_done, sp_done, relu_done, da_ready):
            act.sem_inc(s.sem, 2 * s.per)
        act.wait_ge(loaded, LOADED)
        nc.scalar.activation(A[:], A[:], ACT.Exp).then_inc(aexp, 1)
        act.wait_ge(stat_step, 7)
        nc.scalar.activation(stats[:, :, 0], q1[:], ACT.Sqrt).then_inc(root_done, 1)
        act.wait_ge(stat_step, 15)
        nc.scalar.activation(stats[:, :, 0], q2[:], ACT.Sqrt).then_inc(root_done, 1)
        act.wait_ge(prep, 1)

        def make_da(s, it, par):
            q = par if s < S else 1 - par
            if s == S:
                act.wait_ge(delta_done.sem, delta_done.at(it + 1, 1))
            act.wait_ge(scan_done.sem, scan_done.at(it, s))
            for h in range(HALF):
                nc.scalar.activation(dA[:, h, :].rearrange("p (b l) -> p b l", l=L)[:, :, 1:L],
                                     delta[:, q, h, :].rearrange("p (b l) -> p b l", l=L)[:, :, 1:L],
                                     ACT.Exp, scale=A[:, h, s % S:s % S + 1]).then_inc(da_ready.sem, 1)

        def relus(e, it, blocks):
            for f in blocks:
                k = e * FB + f
                act.wait_ge(upf.sem, upf.at(it, k + 1))
                if f == 0:
                    act.wait_ge(downf.sem, downf.at(it, e - 1))
                nc.scalar.activation(hT[:, e % 2, f, :], UP[k % 2][:], ACT.Relu, bias=b1[:, e % E0, f:f + 1]).then_inc(relu_done.sem, 1)

        def start():
            relus(E0, -1, range(FB))
            make_da(S, -1, 1)

        def slot(s, it, par, first=False, final=False):
            ups = s % 2 == 0 and not (final and s == S - 2)
            if ups:
                relus(s // 2 + 1, it, range(0, 2))
            if not (final and s + 1 >= S):
                make_da(s + 1, it, par)
            if ups:
                relus(s // 2 + 1, it, range(2, FB))

        def fore(s, n, q):
            if s == 2:
                act.wait_ge(upf.sem, upf.at(n - 2, E0 * FB))
                act.wait_ge(front.sem, front.at(n, 1))
                nc.scalar.copy(xnT[:, q, :], FRO[:]).then_inc(xT_copied.sem, 1)
            elif s == 3:
                act.wait_ge(front.sem, front.at(n, 2))
                nc.scalar.copy(xrT[:], FRO[:]).then_inc(xT_copied.sem, 1)
            elif s == 5 or s == 7:
                b = (s - 5) // 2
                if b == 0:
                    act.wait_ge(delta_done.sem, delta_done.at(n - 1, 1))
                act.wait_ge(front.sem, front.at(n, 4 + 2 * b))
                nc.scalar.activation(tz[:, b, :], FRO[:], ACT.Tanh, scale=0.5).then_inc(tanh_z.sem, 1)
                if b == 1:
                    act.wait_ge(conv_step.sem, conv_step.at(n, 8))
                    nc.scalar.activation(th[:], xch[:], ACT.Tanh).then_inc(tanh_x.sem, 1)
            elif s == 8:
                act.wait_ge(gate_step.sem, gate_step.at(n, 3))
                nc.scalar.activation(pe_[:], lg[:], ACT.Exp).then_inc(gexp.sem, 1)
            elif s == 9:
                act.wait_ge(front.sem, front.at(n, 8))
                act.wait_ge(b_stored.sem, b_stored.at(n - 1, 16))
                nc.scalar.copy(dtB[B_AT:DT_AT + RANK, :], FRO[B_AT:DT_AT + RANK, :]).then_inc(dt_copied.sem, 1)
                nc.scalar.copy(hi[:], FRO[0:3 * S, :]).then_inc(hi_done.sem, 1)
            elif s == 10:
                act.wait_ge(rest_done.sem, rest_done.at(n, 1))
                act.wait_ge(cc_done.sem, cc_done.at(n - 1, 1))
                nc.scalar.copy(mid[:], rest[:]).then_inc(mid_done.sem, 1)
            elif s == 12:
                act.wait_ge(outf.sem, outf.at(n - 2, 1))
                act.wait_ge(front.sem, front.at(n, 11))
                nc.scalar.copy(gT[:, q, :], FRO[0:J0 * E0, 0:P]).then_inc(gT_copied.sem, 1)
                act.wait_ge(u_done.sem, u_done.at(n, 2))
                nc.scalar.activation(soft[:], u[:], ACT.Abs).then_inc(sp_done.sem, 1)
                act.wait_ge(sp_done.sem, sp_done.at(n, 1))
                nc.scalar.activation(soft[:], soft[:], ACT.Exp, scale=-1.0).then_inc(sp_done.sem, 1)
            elif s == 13:
                act.wait_ge(log_step.sem, log_step.at(n, 2))
                nc.scalar.activation(lnw[:], one_w[:], ACT.Ln).then_inc(sp_done.sem, 1)

        pipeline(fore, start, slot, lambda it, par: None, act)

    @block.gpsimd
    def _(pool):
        for s in (xn_ready, dbx_ready, y_init, dx_done):
            pool.sem_inc(s.sem, 2 * s.per)
        nc.gpsimd.memset(xproj[:], 0.0)
        nc.gpsimd.memset(b2[:], 0.0).then_inc(zeroed, 1)
        pool.wait_ge(stat_step, 20)
        pool.wait_ge(prep, 1)

        def make_dbx(s, it, par):
            q = par if s < S else 1 - par
            if s == S:
                pool.wait_ge(dx_done.sem, dx_done.at(it + 1, 1))
            k = s // 2
            pool.wait_ge(b_loaded[k % 2].sem, b_loaded[k % 2].at(it, 16 * (k // 2 + 1)))
            pool.wait_ge(scan_done.sem, scan_done.at(it, s - 1))
            nc.gpsimd.tensor_tensor(dBx[:, s % 2], dx[:, q], Bs[:, k % 2, s % 2, :].unsqueeze(1).to_broadcast([P, HALF, T0]),
                                    ALU.mult).then_inc(dbx_ready.sem, 1)

        def slot(s, it, par, first=False, final=False):
            if not (final and s + 1 >= S):
                make_dbx(s + 1, it, par)

        def fore(s, n, q):
            def wide(v):
                return v[:, bass.ds(n * J0, J0)].unsqueeze(2).to_broadcast([P, J0, D])

            xs = X[:, bass.ds(n * J0, J0), :]
            if s == 0:
                pool.wait_ge(front.sem, front.at(n - 1, 2))
                pool.sem_inc(paced, 1)
                nc.gpsimd.tensor_tensor(XR[:], xs, wide(mean), ALU.subtract).then_inc(xn_ready.sem, 1)
                pool.wait_ge(xn_ready.sem, xn_ready.at(n, 1))
                nc.gpsimd.tensor_tensor(XN[:], XR[:], wide(rstd), ALU.mult).then_inc(xn_ready.sem, 1)
            elif s == 1:
                pool.wait_ge(xn_ready.sem, xn_ready.at(n, 2))
                nc.gpsimd.tensor_tensor(XR[:], XN[:], wide(rrms), ALU.mult).then_inc(xn_ready.sem, 1)
            elif s == 2:
                pool.wait_ge(x_done.sem, x_done.at(n - 2, 1))
                pool.sem_inc(paced, 1)
                nc.gpsimd.tensor_tensor(FF[:, q], XN[:], xs, ALU.add).then_inc(xn_ready.sem, 1)
            elif s == 9:
                pool.wait_ge(outf.sem, outf.at(n - 2, 1))
                pool.wait_ge(xi_done.sem, xi_done.at(n, 1))
                nc.gpsimd.tensor_tensor(y[:, q], xi[:], Dp[:].unsqueeze(2).to_broadcast([P, HALF, T0]), ALU.mult).then_inc(y_init.sem, 1)
            elif s == 13:
                pool.wait_ge(dbx_ready.sem, dbx_ready.at(n - 2, S))
                pool.wait_ge(delta_done.sem, delta_done.at(n, 1))
                nc.gpsimd.tensor_tensor(dx[:, q], delta[:, q], xi[:], ALU.mult).then_inc(dx_done.sem, 1)

        pipeline(fore, lambda: make_dbx(S, -1, 1), slot, lambda it, par: None, pool)

    @block.vector
    def _(dve):
        for s in (conv_step, gate_step, z_done, xi_done, rest_done, cc_done, u_done, log_step, delta_done,
                  scan_done, prod_done, add_done, acc_done, yz_done, x_done):
            dve.sem_inc(s.sem, 2 * s.per)
        nc.vector.memset(dA[:].rearrange("p h (b l) -> p h b l", l=L)[:, :, :, 0:1], 0.0)
        dve.wait_ge(xloaded, 16 * 8)
        token_stats(nc, dve, X, stats, mean, rstd, q1, q2, stat_step, root_done)
        dve.wait_ge(stat_step, 12)
        nc.vector.tensor_tensor(q2[:], q2[:], rstd[:], ALU.mult).then_inc(stat_step, 1)
        dve.wait_ge(stat_step, 13)
        nc.vector.tensor_tensor(q2[:], q2[:], rstd[:], ALU.mult).then_inc(stat_step, 1)
        dve.wait_ge(stat_step, 14)
        nc.vector.tensor_scalar(q2[:], q2[:], EPS, None, ALU.add).then_inc(stat_step, 1)
        inverse_root(nc, dve, rrms, q2, stats, stat_step, root_done, 15, 2)
        dve.wait_ge(loaded, LOADED)
        nc.vector.tensor_scalar(inproj[:], inproj[:], rmsw[:], None, ALU.mult)
        nc.vector.tensor_scalar(convw[:], convw[:], 0.5, None, ALU.mult)
        nc.vector.tensor_scalar(convb[:], convb[:], 0.5, None, ALU.mult)
        nc.vector.tensor_scalar(outproj[:], outproj[:], 0.5, None, ALU.mult)
        dve.wait_ge(aexp, 1)
        nc.vector.tensor_scalar(A[:], A[:], -1.0, None, ALU.mult).then_inc(prep, 1)
        dve.wait_ge(prep, 1)

        def add(s, it, par):
            if s == 0:
                dve.wait_ge(y_init.sem, y_init.at(it, 1))
            dve.wait_ge(prod_done.sem, prod_done.at(it, s + 1))
            dve.wait_ge(add_done.sem, add_done.at(it, s))
            nc.vector.tensor_tensor(y[:, par], y[:, par], H[:, s % 2], ALU.add).then_inc(add_done.sem, 1)

        def close(it, par):
            add(S - 1, it, par)
            dve.wait_ge(add_done.sem, add_done.at(it, S))
            nc.vector.tensor_tensor(y[:, par], y[:, par], zs[:, par], ALU.mult).then_inc(yz_done.sem, 1)

        def store(it, par):
            dve.wait_ge(outf.sem, outf.at(it, 1))
            dve.wait_ge(acc_done.sem, acc_done.at(it, E0))
            nc.vector.tensor_tensor(X[:, bass.ds(it * J0, J0), :], FRO[:].rearrange("p (j d) -> p j d", d=D), FF[:, par],
                                    ALU.add).then_inc(x_done.sem, 1)

        def accumulate(e, it, par):
            dve.wait_ge(downf.sem, downf.at(it, e + 1))
            dve.wait_ge(acc_done.sem, acc_done.at(it, e))
            if e == 0:
                dve.wait_ge(xn_ready.sem, xn_ready.at(it, 4))
            for j in range(J0):
                last = nc.vector.scalar_tensor_tensor(FF[:, par, j, :], DN[:, j * P:(j + 1) * P], gate[:, par, j, e:e + 1],
                                                      FF[:, par, j, :], ALU.mult, ALU.add)
            last.then_inc(acc_done.sem, 1)

        def slot(s, it, par, first=False, final=False):
            dve.wait_ge(da_ready.sem, da_ready.at(it, 2 * s + 2))
            dve.wait_ge(dbx_ready.sem, dbx_ready.at(it, s + 1))
            dve.wait_ge(add_done.sem, add_done.at(it, s - 1))
            nc.vector.tensor_tensor_scan(H[:, s % 2].rearrange("p h t -> p (h t)"), dA[:].rearrange("p h t -> p (h t)"),
                                         dBx[:, s % 2].rearrange("p h t -> p (h t)"), 0.0, ALU.mult, ALU.add).then_inc(scan_done.sem, 1)
            if s == 0 and not first:
                close(it - 1, 1 - par)
                accumulate(E0 - 1, it - 1, 1 - par)
            if s == 1 and not first:
                store(it - 1, 1 - par)
            if s > 0:
                if s % 2 == 0:
                    accumulate(s // 2 - 1, it, par)
                add(s - 1, it, par)
            dve.wait_ge(scan_done.sem, scan_done.at(it, s + 1))
            dve.wait_ge(cready.sem, cready.at(it, s + 1))
            nc.vector.tensor_tensor(H[:, s % 2], H[:, s % 2], Cp[s % 2][:].unsqueeze(1).to_broadcast([P, HALF, T0]), ALU.mult).then_inc(prod_done.sem, 1)

        def end(it, par):
            accumulate(E0 - 1, it, par)
            close(it, par)
            store(it, par)

        def seqs(ap):
            return ap.rearrange("p (b l) -> p b l", l=L)

        def over(v, n=E0):
            return v.unsqueeze(2).to_broadcast([P, J0, n])

        def delta_input(h, n):
            dve.wait_ge(front.sem, front.at(n, 9 + h))
            nc.vector.tensor_scalar(u[:, h, :], FRO[:], dtb[:, h:h + 1], None, ALU.add).then_inc(u_done.sem, 1)

        def fore(s, n, q):
            def gstep(ins, k):
                ins.then_inc(gate_step.sem, 1)
                dve.wait_ge(gate_step.sem, gate_step.at(n, k))

            other = pr[:].unsqueeze(2).to_broadcast([P, J0, E0, E0])
            this = pr[:].unsqueeze(3).to_broadcast([P, J0, E0, E0])
            if s == 4 or s == 6:
                b = (s - 4) // 2
                dve.wait_ge(front.sem, front.at(n, 3 + 2 * b))
                src, dst = seqs(FRO[:]), seqs(xch[:, b, :])
                nc.vector.tensor_scalar(xch[:, b, :], FRO[:], convw[:, b, 3:4], convb[:, b:b + 1],
                                        ALU.mult, ALU.add).then_inc(conv_step.sem, 1)
                for k in range(1, 4):
                    dve.wait_ge(conv_step.sem, conv_step.at(n, 4 * b + k))
                    nc.vector.scalar_tensor_tensor(dst[:, :, k:], src[:, :, :L - k], convw[:, b, 3 - k:4 - k], dst[:, :, k:],
                                                   ALU.mult, ALU.add).then_inc(conv_step.sem, 1)
            elif s == 5:
                dve.wait_ge(tanh_z.sem, tanh_z.at(n, 1))
                nc.vector.scalar_tensor_tensor(zs[:, q, 0, :], tz[:, 0, :], 1.0, FRO[:], ALU.add, ALU.mult).then_inc(z_done.sem, 1)
            elif s == 7:
                dve.wait_ge(tanh_x.sem, tanh_x.at(n, 1))
                dve.wait_ge(dx_done.sem, dx_done.at(n - 1, 1))
                nc.vector.scalar_tensor_tensor(xi[:], th[:], 1.0, xch[:], ALU.add, ALU.mult).then_inc(xi_done.sem, 1)
                dve.wait_ge(tanh_z.sem, tanh_z.at(n, 2))
                nc.vector.scalar_tensor_tensor(zs[:, q, 1, :], tz[:, 1, :], 1.0, FRO[:], ALU.add, ALU.mult).then_inc(z_done.sem, 1)
            elif s == 8:
                dve.wait_ge(front.sem, front.at(n, 7))
                gstep(nc.vector.tensor_tensor(lg[:], FRO[:, 0:J0 * E0].rearrange("p (j e) -> p j e", e=E0),
                                              br[:].unsqueeze(1).to_broadcast([P, J0, E0]), ALU.add), 1)
                gstep(nc.vector.tensor_reduce(g4[:, 0, :], lg[:], AX.X, ALU.max), 2)
                nc.vector.tensor_tensor(lg[:], lg[:], over(g4[:, 0, :]), ALU.subtract).then_inc(gate_step.sem, 1)
            elif s == 9:
                dve.wait_ge(hi_done.sem, hi_done.at(n, 1))
                nc.vector.scalar_tensor_tensor(rest[:], hi[:], split[0:3 * S, 0:1], FRO[0:3 * S, :], ALU.mult, ALU.add).then_inc(rest_done.sem, 1)
                dve.wait_ge(gexp.sem, gexp.at(n, 1))
                gstep(nc.vector.tensor_reduce(g4[:, 1, :], pe_[:], AX.X, ALU.add), 4)
                gstep(nc.vector.reciprocal(g4[:, 2, :], g4[:, 1, :]), 5)
                gstep(nc.vector.tensor_tensor(pr[:], pe_[:], over(g4[:, 2, :]), ALU.mult), 6)
                gstep(nc.vector.tensor_tensor(gt[:], other, this, ALU.is_gt), 7)
                gstep(nc.vector.tensor_tensor(eq[:], other, this, ALU.is_equal), 8)
                tri = tri8[:].rearrange("p (e o) -> p e o", o=E0).unsqueeze(1).to_broadcast([P, J0, E0, E0])
                gstep(nc.vector.tensor_tensor(eq[:], eq[:], tri, ALU.mult), 9)
            elif s == 10:
                delta_input(0, n)
                gstep(nc.vector.tensor_tensor(gt[:], gt[:], eq[:], ALU.add), 10)
                nc.vector.tensor_reduce(cnt[:], gt[:], AX.X, ALU.add)
                gstep(nc.vector.tensor_tensor(eq[:], gt[:], other, ALU.mult), 11)
                gstep(nc.vector.tensor_reduce(cum[:], eq[:], AX.X, ALU.add), 12)
                gstep(nc.vector.tensor_scalar(cum[:], cum[:], TOP_P, None, ALU.is_lt), 13)
                gstep(nc.vector.scalar_tensor_tensor(cum[:], cnt[:], 1.5, cum[:], ALU.is_lt, ALU.max), 14)
                nc.vector.tensor_tensor(gate[:, q], pr[:], cum[:], ALU.mult).then_inc(gate_step.sem, 1)
            elif s == 11:
                delta_input(1, n)
                dve.wait_ge(mid_done.sem, mid_done.at(n, 1))
                dve.wait_ge(cready.sem, cready.at(n - 2, S))
                nc.vector.scalar_tensor_tensor(CC[:, q, :], mid[:], split[0:3 * S, 1:2], rest[:], ALU.mult, ALU.add).then_inc(cc_done.sem, 1)
            elif s == 12:
                dve.wait_ge(sp_done.sem, sp_done.at(n, 2))
                nc.vector.tensor_scalar(one_w[:], soft[:], 1.0, None, ALU.add).then_inc(log_step.sem, 1)
                dve.wait_ge(log_step.sem, log_step.at(n, 1))
                nc.vector.scalar_tensor_tensor(soft[:], one_w[:], -1.0, soft[:], ALU.add, ALU.subtract).then_inc(log_step.sem, 1)
                dve.wait_ge(log_step.sem, log_step.at(n, 2))
                nc.vector.scalar_tensor_tensor(u[:], u[:], 0.0, soft[:], ALU.max, ALU.subtract).then_inc(log_step.sem, 1)
            elif s == 13:
                dve.wait_ge(sp_done.sem, sp_done.at(n, 3))
                nc.vector.scalar_tensor_tensor(lnw[:], one_w[:], 1.0, lnw[:], ALU.is_gt, ALU.mult).then_inc(log_step.sem, 1)
                dve.wait_ge(log_step.sem, log_step.at(n, 4))
                dve.wait_ge(da_ready.sem, da_ready.at(n - 2, 2 * S))
                nc.vector.tensor_tensor(delta[:, q], u[:], lnw[:], ALU.add).then_inc(delta_done.sem, 1)

        pipeline(fore, lambda: None, slot, end, dve)
        dve.wait_ge(x_done.sem, x_done.at(IT0 - 1, 1))




J1 = L // P
NSEQ = NTOK // L
HEADS, LAT, DH = 16, 64, 8
GROUPS = 4
HG = HEADS // GROUPS
TERMS = ((0, 0), (0, 1), (0, 2), (1, 0), (1, 1), (2, 0))
KQ = len(TERMS) * DH
SCALE = 1.0 / float(np.sqrt(DH))
E1, CAP = 128, 32
NSLOT = E1 * CAP


def token_stats(nc, dve, X, stats, mean, rstd, q1, q2, stat_step, root_done):
    for i in range(NT):
        last = nc.vector.bn_stats(stats[:, i, :], X[:, i, :])
    last.then_inc(stat_step, 1)
    dve.wait_ge(stat_step, 1)
    me, mo = stats[:, :, 1], stats[:, :, 4]
    nc.vector.tensor_tensor(q1[:], me, mo, ALU.subtract).then_inc(stat_step, 1)
    nc.vector.tensor_tensor(mean[:], me, mo, ALU.add)
    nc.vector.tensor_tensor(rstd[:], stats[:, :, 2], stats[:, :, 5], ALU.add).then_inc(stat_step, 1)
    dve.wait_ge(stat_step, 3)
    nc.vector.tensor_tensor(q2[:], q1[:], q1[:], ALU.mult)
    nc.vector.tensor_scalar(mean[:], mean[:], 0.5, None, ALU.mult).then_inc(stat_step, 1)
    dve.wait_ge(stat_step, 4)
    nc.vector.tensor_scalar(q2[:], q2[:], 0.25, None, ALU.mult).then_inc(stat_step, 1)
    dve.wait_ge(stat_step, 5)
    nc.vector.scalar_tensor_tensor(q2[:], rstd[:], 1.0 / D, q2[:], ALU.mult, ALU.add).then_inc(stat_step, 1)
    dve.wait_ge(stat_step, 6)
    nc.vector.tensor_scalar(q1[:], q2[:], EPS, None, ALU.add).then_inc(stat_step, 1)
    inverse_root(nc, dve, rstd, q1, stats, stat_step, root_done, 7, 1)


def inverse_root(nc, dve, out, v, root, stat_step, root_done, k, r):
    dve.wait_ge(root_done, r)
    nc.vector.reciprocal(out[:], root[:, :, 0]).then_inc(stat_step, 1)
    dve.wait_ge(stat_step, k + 1)
    nc.vector.tensor_tensor(root[:, :, 0], out[:], out[:], ALU.mult).then_inc(stat_step, 1)
    dve.wait_ge(stat_step, k + 2)
    nc.vector.tensor_tensor(root[:, :, 0], root[:, :, 0], v[:], ALU.mult).then_inc(stat_step, 1)
    dve.wait_ge(stat_step, k + 3)
    nc.vector.tensor_scalar(root[:, :, 0], root[:, :, 0], -0.5, 1.5, ALU.mult, ALU.add).then_inc(stat_step, 1)
    dve.wait_ge(stat_step, k + 4)
    nc.vector.tensor_tensor(out[:], out[:], root[:, :, 0], ALU.mult).then_inc(stat_step, 1)


def layer1(nc, ctx, t, dram, scratch):
    def sb(name, shape, dt=F32):
        return ctx.enter_context(nc.sbuf_tensor(name, shape, dt))

    def signal(name, per):
        return Signal(ctx.enter_context(nc.semaphore(name)), per)

    def sem(name):
        return ctx.enter_context(nc.semaphore(name))

    X, ident, identb, WE, carry = t["X"], t["ident"], t["identb"], t["WE"], t["carry"]
    EF, EU, LG, LOC, iota = t["EF"], t["EU"], t["LG"], t["LOC"], t["iota"]
    stats = sb("stats1", [P, NT, 6]); mean = sb("mean1", [P, NT]); rstd = sb("rstd1", [P, NT])
    q1 = sb("q11", [P, NT]); q2 = sb("q21", [P, NT])
    wq = sb("wq", [P, P]); wk = sb("wk", [P, P]); wqr = sb("wqr", [P, P]); wkr = sb("wkr", [P, P])
    wvg = sb("wvg", [P, 2 * P]); wc = sb("wc", [P, D])
    cos = sb("cos", [P, L]); sin = sb("sin", [P, L])
    maskq = sb("maskq", [P, HG, P], BF16); maskk = sb("maskk", [P, HG, P], BF16)
    tri = sb("tri", [P, P], BF16); ones = sb("ones", [P, P], BF16)
    XN = sb("XN2", [P, 2, J1, D]); XM = sb("XM2", [P, J1, D]); xnT = sb("xnT2", [P, L])
    t1 = sb("t1", [P, 2, L]); t2 = sb("t2", [P, 2, L]); QK = sb("QK", [P, 2, L]); R1 = sb("R1", [P, 2, L])
    SPL = sb("SPL", [P, 3, 2, L], BF16)
    QS = [sb(f"QS{i}", [64, HEADS, L], BF16) for i in range(2)]
    KS = [sb(f"KS{i}", [64, HEADS, L], BF16) for i in range(2)]
    V = [sb(f"V{i}", [P, J1, HEADS, DH + 1]) for i in range(2)]; VN = sb("VN", [P, 2, J1, HEADS, DH])
    PT = sb("PT", [P, 2, 1536])
    OSB = sb("OSB", [P, GROUPS, L]); rec = sb("rec", [P, HEADS]); YN = sb("YN", [P, J1, HEADS, DH]); yT = sb("yT", [P, L])
    NM = sb("NM", [P, J1, HEADS]); NR = sb("NR", [P, J1, HEADS]); NMS = sb("NMS", [P, J1, P // HEADS, HEADS], BF16)
    NMT = sb("NMT", [3 * HEADS, L], BF16)
    mx = sb("mx", [P, J1, 8]); ix = sb("ix", [P, J1, 8], mybir.dt.uint32); ef = sb("ef", [P, J1, 2])
    MK = sb("MK", [P, J1, 2, P], BF16); cs = sb("cs", [P, 2, P]); loc = sb("loc", [P, J1, 2])
    zeros = sb("zeros", [P, 2 * NTOK * D // (P * NSEQ)])
    SS = [ctx.enter_context(nc.psum_tensor(f"SS{i}", [P, 1536], F32)) for i in range(2)]
    FR = ctx.enter_context(nc.psum_tensor("FR", [P, 512], F32))
    OT = ctx.enter_context(nc.psum_tensor("OT", [P, 2, L], F32))
    FRb = FR[:].bitcast(BF16)

    fr_x = signal("fr_x", 1); fr_vg = signal("fr_vg", 1); fr_qk = signal("fr_qk", 1); fr_rot = signal("fr_rot", 1)
    fr_route = signal("fr_route", 2); fr_nm = signal("fr_nm", 1); fr_o = signal("fr_o", 2); fr_y = signal("fr_y", 1)
    fr_wc = signal("fr_wc", 1); p1 = signal("p1", GROUPS); p2 = signal("p2", GROUPS); pv = signal("pv", GROUPS)
    xT_done = signal("xT_done", 1); v_done = signal("v_done", 1); part_done = signal("part_done", 2)
    nm_copied = signal("nm_copied", 1); exp_done = signal("exp_done", GROUPS); ot_copied = signal("ot_copied", 2)
    yT_done = signal("yT_done", 1)
    top = signal("top", 4); rope = signal("rope", 2); route = signal("route", 13); max_done = signal("max_done", 8)
    nm_step = signal("nm_step", 4); epi = signal("epi", 4); x_upd = signal("x_upd", 1)
    xn_ready = signal("xn_ready1", 2); rest = signal("rest1", 3); v_placed = signal("v_placed", 1)
    xn_stored = signal("xn_stored", 16); parts_out = signal("parts_out", 16); parts_in = [signal(f"parts_in{i}", 16 * 12) for i in range(2)]
    nm_out = signal("nm_out", 16); nm_in = signal("nm_in", 16)
    loaded = sem("loaded1"); stat_step = sem("stat_step1"); root_done = sem("root_done1"); we_loaded = sem("we_loaded")
    wT = sem("wT"); wTc = sem("wTc"); wE = sem("wE"); cleared = sem("cleared"); yzero = sem("yzero")
    poolset = sem("poolset"); paced = sem("paced"); pool_paced = sem("pool_paced")

    down = {n: dram[f"L1_attn_W{n}_down"] for n in "qkv"}
    WD = sb("WD", [P, 3, HEADS * LAT]); BD = sb("BD", [P, 3, 2, 2, DH])
    WDT = PT[:, 0, 0:8 * P]

    block = ctx.enter_context(nc.Block())
    loads = [(WD[:, n, :], down[k]) for n, k in enumerate("qkv")]
    for hh in range(2):
        rows = slice(LAT * hh, LAT * hh + LAT)
        for n, k in enumerate("qk"):
            c_, e_ = dram[f"L1_attn_W{k}_up_c"], dram[f"L1_attn_W{k}_up_e"]
            loads += [(BD[rows, n, 0, hh, 0:4], c_), (BD[rows, n, 0, hh, 4:8], e_)]
            pair = e_.rearrange("l (i two) -> l i two", two=2)
            dst = BD[rows, n, 1, hh, 4:8].rearrange("p (i two) -> p i two", two=2)
            loads += [(dst[:, :, 0:1], pair[:, :, 1:2]), (dst[:, :, 1:2], pair[:, :, 0:1])]
        loads += [(BD[rows, 2, 0, hh, :], dram["L1_attn_Wv_up"])]
    loads += [(wvg[:, P:], dram["L1_ffn_wg"]), (wc[:], dram["L1_attn_Wc"]), (cos[:], dram["c_cos"]), (sin[:], dram["c_sin"]),
              (maskq[:].rearrange("p a b -> p (a b)"), dram["c_maskq"]), (maskk[:].rearrange("p a b -> p (a b)"), dram["c_maskk"]),
              (tri[:], dram["c_tri"]), (iota[:], dram["c_iota"])]
    LOADED = 16 * len(loads)

    parts_d, nm_d, xn_d, y_d = scratch["parts"], scratch["nm"], scratch["xn"], scratch["y"]

    def schedule(eng, norm=None, front=None, split=None, pass1=None, maxima=None, pass2=None, values=None, epilogue=None):
        def do(piece, *args):
            if piece is not None:
                piece(*args)

        def step(c, par, normed=True, fronted=True, passed1=True, passed2=True, closed=True):
            other = 1 - par
            for g in range(GROUPS):
                if passed1:
                    do(pass1, g, c + 1, other)
                if g == 0:
                    if fronted:
                        do(front, 0, c + 2, par)
                    if closed:
                        do(values, GROUPS - 1, c - 1, other)
                    if fronted:
                        do(front, 1, c + 2, par)
                if g == 1 and fronted:
                    do(front, 3, c + 2, par)
                if g == 2 and closed:
                    do(epilogue, 2, c - 1, other)
                if g == 3 and fronted:
                    do(front, 5, c + 2, par)
                if passed2:
                    do(pass2, g, c, par)
                if g == 0 and fronted:
                    do(front, 2, c + 2, par)
                if g == 1 and fronted:
                    do(split, 0, c + 2, par)
                if g == 1 and closed:
                    do(epilogue, 0, c - 1, other)
                if g == 2:
                    if closed:
                        do(epilogue, 3, c - 1, other)
                    if normed:
                        do(norm, c + 3, other)
                if g == 3 and passed1:
                    do(maxima, c + 1, other)
                if passed2 and g:
                    do(values, g - 1, c, par)
                if g == 1:
                    if closed:
                        do(epilogue, 1, c - 1, other)
                    if fronted:
                        do(split, 1, c + 2, par)
                if g == 2 and fronted:
                    do(front, 4, c + 2, par)

        do(norm, 0, 0)
        step(-2, 0, passed1=False, passed2=False, closed=False)
        step(-1, 1, passed2=False, closed=False)
        step(0, 0, closed=False)
        with eng.Fori(0, NSEQ // 2 - 2) as i:
            for k in range(2):
                step(i * 2 + (1 + k), 1 - k)
        step(NSEQ - 3, 1, normed=False)
        step(NSEQ - 2, 0, normed=False, fronted=False)
        step(NSEQ - 1, 1, normed=False, fronted=False, passed1=False)
        step(NSEQ, 0, normed=False, fronted=False, passed1=False, passed2=False)

    @block.sync
    def _(sp):
        sp.wait_ge(cleared, 1)
        for dst, src in loads:
            sp.dma_start(dst, src, allow_slow_non_contiguous=True).then_inc(loaded, 16)
        sp.wait_ge(poolset, 2)
        sp.wait_ge(stat_step, 1)
        sp.sem_inc(xn_stored.sem, 32)
        sp.sem_inc(parts_out.sem, 32)
        for half in range(2):
            sp.sem_inc(parts_in[half].sem, 2 * 16 * 12)
        sp.sem_inc(nm_out.sem, 32)
        sp.sem_inc(nm_in.sem, 32)

        def norm(c, par):
            sp.wait_ge(xn_ready.sem, xn_ready.at(c, 2))
            sp.dma_start(xn_d.rearrange("(i p) d -> p i d", p=P)[:, bass.ds(c * J1, J1), :], XN[:, par]).then_inc(xn_stored.sem, 16)
            sp.dma_start(WE[:, bass.ds(c * (E1 // NSEQ), E1 // NSEQ), :],
                         dram["L1_ffn_we"].rearrange("e d f -> d e f")[:, bass.ds(c * (E1 // NSEQ), E1 // NSEQ), :]).then_inc(we_loaded, 16)
            sp.dma_start(y_d.rearrange("(p c r) d -> p c (r d)", p=P, c=NSEQ)[:, bass.ds(c, 1), :],
                         zeros[:].unsqueeze(1)).then_inc(yzero, 16)

        def load(half, c, par):
            sp.wait_ge(p2.sem, p2.at(c - 2, 2 * half + 2))
            heads = slice(half * HEADS // 2, (half + 1) * HEADS // 2)
            src = parts_d[par].rearrange("(h d) (r q t) -> d r q h t", d=DH, r=3, q=2)
            for n, term in enumerate(TERMS):
                for q, dst in enumerate((QS, KS)):
                    sp.dma_start(dst[par][DH * n:DH * n + DH, heads, :], src[:, term[q], q, heads, :]).then_inc(parts_in[half].sem, 16)

        def split(k, c, par):
            if k == 1:
                sp.wait_ge(rest.sem, rest.at(c, 3))
                for half in range(2):
                    sp.wait_ge(parts_in[half].sem, parts_in[half].at(c - 2, 16 * 12))
                sp.dma_start(parts_d[par], SPL[:].rearrange("p r q t -> p (r q t)")).then_inc(parts_out.sem, 16)

        def front(k, c, par):
            if k == 4:
                sp.wait_ge(parts_out.sem, parts_out.at(c, 16))
                load(0, c, par)

        def maxima(c, par):
            sp.wait_ge(nm_copied.sem, nm_copied.at(c, 1))
            sp.wait_ge(nm_in.sem, nm_in.at(c - 1, 16))
            sp.dma_start(nm_d[par], NMT[:]).then_inc(nm_out.sem, 16)
            sp.wait_ge(nm_out.sem, nm_out.at(c, 16))
            sp.dma_start(QS[par][KQ:KQ + 3, :, :], nm_d[par].rearrange("(r h) t -> r h t", r=3)).then_inc(nm_in.sem, 16)

        def pass1(g, c, par):
            if g == 0:
                load(1, c, par)

        schedule(sp, norm=norm, front=front, split=split, pass1=pass1, maxima=maxima)
        sp.wait_ge(xn_stored.sem, xn_stored.at(NSEQ - 1, 16))
        sp.wait_ge(nm_in.sem, nm_in.at(NSEQ - 1, 16))
        sp.wait_ge(we_loaded, 16 * NSEQ)
        sp.wait_ge(yzero, 16 * NSEQ)

    @block.tensor
    def _(pe):
        for s in (fr_x, fr_vg, fr_qk, fr_rot, fr_route, fr_nm, fr_o, fr_y, fr_wc, p1, p2, pv):
            pe.sem_inc(s.sem, 2 * s.per)
        pe.wait_ge(loaded, LOADED)
        for n in range(3):
            if n:
                pe.wait_ge(wTc, 2 * n)
            for b in range(8):
                last = nc.tensor.transpose(SS[0][:, b * P:(b + 1) * P], WD[:, n, b * P:(b + 1) * P], ident[:])
            last.then_inc(wT, 1)
            pe.wait_ge(wTc, 2 * n + 1)
            for b in range(8):
                last = nc.tensor.matmul(SS[1][:, b * 32:b * 32 + 32], WDT[:, b * P:(b + 1) * P],
                                        BD[:, n, :, :, :].rearrange("p r h d -> p (r h d)"), start=True, stop=True)
            last.then_inc(wE, 1)
        pe.wait_ge(wTc, 6)
        pe.wait_ge(poolset, 2)
        pe.wait_ge(stat_step, 1)

        def front(k, c, par):
            if k == 0:
                pe.wait_ge(nm_copied.sem, nm_copied.at(c - 2, 1))
                pe.wait_ge(route.sem, route.at(c - 1, 10))
                pe.wait_ge(xn_ready.sem, xn_ready.at(c, 2))
                for j in range(J1):
                    last = nc.tensor.transpose(FR[:, j * P:(j + 1) * P], XN[:, par, j, :], ident[:])
                last.then_inc(fr_x.sem, 1)
            elif k == 1:
                pe.wait_ge(xT_done.sem, xT_done.at(c, 1))
                for j in range(J1):
                    last = nc.tensor.matmul(FR[:, 2 * j * P:2 * (j + 1) * P], xnT[:, j * P:(j + 1) * P], wvg[:], start=True, stop=True)
                last.then_inc(fr_vg.sem, 1)
            elif k == 2:
                pe.wait_ge(v_done.sem, v_done.at(c, 1))
                pe.wait_ge(top.sem, top.at(c, 4))
                for q, w in enumerate((wq, wk)):
                    last = nc.tensor.matmul(FR[:, q * L:(q + 1) * L], w[:], xnT[:], start=True, stop=True)
                last.then_inc(fr_qk.sem, 1)
            elif k == 3:
                pe.wait_ge(rope.sem, rope.at(c, 1))
                for q, w in enumerate((wqr, wkr)):
                    last = nc.tensor.matmul(FR[:, q * L:(q + 1) * L], w[:], xnT[:], start=True, stop=True)
                last.then_inc(fr_rot.sem, 1)
            else:
                j = k - 4
                if j == 0:
                    pe.wait_ge(rope.sem, rope.at(c, 2))
                    pe.wait_ge(x_upd.sem, x_upd.at(c - 3, 1))
                    pe.wait_ge(route.sem, route.at(c, 4))
                else:
                    pe.wait_ge(route.sem, route.at(c, 6))
                rhs = MK[:, j, :, :].rearrange("p c e -> p (c e)")
                nc.tensor.matmul(FR[:, 0:2 * P], tri[:], rhs, start=True, stop=True)
                nc.tensor.matmul(FR[:, 2 * P:4 * P], ones[:], rhs, start=True, stop=True).then_inc(fr_route.sem, 1)

        def pass1(g, c, par):
            S_ = SS[1]
            if g % 2 == 0:
                pe.wait_ge(parts_in[g // 2].sem, parts_in[g // 2].at(c, 16 * 12))
            pe.wait_ge(max_done.sem, max_done.at(c, 2 * g))
            nc.tensor.matmul(S_[:, 0:512], identb[:], maskq[:].rearrange("p a b -> p (a b)"), start=True, stop=False)
            for j in range(HG):
                h = HG * g + j
                nc.tensor.matmul(S_[:, j * P:(j + 1) * P], QS[par][0:KQ, h, 0:P], KS[par][0:KQ, h, 0:P], start=False, stop=(j == HG - 1))
            for b in range(2):
                bank = S_[:, 512 * (b + 1):512 * (b + 2)]
                for j in range(2):
                    h = HG * g + 2 * b + j
                    nc.tensor.matmul(bank[:, j * L:(j + 1) * L], QS[par][0:KQ, h, P:L], KS[par][0:KQ, h, :], start=(j == 0), stop=False)
                last = nc.tensor.matmul(bank.rearrange("p (j k) -> p j k", j=2)[:, :, P:L], identb[:], maskq[:, 0:2, :], start=False, stop=True)
            last.then_inc(p1.sem, 1)

        def maxima(c, par):
            pe.wait_ge(nm_step.sem, nm_step.at(c, 4))
            if isinstance(c, int) and c == NSEQ - 1:
                pe.wait_ge(x_upd.sem, x_upd.at(c - 2, 1))
            else:
                pe.wait_ge(route.sem, route.at(c + 1, 10))
            for j in range(J1):
                last = nc.tensor.transpose(FRb[:, j * P:(j + 1) * P], NMS[:, j, :, :].rearrange("p r h -> p (r h)"), identb[:])
            last.then_inc(fr_nm.sem, 1)

        def values(g, c, par):
            pe.wait_ge(exp_done.sem, exp_done.at(c, g + 1))
            if g == 0:
                pe.wait_ge(v_placed.sem, v_placed.at(c, 1))
                pe.wait_ge(ot_copied.sem, ot_copied.at(c - 1, 2))
            if g == 2:
                pe.wait_ge(ot_copied.sem, ot_copied.at(c, 1))
            for j in range(HG):
                h, rows = HG * g + j, slice(32 * j, 32 * j + DH + 1)
                nc.tensor.matmul(OT[rows, g % 2, :], V[par][:, 0, h, :], PT[:, g % 2, j * L:(j + 1) * L],
                                 start=True, stop=False, tile_position=(0, 32 * j))
                last = nc.tensor.matmul(OT[rows, g % 2, P:L], V[par][:, 1, h, :], PT[:, g % 2, 1024 + j * P:1024 + (j + 1) * P],
                                        start=False, stop=True, tile_position=(0, 32 * j))
            last.then_inc(pv.sem, 1)

        def pass2(g, c, par):
            S_ = SS[0]
            if g == 0:
                pe.wait_ge(nm_in.sem, nm_in.at(c, 16))
            pe.wait_ge(exp_done.sem, exp_done.at(c, g))
            for b in range(2):
                bank = S_[:, 512 * b:512 * (b + 1)]
                for j in range(2):
                    h = HG * g + 2 * b + j
                    nc.tensor.matmul(bank[:, j * L:(j + 1) * L], KS[par][0:KQ + 3, h, 0:P], QS[par][0:KQ + 3, h, :], start=(j == 0), stop=False)
                nc.tensor.matmul(bank.rearrange("p (j q) -> p j q", j=2)[:, :, 0:P], identb[:], maskk[:, 0:2, :], start=False, stop=True)
            nc.tensor.matmul(S_[:, 1024:1536], identb[:], maskk[:].rearrange("p a b -> p (a b)"), start=True, stop=False)
            for j in range(HG):
                h = HG * g + j
                last = nc.tensor.matmul(S_[:, 1024 + j * P:1024 + (j + 1) * P], KS[par][0:KQ + 3, h, P:L], QS[par][0:KQ + 3, h, P:L],
                                        start=False, stop=(j == HG - 1))
            last.then_inc(p2.sem, 1)

        def epilogue(k, c, par):
            if k < J1:
                if k == 0:
                    pe.wait_ge(ot_copied.sem, ot_copied.at(c, 2))
                    if not isinstance(c, int) or c < NSEQ - 3:
                        pe.wait_ge(rope.sem, rope.at(c + 3, 2))
                    elif c < NSEQ - 1:
                        pe.wait_ge(nm_copied.sem, nm_copied.at(c + 1, 1))
                    else:
                        pe.wait_ge(x_upd.sem, x_upd.at(c - 1, 1))
                else:
                    pe.wait_ge(epi.sem, epi.at(c, 2))
                for g in range(GROUPS):
                    last = nc.tensor.transpose(FR[:, g * P:(g + 1) * P], OSB[:, g, k * P:(k + 1) * P], ident[:])
                last.then_inc(fr_o.sem, 1)
            elif k == J1:
                pe.wait_ge(epi.sem, epi.at(c, 4))
                for j in range(J1):
                    last = nc.tensor.transpose(FR[:, j * P:(j + 1) * P], YN[:, j, :, :].rearrange("p h d -> p (h d)"), ident[:])
                last.then_inc(fr_y.sem, 1)
            else:
                pe.wait_ge(yT_done.sem, yT_done.at(c, 1))
                for j in range(J1):
                    last = nc.tensor.matmul(FR[:, j * P:(j + 1) * P], yT[:, j * P:(j + 1) * P], wc[:], start=True, stop=True)
                last.then_inc(fr_wc.sem, 1)

        schedule(pe, front=front, pass1=pass1, maxima=maxima, pass2=pass2, values=values, epilogue=epilogue)

    @block.scalar
    def _(act):
        for s in (xT_done, v_done, part_done, nm_copied, exp_done, ot_copied, yT_done):
            act.sem_inc(s.sem, 2 * s.per)
        for n in range(3):
            act.wait_ge(wT, n + 1)
            nc.scalar.copy(WDT, SS[0][:, 0:1024]).then_inc(wTc, 1)
            act.wait_ge(wE, n + 1)
            e = SS[1][:, 0:256].rearrange("p (b r d) -> p b r d", r=2, d=2 * DH)
            if n == 2:
                nc.scalar.copy(wvg[:, 0:P].rearrange("p (b d) -> p b d", b=8), e[:, :, 0, :]).then_inc(wTc, 1)
            else:
                nc.scalar.copy((wq, wk)[n][:].rearrange("p (b d) -> p b d", b=8), e[:, :, 0, :])
                nc.scalar.copy((wqr, wkr)[n][:].rearrange("p (b d) -> p b d", b=8), e[:, :, 1, :]).then_inc(wTc, 1)
        act.wait_ge(poolset, 2)
        act.wait_ge(stat_step, 7)
        nc.scalar.activation(stats[:, :, 0], q1[:], ACT.Sqrt).then_inc(root_done, 1)

        def front(k, c, par):
            if k == 0:
                act.wait_ge(fr_x.sem, fr_x.at(c, 1))
                act.wait_ge(fr_rot.sem, fr_rot.at(c - 1, 1))
                nc.scalar.copy(xnT[:], FR[:, 0:L]).then_inc(xT_done.sem, 1)
            elif k == 1:
                act.wait_ge(fr_vg.sem, fr_vg.at(c, 1))
                act.wait_ge(v_placed.sem, v_placed.at(c - 2, 1))
                vg = FR[:].rearrange("p (j v h d) -> p j v h d", j=J1, v=2, d=DH)
                nc.scalar.copy(VN[:, par], vg[:, :, 0, :, :]).then_inc(v_done.sem, 1)

        def split(k, c, par):
            act.wait_ge(rest.sem, rest.at(c, 1 + k))
            if k == 0:
                act.wait_ge(parts_out.sem, parts_out.at(c - 1, 16))
            nc.scalar.copy(SPL[:, k], (QK if k == 0 else R1)[:]).then_inc(part_done.sem, 1)

        def maxima(c, par):
            act.wait_ge(fr_nm.sem, fr_nm.at(c, 1))
            act.wait_ge(nm_out.sem, nm_out.at(c - 1, 16))
            nc.scalar.copy(NMT[:], FRb[0:3 * HEADS, 0:L]).then_inc(nm_copied.sem, 1)

        def pass2(g, c, par):
            act.wait_ge(p2.sem, p2.at(c, g + 1))
            act.wait_ge(pv.sem, pv.at(c, g - 1))
            nc.scalar.activation(PT[:, g % 2, :], SS[0][:], ACT.Exp, scale=SCALE).then_inc(exp_done.sem, 1)

        def values(g, c, par):
            if g % 2 == 1:
                k = g // 2
                act.wait_ge(pv.sem, pv.at(c, 2 * k + 2))
                act.wait_ge(fr_o.sem, fr_o.at(c - 1, 2))
                nc.scalar.copy(OSB[:, 2 * k:2 * k + 2, :], OT[:]).then_inc(ot_copied.sem, 1)

        def epilogue(k, c, par):
            if k == 2:
                act.wait_ge(fr_y.sem, fr_y.at(c, 1))
                act.wait_ge(fr_wc.sem, fr_wc.at(c - 1, 1))
                nc.scalar.copy(yT[:], FR[:, 0:L]).then_inc(yT_done.sem, 1)

        schedule(act, front=front, split=split, maxima=maxima, pass2=pass2, values=values, epilogue=epilogue)

    @block.gpsimd
    def _(pool):
        pool.sem_inc(xn_ready.sem, 2 * xn_ready.per)
        pool.sem_inc(rest.sem, 2 * rest.per)
        pool.sem_inc(v_placed.sem, 2)
        nc.gpsimd.memset(BD[:], 0.0).then_inc(cleared, 1)
        nc.gpsimd.memset(zeros[:], 0.0)
        nc.gpsimd.memset(ones[:], 1.0)
        nc.gpsimd.memset(carry[:], 0.0)
        for i in range(2):
            nc.gpsimd.memset(V[i][:], 1.0).then_inc(poolset, 1)
        pool.wait_ge(stat_step, 12)

        def norm(c, par):
            def wide(v):
                return v[:, bass.ds(c * J1, J1)].unsqueeze(2).to_broadcast([P, J1, D])

            pool.wait_ge(fr_x.sem, fr_x.at(c - 2, 1))
            pool.wait_ge(xn_stored.sem, xn_stored.at(c - 2, 16))
            nc.gpsimd.tensor_tensor(XM[:], X[:, bass.ds(c * J1, J1), :], wide(mean), ALU.subtract).then_inc(xn_ready.sem, 1)
            pool.wait_ge(xn_ready.sem, xn_ready.at(c, 1))
            nc.gpsimd.tensor_tensor(XN[:, par], XM[:], wide(rstd), ALU.mult).then_inc(xn_ready.sem, 1)

        def split(k, c, par):
            if k == 0:
                pool.wait_ge(rope.sem, rope.at(c, 2))
                nc.gpsimd.tensor_tensor(QK[:], t1[:], t2[:], ALU.add).then_inc(rest.sem, 1)
                pool.wait_ge(part_done.sem, part_done.at(c, 1))
                nc.gpsimd.tensor_tensor(R1[:], QK[:], SPL[:, 0], ALU.subtract).then_inc(rest.sem, 1)
            else:
                pool.wait_ge(part_done.sem, part_done.at(c, 2))
                nc.gpsimd.tensor_tensor(SPL[:, 2], R1[:], SPL[:, 1], ALU.subtract).then_inc(rest.sem, 1)

        def pass2(g, c, par):
            if g == 0:
                pool.wait_ge(v_done.sem, v_done.at(c, 1))
                pool.wait_ge(pv.sem, pv.at(c - 2, GROUPS))
                pool.sem_inc(pool_paced, 1)
                nc.gpsimd.tensor_copy(V[par][:, :, :, 0:DH], VN[:, par]).then_inc(v_placed.sem, 1)

        schedule(pool, norm=norm, split=split, pass2=pass2)

    @block.vector
    def _(dve):
        for s in (top, rope, route, max_done, nm_step, epi, x_upd):
            dve.sem_inc(s.sem, 2 * s.per)
        nc.vector.memset(OT[:], 0.0)
        nc.vector.memset(NMS[:], 0.0)
        for i in range(2):
            nc.vector.memset(KS[i][32:64], 1.0)
        token_stats(nc, dve, X, stats, mean, rstd, q1, q2, stat_step, root_done)
        dve.wait_ge(poolset, 2)

        def step(ins, c, k):
            ins.then_inc(route.sem, 1)
            dve.wait_ge(route.sem, route.at(c, k))

        def front(k, c, par):
            fr = FR[:].rearrange("p (q t) -> p q t", q=2)
            tiles = bass.ds(c * J1, J1)
            wide = lambda v: v[:].unsqueeze(1).to_broadcast([P, 2, L])
            if k == 1:
                dve.wait_ge(fr_vg.sem, fr_vg.at(c, 1))
                dve.wait_ge(v_done.sem, v_done.at(c, 1))
                dve.wait_ge(route.sem, route.at(c - 1, 13))
                dve.sem_inc(paced, 1)
                for j in range(J1):
                    nc.vector.max(mx[:, j, :], FR[:, (2 * j + 1) * P:(2 * j + 2) * P]).then_inc(top.sem, 1)
                dve.wait_ge(top.sem, top.at(c, J1))
                dve.sem_inc(paced, 1)
                for j in range(J1):
                    nc.vector.max_index(ix[:, j, :], mx[:, j, :], FR[:, (2 * j + 1) * P:(2 * j + 2) * P]).then_inc(top.sem, 1)
            elif k == 2:
                dve.wait_ge(fr_qk.sem, fr_qk.at(c, 1))
                dve.wait_ge(rest.sem, rest.at(c - 1, 1))
                nc.vector.tensor_tensor(t1[:], fr, wide(cos), ALU.mult).then_inc(rope.sem, 1)
            elif k == 3:
                dve.wait_ge(fr_rot.sem, fr_rot.at(c, 1))
                nc.vector.tensor_tensor(t2[:], fr, wide(sin), ALU.mult).then_inc(rope.sem, 1)
                dve.wait_ge(top.sem, top.at(c, 2 * J1))
                step(nc.vector.tensor_copy(ef[:], ix[:, :, 0:2]), c, 1)
                step(nc.vector.tensor_copy(EF[:, tiles, :], ef[:]), c, 2)
                step(nc.vector.tensor_copy(EU[:, tiles, :], ix[:, :, 0:2]), c, 3)
                nc.vector.tensor_tensor(MK[:], iota[:].unsqueeze(1).unsqueeze(1).to_broadcast([P, J1, 2, P]),
                                        ef[:].unsqueeze(3).to_broadcast([P, J1, 2, P]), ALU.is_equal).then_inc(route.sem, 1)
            elif k >= 4:
                j = k - 4
                dve.wait_ge(fr_route.sem, fr_route.at(c, j + 1))
                fv = FR[:].rearrange("p (s e) -> p s e", e=P)
                n = 4 + 4 * j
                step(nc.vector.tensor_tensor(cs[:], fv[:, 0:2, :], carry[:], ALU.add), c, n + 1)
                step(nc.vector.tensor_tensor(carry[:], fv[:, 2:4, :], carry[:], ALU.add), c, n + 2)
                step(nc.vector.tensor_tensor(cs[:], cs[:], MK[:, j, :, :], ALU.mult), c, n + 3)
                step(nc.vector.tensor_reduce(loc[:, j, :], cs[:], AX.X, ALU.add), c, n + 4)
                if j == J1 - 1:
                    nc.vector.tensor_copy(LG[:, tiles, :], mx[:, :, 0:2])
                    nc.vector.tensor_copy(LOC[:, tiles, :], loc[:]).then_inc(route.sem, 1)

        def pass1(g, c, par):
            dve.wait_ge(p1.sem, p1.at(c, g + 1))
            if g == 0:
                dve.wait_ge(nm_step.sem, nm_step.at(c - 1, 4))
            nc.vector.tensor_reduce(NM[:, 0, HG * g:HG * g + HG], SS[1][:, 0:512].rearrange("p (h k) -> p h k", h=HG),
                                    AX.X, ALU.max, negate=True).then_inc(max_done.sem, 1)
            nc.vector.tensor_reduce(NM[:, 1, HG * g:HG * g + HG], SS[1][:, 512:1536].rearrange("p (h k) -> p h k", h=HG),
                                    AX.X, ALU.max, negate=True).then_inc(max_done.sem, 1)
            if g == GROUPS - 1:
                dve.wait_ge(max_done.sem, max_done.at(c, 8))
                dve.wait_ge(fr_nm.sem, fr_nm.at(c - 1, 1))
                nc.vector.tensor_copy(NMS[:, :, 0, :], NM[:]).then_inc(nm_step.sem, 1)
                dve.wait_ge(nm_step.sem, nm_step.at(c, 1))
                nc.vector.tensor_tensor(NR[:], NM[:], NMS[:, :, 0, :], ALU.subtract).then_inc(nm_step.sem, 1)
                dve.wait_ge(nm_step.sem, nm_step.at(c, 2))
                nc.vector.tensor_copy(NMS[:, :, 1, :], NR[:]).then_inc(nm_step.sem, 1)
                dve.wait_ge(nm_step.sem, nm_step.at(c, 3))
                nc.vector.tensor_tensor(NMS[:, :, 2, :], NR[:], NMS[:, :, 1, :], ALU.subtract).then_inc(nm_step.sem, 1)

        def epilogue(k, c, par):
            if k < J1:
                dve.wait_ge(fr_o.sem, fr_o.at(c, k + 1))
                if k == 0:
                    dve.wait_ge(fr_y.sem, fr_y.at(c - 1, 1))
                else:
                    dve.wait_ge(epi.sem, epi.at(c, 2))
                o = FR[:].rearrange("p (h w) -> p h w", w=32)
                nc.vector.reciprocal(rec[:], o[:, :, DH]).then_inc(epi.sem, 1)
                dve.wait_ge(epi.sem, epi.at(c, 2 * k + 1))
                nc.vector.tensor_tensor(YN[:, k, :, :], o[:, :, 0:DH], rec[:].unsqueeze(2).to_broadcast([P, HEADS, DH]),
                                        ALU.mult).then_inc(epi.sem, 1)
            elif k == J1 + 1:
                dve.wait_ge(fr_wc.sem, fr_wc.at(c, 1))
                xs = X[:, bass.ds(c * J1, J1), :]
                nc.vector.tensor_tensor(xs, FR[:, 0:L].rearrange("p (j d) -> p j d", j=J1), xs, ALU.add).then_inc(x_upd.sem, 1)

        schedule(dve, front=front, pass1=pass1, epilogue=epilogue)


def experts1(nc, ctx, t, dram, scratch, out):
    def sb(name, shape, dt=F32):
        return ctx.enter_context(nc.sbuf_tensor(name, shape, dt))

    def sem(name):
        return ctx.enter_context(nc.semaphore(name))

    X, ident, WE, carry, iota = t["X"], t["ident"], t["WE"], t["carry"], t["iota"]
    EF, EU, LG, LOC = t["EF"], t["EU"], t["LG"], t["LOC"]
    xn_d, y_d = scratch["xn"], scratch["y"]
    U32 = mybir.dt.uint32
    NG = NSLOT // P
    NV = 5
    FAR = float(1 << 20)
    off = sb("off", [P, NT]); junk = sb("junk", [P, 2, P])
    W = sb("W", [P, NT, 2]); wd = sb("wd", [P, NT]); wr = sb("wr", [P, NT, 2])
    VAL = sb("VAL", [P, NT, 2, NV], BF16)
    lo_u = sb("lo_u", [P, NT, 2], U32); hi_u = sb("hi_u", [P, NT, 2], U32)
    lo_e = sb("lo_e", [P, NT, 2]); hi_e = sb("hi_e", [P, NT, 2]); ok = sb("ok", [P, NT, 2])
    A = sb("A1", [P, 2, 2, 2, P], BF16); G = sb("G1", [P, 2, 4, NG], BF16); R = sb("R1c", [P, 2, 4, NV, NG], BF16)
    mhi = sb("mhi", [P, NG]); mlo = sb("mlo", [P, NG]); mw = sb("mw", [P, NG]); m1 = sb("m1", [P, NG]); m2 = sb("m2", [P, NG])
    gi = sb("gi", [P, NG], U32); si = sb("si", [P, NG], U32)
    XG = sb("XG", [P, NG, D]); XGT = sb("XGT", [P, 2, 4, P]); YB = sb("YB", [P, 2, 4, D])
    YC = sb("YC", [P, 2, 2, 8, D])
    MAP = ctx.enter_context(nc.psum_tensor("MAP", [P, 512], F32))
    TR = [ctx.enter_context(nc.psum_tensor(f"TR{i}", [P, 512], F32)) for i in range(2)]
    EO = [ctx.enter_context(nc.psum_tensor(f"EO{i}", [P, 512], F32)) for i in range(2)]

    val_loaded = sem("val_loaded"); offs = sem("offs"); bulk = sem("bulk"); gexp = sem("gexp1"); onehot = sem("onehot")
    told = sem("told"); mapped = sem("mapped"); decoded = sem("decoded"); gathered = [sem(f"gathered{i}") for i in range(8)]
    blank = sem("blank"); transposed = sem("transposed"); tr_copied = sem("tr_copied"); applied = sem("applied"); weighted = sem("weighted")
    scattered = [sem(f"scattered{i}") for i in range(2)]; y_loaded = [sem(f"y_loaded{i}") for i in range(2)]; half_added = sem("half_added"); added = sem("added")
    stored = sem("stored")

    block = ctx.enter_context(nc.Block())

    @block.sync
    def _(sp):
        sp.dma_start(VAL[:, :, :, 0:2], dram["c_rowval"].rearrange("p (i c v) -> p i c v", c=2, v=2), allow_slow_non_contiguous=True).then_inc(val_loaded, 16)
        yv, ov = y_d.rearrange("(c i p) d -> p c i d", c=2, p=P), out.rearrange("(i p) d -> p i d", p=P)
        for i in range(2):
            sp.wait_ge(scattered[i], 16 * NG // 2)
        for g in range(8):
            if g >= 2:
                sp.wait_ge(added, g - 1)
            for c in range(2):
                sp.dma_start(YC[:, g % 2, c, :, :], yv[:, c, 8 * g:8 * g + 8, :]).then_inc(y_loaded[g % 2], 16)
            if g:
                sp.wait_ge(added, g)
                sp.dma_start(ov[:, 8 * g - 8:8 * g, :], X[:, 8 * g - 8:8 * g, :]).then_inc(stored, 16)
        sp.wait_ge(added, 8)
        sp.dma_start(ov[:, 56:64, :], X[:, 56:64, :]).then_inc(stored, 16)
        sp.wait_ge(stored, 16 * 8)

    @block.tensor
    def _(pe):
        for i in range(NT // 2):
            pe.wait_ge(told, i + 1)
            for k in range(4):
                last = nc.tensor.matmul(MAP[:, 0:NV * NG], A[:, i % 2, k // 2, k % 2, :], R[:, i % 2, k, :, :].rearrange("p v g -> p (v g)"),
                                        start=(i == 0 and k == 0), stop=(i == NT // 2 - 1 and k == 3))
            last.then_inc(mapped, 1)
        for b in range(8):
            pe.wait_ge(gathered[b], 64)
            if b >= 2:
                pe.wait_ge(tr_copied, b - 1)
            for k in range(4):
                last = nc.tensor.transpose(TR[b % 2][:, k * P:(k + 1) * P], XG[:, 4 * b + k, :], ident[:])
            last.then_inc(transposed, 1)
            pe.wait_ge(tr_copied, b + 1)
            if b >= 2:
                pe.wait_ge(weighted, b - 1)
            for k in range(4):
                for j in range(4):
                    e = 4 * (4 * b + k) + j
                    last = nc.tensor.matmul(EO[b % 2][32 * j:32 * j + 32, k * P:(k + 1) * P], XGT[:, b % 2, k, 32 * j:32 * j + 32], WE[:, e, :],
                                            start=True, stop=True, tile_position=(0, 32 * j))
            last.then_inc(applied, 1)

    @block.scalar
    def _(act):
        act.wait_ge(bulk, 1)
        nc.scalar.activation(wd[:], wd[:], ACT.Exp).then_inc(gexp, 1)
        for b in range(8):
            act.wait_ge(transposed, b + 1)
            if b >= 2:
                act.wait_ge(applied, b - 1)
            nc.scalar.copy(XGT[:, b % 2].rearrange("p k q -> p (k q)"), TR[b % 2][:]).then_inc(tr_copied, 1)

    @block.gpsimd
    def _(pool):
        nc.gpsimd.memset(XG[:], 0.0).then_inc(blank, 1)
        for i in range(NT // 2):
            pool.wait_ge(onehot, 2 * i + 2)
            if i >= 2:
                pool.wait_ge(mapped, i - 1)
            val = VAL[:, 2 * i:2 * i + 2, :, :].rearrange("p i c v -> p (i c) v")
            nc.gpsimd.tensor_tensor(R[:, i % 2], G[:, i % 2].unsqueeze(2).to_broadcast([P, 4, NV, NG]),
                                    val.unsqueeze(3).to_broadcast([P, 4, NV, NG]), ALU.mult).then_inc(told, 1)
        pool.wait_ge(decoded, 11)
        pool.wait_ge(blank, 1)
        for b in range(8):
            for k in range(4):
                g = 4 * b + k
                nc.gpsimd.indirect_dma_start(out=XG[:, g, :], out_offset=None, in_=xn_d, in_offset=bass.IndirectOffsetOnAxis(ap=gi[:, g:g + 1], axis=0),
                                             bounds_check=NTOK - 1, oob_is_err=False).then_inc(gathered[b], 16)
        for b in range(8):
            pool.wait_ge(weighted, b + 1)
            for k in range(4):
                g = 4 * b + k
                nc.gpsimd.indirect_dma_start(out=y_d, out_offset=bass.IndirectOffsetOnAxis(ap=si[:, g:g + 1], axis=0), in_=YB[:, b % 2, k, :], in_offset=None,
                                             bounds_check=2 * NTOK - 1, oob_is_err=False).then_inc(scattered[b % 2], 16)

    @block.vector
    def _(dve):
        nc.vector.tensor_tensor(wd[:], LG[:, :, 1], LG[:, :, 0], ALU.subtract).then_inc(bulk, 1)
        for i in range(NT):
            if i >= 2:
                dve.wait_ge(offs, i - 1)
            nc.vector.scalar_tensor_tensor(junk[:, i % 2, :], iota[:], EF[:, i, 1:2], carry[:, 0, :], ALU.is_equal, ALU.mult,
                                           accum_out=off[:, i:i + 1]).then_inc(offs, 1)
        n = [1]

        def step(ins):
            ins.then_inc(bulk, 1)
            n[0] += 1
            dve.wait_ge(bulk, n[0])

        dve.wait_ge(gexp, 1)
        dve.wait_ge(offs, NT)
        step(nc.vector.tensor_scalar(W[:, :, 0], wd[:], 1.0, None, ALU.add))
        step(nc.vector.reciprocal(W[:, :, 0], W[:, :, 0]))
        step(nc.vector.tensor_tensor(W[:, :, 1], wd[:], W[:, :, 0], ALU.mult))
        dve.wait_ge(val_loaded, 16)
        for r in range(3):
            step(nc.vector.tensor_copy(VAL[:, :, :, 2 + r], W[:]))
            if r < 2:
                step(nc.vector.tensor_tensor(W[:], W[:], VAL[:, :, :, 2 + r], ALU.subtract))
        step(nc.vector.tensor_tensor(LOC[:, :, 1], LOC[:, :, 1], off[:], ALU.add))
        step(nc.vector.tensor_scalar(ok[:], LOC[:], float(CAP) + 0.5, None, ALU.is_lt))
        step(nc.vector.tensor_single_scalar(lo_u[:], EU[:], 3, ALU.bitwise_and))
        step(nc.vector.tensor_single_scalar(hi_u[:], EU[:], 2, ALU.logical_shift_right))
        step(nc.vector.tensor_copy(lo_e[:], lo_u[:]))
        step(nc.vector.tensor_copy(hi_e[:], hi_u[:]))
        step(nc.vector.scalar_tensor_tensor(lo_e[:], lo_e[:], float(CAP), LOC[:], ALU.mult, ALU.add))
        step(nc.vector.tensor_tensor(lo_e[:], lo_e[:], ok[:], ALU.mult))
        step(nc.vector.tensor_scalar(lo_e[:], lo_e[:], -1.0, None, ALU.add))
        for i in range(NT // 2):
            if i >= 2:
                dve.wait_ge(mapped, i - 1)
                dve.wait_ge(told, i - 1)
            def wide(v, m):
                return v[:, 2 * i:2 * i + 2, :].rearrange("p i c -> p (i c)").unsqueeze(2).to_broadcast([P, 4, m])
            nc.vector.tensor_tensor(A[:, i % 2].rearrange("p i c q -> p (i c) q"), iota[:].unsqueeze(1).to_broadcast([P, 4, P]), wide(lo_e, P),
                                    ALU.is_equal).then_inc(onehot, 1)
            nc.vector.tensor_tensor(G[:, i % 2], iota[:, 0:NG].unsqueeze(1).to_broadcast([P, 4, NG]), wide(hi_e, NG), ALU.is_equal).then_inc(onehot, 1)
        dve.wait_ge(mapped, NT // 2)
        m = [0]

        def dstep(ins):
            ins.then_inc(decoded, 1)
            m[0] += 1
            dve.wait_ge(decoded, m[0])

        mv = MAP[:, 0:NV * NG].rearrange("p (v g) -> p v g", v=NV)
        dstep(nc.vector.tensor_scalar(mhi[:], mv[:, 0, :], -1.0, float(P), ALU.add, ALU.mult))
        dstep(nc.vector.tensor_tensor(mlo[:], mhi[:], mv[:, 1, :], ALU.add))
        dstep(nc.vector.tensor_scalar(m1[:], mv[:, 0, :], 0.5, FAR, ALU.is_lt, ALU.mult))
        dstep(nc.vector.tensor_tensor(mlo[:], mlo[:], m1[:], ALU.add))
        dstep(nc.vector.tensor_copy(si[:], mlo[:]))
        dstep(nc.vector.tensor_scalar(m2[:], mv[:, 0, :], NT + 0.5, -float(NTOK), ALU.is_gt, ALU.mult))
        dstep(nc.vector.tensor_tensor(mlo[:], mlo[:], m2[:], ALU.add))
        dstep(nc.vector.tensor_copy(gi[:], mlo[:]))
        dstep(nc.vector.tensor_copy(mw[:], mv[:, 2, :]))
        dstep(nc.vector.tensor_tensor(mw[:], mw[:], mv[:, 3, :], ALU.add))
        dstep(nc.vector.tensor_tensor(mw[:], mw[:], mv[:, 4, :], ALU.add))
        for b in range(8):
            dve.wait_ge(applied, b + 1)
            if b >= 2:
                dve.wait_ge(scattered[b % 2], 64 * (b // 2))
            nc.vector.tensor_tensor(YB[:, b % 2], EO[b % 2][:].rearrange("p (k d) -> p k d", k=4),
                                    mw[:, 4 * b:4 * b + 4].unsqueeze(2).to_broadcast([P, 4, D]), ALU.mult).then_inc(weighted, 1)
        for g in range(8):
            dve.wait_ge(y_loaded[g % 2], 32 * (g // 2 + 1))
            xs = X[:, 8 * g:8 * g + 8, :]
            nc.vector.tensor_tensor(xs, xs, YC[:, g % 2, 0], ALU.add).then_inc(half_added, 1)
            dve.wait_ge(half_added, g + 1)
            nc.vector.tensor_tensor(xs, xs, YC[:, g % 2, 1], ALU.add).then_inc(added, 1)


def constants():
    bf16 = np.dtype("bfloat16")
    c = {}
    c["c_ident"] = np.eye(P, dtype=np.float32)
    c["c_identb"] = np.eye(P).astype(bf16)
    sel = np.zeros((3 * S, S, P), np.float32)
    for r in range(3):
        for n in range(S):
            sel[S * r + n, n, :] = 1
    c["c_sel"] = sel.reshape(3 * S, -1).astype(bf16)
    c["c_tri8"] = np.tile(np.tril(np.ones((E0, E0), np.float32)).reshape(1, -1), (P, 1))
    split = np.zeros((P, 2), np.float32)
    split[S:3 * S, 0] = -1
    split[2 * S:3 * S, 1] = -1
    c["c_split"] = split
    dim = DH // 2
    inv = (1.0 / np.float32(10000.0) ** (np.arange(0, dim, 2, dtype=np.float32) / np.float32(dim))).astype(np.float32)
    freqs = np.arange(L, dtype=np.float32)[:, None] * inv[None, :]
    emb = np.concatenate((freqs, freqs), axis=-1)
    cos, sin = np.ones((HEADS, DH, L), np.float32), np.zeros((HEADS, DH, L), np.float32)
    cos[:, dim:, :] = np.cos(emb).T
    sin[:, dim:, :] = (np.sin(emb) * np.array([-1, 1] * (dim // 2), np.float32)).T
    c["c_cos"], c["c_sin"] = cos.reshape(P, L), sin.reshape(P, L)
    q = np.where(np.arange(P)[None, :] <= np.arange(P)[:, None], 0, -1e30).astype(np.float32)
    c["c_maskq"], c["c_maskk"] = np.tile(q, (1, HG)).astype(bf16), np.tile(q.T, (1, HG)).astype(bf16)
    c["c_tri"] = np.triu(np.ones((P, P), np.float32)).astype(bf16)
    c["c_iota"] = np.tile(np.arange(P, dtype=np.float32), (P, 1))
    row = np.zeros((P, NT, 2, 2), np.float32)
    row[:, :, :, 0] = np.arange(NT)[None, :, None] + NT * np.arange(2)[None, None, :] + 1
    row[:, :, :, 1] = np.arange(P)[:, None, None]
    c["c_rowval"] = row.reshape(P, -1).astype(bf16)
    return c


def build(nc, dram, out):
    def scr(name, shape, dt):
        return nc.dram_tensor(name, shape, dt, kind="Internal").ap()

    scratch = {
        "xn": scr("s_xn", [NTOK, D], F32), "y": scr("s_y", [2 * NTOK, D], F32),
        "parts": [scr(f"s_parts{i}", [P, 3 * 2 * L], BF16) for i in range(2)],
        "b": [scr(f"s_b{i}", [S, T0], F32) for i in range(2)],
        "nm": [scr(f"s_nm{i}", [3 * HEADS, L], BF16) for i in range(2)],
    }
    with ExitStack() as ctx:
        def sb(name, shape, dt=F32):
            return ctx.enter_context(nc.sbuf_tensor(name, shape, dt))

        U32 = mybir.dt.uint32
        t = {"X": sb("X", [P, NT, D]), "ident": sb("ident", [P, P]), "identb": sb("identb", [P, P], BF16)}
        with ExitStack() as c0:
            layer0(nc, c0, t, dram, scratch["b"])
        t.update(WE=sb("WE", [P, E1, D]), carry=sb("carry", [P, 2, P]), EF=sb("EF", [P, NT, 2]), EU=sb("EU", [P, NT, 2], U32),
                 LG=sb("LG", [P, NT, 2]), LOC=sb("LOC", [P, NT, 2]), iota=sb("iota", [P, P]))
        with ExitStack() as c1:
            layer1(nc, c1, t, dram, scratch)
        with ExitStack() as c2:
            experts1(nc, c2, t, dram, scratch, out)


_INS = ['L0_attn_x', 'L0_attn_rms_w', 'L0_attn_in_proj', 'L0_attn_conv_w', 'L0_attn_conv_b', 'L0_attn_x_proj', 'L0_attn_dt_w',
        'L0_attn_dt_b', 'L0_attn_A_log', 'L0_attn_D', 'L0_attn_out_proj', 'L0_ffn_Wr', 'L0_ffn_br', 'L0_ffn_W1', 'L0_ffn_b1',
        'L0_ffn_W2', 'L0_ffn_b2', 'L1_attn_Wq_down', 'L1_attn_Wk_down', 'L1_attn_Wv_down', 'L1_attn_Wq_up_c', 'L1_attn_Wq_up_e',
        'L1_attn_Wk_up_c', 'L1_attn_Wk_up_e', 'L1_attn_Wv_up', 'L1_attn_Wc', 'L1_ffn_wg', 'L1_ffn_we']


def kernel(**inputs):
    import concourse.bacc as bacc
    from concourse.bass_utils import run_bass_kernel_spmd

    nc = bacc.Bacc("TRN2", target_bir_lowering=False, num_devices=1)
    given = {name: np.ascontiguousarray(inputs[name]) for name in _INS}
    given.update(constants())
    arrays, dram = {}, {}
    for name, a in given.items():
        arrays[f"in_{name}"] = a
        dram[name] = nc.dram_tensor(f"in_{name}", a.shape, mybir.dt.from_np(a.dtype), kind="ExternalInput").ap()
    out = nc.dram_tensor("out_0", (NTOK, D), F32, kind="ExternalOutput").ap()
    build(nc, dram, out)
    r = run_bass_kernel_spmd(nc, [arrays], core_ids=[0])
    return r.results[0]["out_0"].reshape(NTOK // L, L, D)
```

```python
from contextlib import ExitStack

import numpy as np

import concourse.bass as bass
from concourse import mybir

F32 = mybir.dt.float32
BF16 = mybir.dt.bfloat16
ALU = mybir.AluOpType
ACT = mybir.ActivationFunctionType
AX = mybir.AxisListType

P = 128
NTOK = 32 * 256
NT = NTOK // P
D = 128
L = 256
EPS = 1e-5

T0 = 512
J0 = T0 // P
IT0 = NTOK // T0
HALF = 2
S = 16
RANK = 8
E0 = 8
FB = 4
TOP_P = 0.8
B_AT, DT_AT = 64, 96


class Signal:

    def __init__(self, sem, per):
        self.sem, self.per = sem, per

    def at(self, c, k):
        return c * self.per + (2 * self.per + k)


def layer0(nc, ctx, t, dram, b_d):
    def sb(name, shape, dt=F32):
        return ctx.enter_context(nc.sbuf_tensor(name, shape, dt))

    def signal(name, per):
        return Signal(ctx.enter_context(nc.semaphore(name)), per)

    def sem(name):
        return ctx.enter_context(nc.semaphore(name))

    XC, XT = 6, (NT - J0) // 6
    X, stats = t["X"], t["stats"]
    ident, identb, wvg = t["ident"], t["identb"], t["wvg"]
    inproj = sb("inproj", [P, 4 * P]); rmsw = sb("rmsw", [P, 1])
    convw = sb("convw", [P, HALF, 4]); convb = sb("convb", [P, HALF])
    xproj = sb("xproj", [P, HALF, 104]); dtw = sb("dtw", [P, HALF * P]); dtb = sb("dtb", [P, HALF])
    A = sb("A", [P, HALF, S]); Dp = sb("Dp", [P, HALF]); outproj = sb("outproj", [P, HALF, D])
    Wr = sb("Wr", [P, E0]); br = sb("br", [P, E0]); W1 = sb("W1", [P, E0, FB * P]); b1 = sb("b1", [P, E0, FB])
    W2 = sb("W2", [P, E0, FB, D]); b2 = sb("b2", [J0 * E0, J0, D])
    sel = sb("sel", [3 * S, S, P], BF16); tri8 = sb("tri8", [P, E0 * E0]); split = sb("split", [P, 2])
    mean = sb("mean", [P, NT]); rstd = sb("rstd", [P, NT]); rrms = sb("rrms", [P, NT])
    q1 = sb("q1", [P, NT]); q2 = sb("q2", [P, NT])
    XN = sb("XN", [P, J0, D]); XR = sb("XR", [P, J0, D]); xrT = sb("xrT", [P, T0])
    xch = sb("xch", [P, HALF, T0]); xi = sb("xi", [P, HALF, T0]); th = sb("th", [P, HALF, T0]); tz = sb("tz", [P, HALF, T0])
    hi = sb("hi", [3 * S, T0], BF16); rest = sb("rest", [3 * S, T0]); mid = sb("mid", [3 * S, T0], BF16)
    dtB = sb("dtB", [P, T0])
    soft = sb("soft", [P, HALF, T0])
    umax, lnw, one_w = xch, th, tz
    lg = sb("lg", [P, J0, E0]); pe_ = sb("pe_", [P, J0, E0]); pr = sb("pr", [P, J0, E0]); g4 = sb("g4", [P, 3, J0])
    gt = sb("gt", [P, J0, E0, E0]); eq = sb("eq", [P, J0, E0, E0]); cnt = sb("cnt", [P, J0, E0]); cum = sb("cum", [P, J0, E0])
    xnT = sb("xnT", [P, 2, T0]); zs = sb("zs", [P, 2, HALF, T0]); CC = sb("CC", [3 * S, 2, T0], BF16)
    delta = sb("delta", [P, 2, HALF, T0]); dx = sb("dx", [P, 2, HALF, T0])
    y = sb("y", [P, 2, HALF, T0]); FF = sb("FF", [P, 2, J0, D])
    gate = sb("gate", [P, 2, J0, E0]); gT = sb("gT", [J0 * E0, 2, P])
    Bs = sb("Bs", [P, 2, 2, T0]); dBx = sb("dBx", [P, 2, HALF, T0]); H = sb("H", [P, 2, HALF, T0])
    hT = sb("hT", [P, 2, FB, T0])
    dA = ctx.enter_context(nc.psum_tensor("dA", [P, HALF, T0], F32))
    UP = [ctx.enter_context(nc.psum_tensor(f"UP{i}", [P, 512], F32)) for i in range(2)]
    DN = ctx.enter_context(nc.psum_tensor("DN", [P, 512], F32))
    Cp = [ctx.enter_context(nc.psum_tensor(f"Cp{i}", [P, 512], F32)) for i in range(2)]
    FRO = ctx.enter_context(nc.psum_tensor("FRO", [P, 512], F32))

    front = signal("front", 11)
    upf = signal("upf", E0 * FB); downf = signal("downf", E0)
    cready = signal("cready", S); outf = signal("outf", 1)
    xT_copied = signal("xT_copied", 2); tanh_z = signal("tanh_z", 2); tanh_x = signal("tanh_x", 1); tap_done = signal("tap_done", 2); u_done = signal("u_done", 2)
    gexp = signal("gexp", 1); gT_copied = signal("gT_copied", 1); dt_copied = signal("dt_copied", 1)
    hi_done = signal("hi_done", 1); mid_done = signal("mid_done", 1); sp_done = signal("sp_done", 3)
    relu_done = signal("relu_done", E0 * FB); da_ready = signal("da_ready", 2 * S)
    conv_step = signal("conv_step", 6); gate_step = signal("gate_step", 12); z_done = signal("z_done", 2)
    xi_done = signal("xi_done", 1); rest_done = signal("rest_done", 1); cc_done = signal("cc_done", 1)
    log_step = signal("log_step", 2); delta_done = signal("delta_done", 1)
    scan_done = signal("scan_done", S); prod_done = signal("prod_done", S)
    add_done = signal("add_done", S); acc_done = signal("acc_done", E0); yz_done = signal("yz_done", 1)
    x_done = signal("x_done", 1); restat = signal("restat", 1)
    xn_ready = signal("xn_ready", 4); dbx_ready = signal("dbx_ready", S); y_init = signal("y_init", 1)
    dx_done = signal("dx_done", 1); rank_step = signal("rank_step", 3); r_done = signal("r_done", 1)
    b_stored = signal("b_stored", 16); b_loaded = [signal(f"b_loaded{i}", 16 * S // 4) for i in range(2)]
    wloaded = sem("wloaded"); dloaded = sem("dloaded"); wT = sem("wT"); wTc = sem("wTc"); wE = sem("wE"); blanked = sem("blanked"); stat_step2 = sem("stat_step2")
    root_done2 = sem("root_done2"); loaded = sem("loaded"); xloaded = [sem(f"xloaded{i}") for i in range(XC + 1)]; zeroed = sem("zeroed"); stat_step = sem("stat_step")
    root_done = sem("root_done"); prep = sem("prep"); aexp = sem("aexp"); paced = sem("paced0"); sp_paced = sem("sp_paced")

    block = ctx.enter_context(nc.Block())

    loads = [
        (rmsw[:], dram["L0_attn_rms_w"].rearrange("(p a) -> p a", a=1)),
        (inproj[:], dram["L0_attn_in_proj"]),
        (ident[:], dram["c_ident"]), (identb[:], dram["c_identb"]), (sel[:].rearrange("p a b -> p (a b)"), dram["c_sel"]),
        (tri8[:], dram["c_tri8"]), (split[:], dram["c_split"]),
        (convw[:], dram["L0_attn_conv_w"].rearrange("(h p) k -> p h k", p=P)),
        (convb[:], dram["L0_attn_conv_b"].rearrange("(h p) -> p h", p=P)),
        (dtb[:], dram["L0_attn_dt_b"].rearrange("(h p) -> p h", p=P)),
        (dtw[DT_AT:DT_AT + RANK, :], dram["L0_attn_dt_w"]),
        (A[:], dram["L0_attn_A_log"].rearrange("(h p) s -> p h s", p=P)),
        (Dp[:], dram["L0_attn_D"].rearrange("(h p) -> p h", p=P)),
        (outproj[:], dram["L0_attn_out_proj"].rearrange("(h p) n -> p h n", p=P)),
        (Wr[:], dram["L0_ffn_Wr"]),
        (br[:], dram["L0_ffn_br"].rearrange("(a e) -> a e", a=1).to_broadcast([P, E0])),
    ]
    xp = dram["L0_attn_x_proj"].rearrange("(h p) n -> p h n", p=P)
    for r in range(3):
        loads.append((xproj[:, :, S * r:S * r + S], xp[:, :, RANK + S:RANK + 2 * S]))
    loads.append((xproj[:, :, B_AT:B_AT + S], xp[:, :, RANK:RANK + S]))
    loads.append((xproj[:, :, DT_AT:DT_AT + RANK], xp[:, :, 0:RANK]))
    wloads = [
        (b1[:], dram["L0_ffn_b1"].rearrange("e (b p) -> p e b", p=P)),
        (W1[:], dram["L0_ffn_W1"].rearrange("e p f -> p e f")),
        (W2[:].rearrange("p e b n -> p (e b) n"), dram["L0_ffn_W2"].rearrange("e (b p) n -> p (e b) n", p=P)),
    ]
    flat = hT[:].rearrange("p a b c -> p (a b c)")
    WD, WDT = flat[:, 0:3 * HEADS * LAT].rearrange("p (n c) -> p n c", n=3), flat[:, 3 * HEADS * LAT:4 * HEADS * LAT]
    BD = H[:].rearrange("p a b c -> p (a b c)")[:, 0:3 * 4 * DH].rearrange("p (n r h d) -> p n r h d", n=3, r=2, h=2)
    dloads = [(WD[:, n, :], dram[f"L1_attn_W{k}_down"]) for n, k in enumerate("qkv")]
    for hh in range(2):
        rows = slice(LAT * hh, LAT * hh + LAT)
        for n, k in enumerate("qk"):
            c_, e_ = dram[f"L1_attn_W{k}_up_c"], dram[f"L1_attn_W{k}_up_e"]
            dloads += [(BD[rows, n, 0, hh, 0:4], c_), (BD[rows, n, 0, hh, 4:8], e_)]
            pair = e_.rearrange("l (i two) -> l i two", two=2)
            dst = BD[rows, n, 1, hh, 4:8].rearrange("p (i two) -> p i two", two=2)
            dloads += [(dst[:, :, 0:1], pair[:, :, 1:2]), (dst[:, :, 1:2], pair[:, :, 0:1])]
        dloads += [(BD[rows, 2, 0, hh, :], dram["L1_attn_Wv_up"])]

    FIRST, OTHERS = slice(0, J0), slice(J0, NT)
    STATS_END = 2 * XC
    PROJ0 = 8

    def pipeline(fore, start, slot, end, eng, between=lambda s: None, finish=None):
        def stage_and_slot(s, it, par, first=False):
            if finish is None:
                slot(s, it, par, first=first)
                fore(s, it + 1, 1 - par)
            else:
                fore(s, it + 1, 1 - par)
                slot(s, it, par, first=first)
                finish(s, it, False)

        for s in range(S):
            fore(s, 0, 0)
            between(s)
        start()
        for s in range(S):
            stage_and_slot(s, 0, 0, first=True)
        with eng.Fori(0, IT0 // 2 - 1) as i:
            for k in range(2):
                it, par = i * 2 + (1 + k), 1 - k
                for s in range(S):
                    stage_and_slot(s, it, par)
        for s in range(S):
            slot(s, IT0 - 1, 1, final=True)
            if finish is not None:
                finish(s, IT0 - 1, True)
        end(IT0 - 1, 1)

    @block.sync
    def _(sp):
        xd = dram["L0_attn_x"].rearrange("b (j p) d -> p (b j) d", p=P)
        sp.dma_start(X[:, 0:J0, :], xd[:, 0:J0, :]).then_inc(xloaded[0], 16)
        sp.wait_ge(zeroed, 1)
        for dst, src in loads:
            sp.dma_start(dst, src, allow_slow_non_contiguous=True).then_inc(loaded, 16)
        for g in range(XC):
            tiles = slice(J0 + g * XT, J0 + (g + 1) * XT)
            sp.dma_start(X[:, tiles, :], xd[:, tiles, :]).then_inc(xloaded[g + 1], 16)
        for dst, src in wloads:
            sp.dma_start(dst, src, allow_slow_non_contiguous=True).then_inc(wloaded, 16)
        for dst, src in dloads:
            sp.dma_start(dst, src, allow_slow_non_contiguous=True).then_inc(dloaded, 16)
        for j in range(J0):
            sp.dma_start(b2[E0 * j:E0 * j + E0, j, :], dram["L0_ffn_b2"]).then_inc(wloaded, 16)
        for s in (b_stored, *b_loaded):
            sp.sem_inc(s.sem, 2 * s.per)

        def load_b(k, it, par):
            src = b_d[par if k < S // 2 else 1 - par]
            if k == S // 2:
                sp.wait_ge(b_stored.sem, b_stored.at(it + 1, 16))
                sp.sem_inc(sp_paced, 1)
            sp.wait_ge(dbx_ready.sem, dbx_ready.at(it, 2 * k - 2))
            pair = 2 * k % S
            sp.dma_start(Bs[:, k % 2], src[pair:pair + 2, :].unsqueeze(0).to_broadcast([P, 2, T0])).then_inc(b_loaded[k % 2].sem, 16)

        def slot(s, it, par, first=False, final=False):
            if s % 2 == 1 and not (final and s + 3 >= S):
                load_b((s + 3) // 2, it, par)

        def fore(s, n, q):
            if s == 9:
                sp.wait_ge(dt_copied.sem, dt_copied.at(n, 1))
                sp.dma_start(b_d[q], dtB[B_AT:B_AT + S, :]).then_inc(b_stored.sem, 16)

        def start():
            load_b(S // 2, -1, 1)
            load_b(S // 2 + 1, -1, 1)

        pipeline(fore, start, slot, lambda it, par: None, sp)

    LOADED = 16 * len(loads)

    @block.tensor
    def _(pe):
        for s in (front, upf, downf, cready, outf):
            pe.sem_inc(s.sem, 2 * s.per)
        pe.wait_ge(loaded, LOADED)
        pe.wait_ge(prep, 1)

        def project(n, part):
            if part == 0:
                pe.wait_ge(dloaded, 16 * len(dloads))
                if n:
                    pe.wait_ge(wTc, 2 * n)
                for b in range(8):
                    last = nc.tensor.transpose(dA[:].rearrange("p h t -> p (h t)")[:, b * P:(b + 1) * P], WD[:, n, b * P:(b + 1) * P], ident[:])
                last.then_inc(wT, 1)
            else:
                pe.wait_ge(wTc, 2 * n + 1)
                for b in range(8):
                    last = nc.tensor.matmul(Cp[0][:, b * 32:b * 32 + 32], WDT[:, b * P:(b + 1) * P],
                                            BD[:, n, :, :, :].rearrange("p r h d -> p (r h d)"), start=True, stop=True)
                last.then_inc(wE, 1)

        def up(e, it, par, blocks):
            q = par if e < E0 else 1 - par
            if e == E0 and blocks[0] == 0:
                pe.wait_ge(xT_copied.sem, xT_copied.at(it + 1, 1))
            for f in blocks:
                k = e * FB + f
                pe.wait_ge(relu_done.sem, relu_done.at(it, k - 1))
                nc.tensor.matmul(UP[k % 2][:], W1[:, e % E0, f * P:(f + 1) * P], xnT[:, q, :], start=True, stop=True).then_inc(upf.sem, 1)

        def down(e, it, tiles):
            if tiles[0] == 0:
                pe.wait_ge(relu_done.sem, relu_done.at(it, (e + 1) * FB))
                pe.wait_ge(acc_done.sem, acc_done.at(it, e))
            for j in tiles:
                for f in range(FB):
                    last = nc.tensor.matmul(DN[:, j * P:(j + 1) * P], hT[:, e % 2, f, j * P:(j + 1) * P], W2[:, e, f, :],
                                            start=(f == 0), stop=(f == FB - 1))
            if tiles[-1] == J0 - 1:
                last.then_inc(downf.sem, 1)

        def output(it, par, tiles, last_one=False):
            if tiles[0] == 0:
                if not last_one:
                    pe.wait_ge(gT_copied.sem, gT_copied.at(it + 1, 1))
                pe.wait_ge(yz_done.sem, yz_done.at(it, 1))
            for j in tiles:
                nc.tensor.matmul(FRO[:, j * P:(j + 1) * P], gT[:, par, :], b2[:, j, :], start=True, stop=False)
                for h in range(HALF):
                    last = nc.tensor.matmul(FRO[:, j * P:(j + 1) * P], y[:, par, h, j * P:(j + 1) * P], outproj[:, h, :],
                                            start=False, stop=(h == 1))
            if tiles[-1] == J0 - 1:
                last.then_inc(outf.sem, 1)

        def make_c(s, it, par):
            q = par if s < S else 1 - par
            if s == S:
                pe.wait_ge(cc_done.sem, cc_done.at(it + 1, 1))
            pe.wait_ge(prod_done.sem, prod_done.at(it, s - 1))
            nc.tensor.matmul(Cp[s % 2][:], sel[:, s % S, :], CC[:, q, :], start=True, stop=True).then_inc(cready.sem, 1)

        def start():
            pe.wait_ge(wloaded, 16 * (len(wloads) + J0))
            up(E0, -1, 1, range(FB))
            make_c(S, -1, 1)

        def slot(s, it, par, first=False, final=False):
            more_up = not (final and s == S - 2)
            if s % 2 == 1:
                down(s // 2, it, range(0, 2))
            elif more_up:
                up(s // 2 + 1, it, par, range(0, 1))
            if not (final and s + 1 >= S):
                make_c(s + 1, it, par)
            if s % 2 == 1:
                down(s // 2, it, range(2, J0))
            elif more_up:
                up(s // 2 + 1, it, par, range(1, FB))
            if s < 2 and not first:
                output(it - 1, 1 - par, range(2 * s, 2 * s + 2))

        def fore(s, n, q):
            if s == 2:
                pe.wait_ge(xn_ready.sem, xn_ready.at(n, 2))
                pe.wait_ge(gT_copied.sem, gT_copied.at(n - 1, 1))
                pe.wait_ge(x_done.sem, x_done.at(n - 2, 1))
                for j in range(J0):
                    last = nc.tensor.transpose(FRO[:, j * P:(j + 1) * P], XN[:, j, :], ident[:])
                last.then_inc(front.sem, 1)
            elif s == 3:
                pe.wait_ge(xn_ready.sem, xn_ready.at(n, 3))
                pe.wait_ge(xT_copied.sem, xT_copied.at(n, 1))
                for j in range(J0):
                    last = nc.tensor.transpose(FRO[:, j * P:(j + 1) * P], XR[:, j, :], ident[:])
                last.then_inc(front.sem, 1)
            elif 4 <= s < 8:
                k = s - 4
                b = (0, 2, 1, 3)[k]
                if k == 0:
                    pe.wait_ge(xT_copied.sem, xT_copied.at(n, 2))
                elif k == 2:
                    pe.wait_ge(z_done.sem, z_done.at(n, 1))
                else:
                    pe.wait_ge(conv_step.sem, conv_step.at(n, 3 * (b - 1)))
                nc.tensor.matmul(FRO[:], inproj[:, b * P:(b + 1) * P], xrT[:], start=True, stop=True).then_inc(front.sem, 1)
            elif s == 8:
                pe.wait_ge(z_done.sem, z_done.at(n, 2))
                for j in range(J0):
                    last = nc.tensor.matmul(FRO[:, j * E0:(j + 1) * E0], xnT[:, q, j * P:(j + 1) * P], Wr[:], start=True, stop=True)
                last.then_inc(front.sem, 1)
            elif s == 9:
                pe.wait_ge(xi_done.sem, xi_done.at(n, 1))
                pe.wait_ge(gate_step.sem, gate_step.at(n, 1))
                for h in range(HALF):
                    last = nc.tensor.matmul(FRO[0:DT_AT + RANK, :], xproj[:, h, :], xi[:, h, :], start=(h == 0), stop=(h == 1))
                last.then_inc(front.sem, 1)
            elif s == 10 or s == 11:
                h = s - 10
                if h == 0:
                    pe.wait_ge(dt_copied.sem, dt_copied.at(n, 1))
                    pe.wait_ge(rest_done.sem, rest_done.at(n, 1))
                else:
                    pe.wait_ge(u_done.sem, u_done.at(n, 1))
                nc.tensor.matmul(FRO[:], dtw[DT_AT:DT_AT + RANK, h * P:(h + 1) * P], dtB[DT_AT:DT_AT + RANK, :], start=True, stop=True).then_inc(front.sem, 1)
            elif s == 13:
                pe.wait_ge(gate_step.sem, gate_step.at(n, 12))
                pe.wait_ge(u_done.sem, u_done.at(n, 2))
                nc.tensor.transpose(FRO[0:J0 * E0, 0:P], gate[:, q].rearrange("p j e -> p (j e)"), ident[:]).then_inc(front.sem, 1)

        def between(s):
            if PROJ0 <= s < PROJ0 + 6:
                project((s - PROJ0) // 2, (s - PROJ0) % 2)

        pipeline(fore, start, slot, lambda it, par: output(it, par, range(J0), last_one=True), pe, between)

    @block.scalar
    def _(act):
        for s in (xT_copied, tanh_z, tanh_x, gexp, gT_copied, dt_copied, hi_done, mid_done, sp_done, relu_done, da_ready, tap_done, u_done):
            act.sem_inc(s.sem, 2 * s.per)

        def roots(tiles, stat_step, root_done):
            act.wait_ge(stat_step, 7)
            nc.scalar.activation(stats[:, tiles, 0], q1[:, tiles], ACT.Sqrt).then_inc(root_done, 1)
            act.wait_ge(stat_step, 15)
            nc.scalar.activation(stats[:, tiles, 0], q2[:, tiles], ACT.Sqrt).then_inc(root_done, 1)

        roots(FIRST, stat_step, root_done)
        act.wait_ge(loaded, LOADED)
        nc.scalar.activation(A[:], A[:], ACT.Exp).then_inc(aexp, 1)
        act.wait_ge(prep, 1)

        def project(n, part):
            if part == 0:
                act.wait_ge(wT, n + 1)
                nc.scalar.copy(WDT, dA[:].rearrange("p h t -> p (h t)")).then_inc(wTc, 1)
                return
            act.wait_ge(wE, n + 1)
            e = Cp[0][:, 0:256].rearrange("p (b r d) -> p b r d", r=2, d=2 * DH)
            if n == 2:
                nc.scalar.copy(wvg[:, 0:P].rearrange("p (b d) -> p b d", b=8), e[:, :, 0, :]).then_inc(wTc, 1)
            else:
                nc.scalar.copy(t["wq" if n == 0 else "wk"][:].rearrange("p (b d) -> p b d", b=8), e[:, :, 0, :])
                nc.scalar.copy(t["wqr" if n == 0 else "wkr"][:].rearrange("p (b d) -> p b d", b=8), e[:, :, 1, :]).then_inc(wTc, 1)

        def between(s):
            if PROJ0 <= s < PROJ0 + 6:
                project((s - PROJ0) // 2, (s - PROJ0) % 2)
            if s == STATS_END:
                roots(OTHERS, stat_step2, root_done2)

        def make_da(s, it, par):
            q = par if s < S else 1 - par
            if s == S:
                act.wait_ge(delta_done.sem, delta_done.at(it + 1, 1))
            act.wait_ge(scan_done.sem, scan_done.at(it, s))
            for h in range(HALF):
                nc.scalar.activation(dA[:, h, :].rearrange("p (b l) -> p b l", l=L)[:, :, 1:L],
                                     delta[:, q, h, :].rearrange("p (b l) -> p b l", l=L)[:, :, 1:L],
                                     ACT.Exp, scale=A[:, h, s % S:s % S + 1]).then_inc(da_ready.sem, 1)

        def relus(e, it, blocks):
            for f in blocks:
                k = e * FB + f
                act.wait_ge(upf.sem, upf.at(it, k + 1))
                if f == 0:
                    act.wait_ge(downf.sem, downf.at(it, e - 1))
                nc.scalar.activation(hT[:, e % 2, f, :], UP[k % 2][:], ACT.Relu, bias=b1[:, e % E0, f:f + 1]).then_inc(relu_done.sem, 1)

        def start():
            relus(E0, -1, range(FB))
            act.wait_ge(blanked, 1)
            make_da(S, -1, 1)

        def slot(s, it, par, first=False, final=False):
            if s % 2 == 0 and not (final and s == S - 2):
                relus(s // 2 + 1, it, range(0, 2))
            if not (final and s + 1 >= S):
                make_da(s + 1, it, par)

        def finish(s, it, final):
            if s % 2 == 0 and not (final and s == S - 2):
                relus(s // 2 + 1, it, range(2, FB))

        def delta_input(h, n):
            if h == 0:
                act.wait_ge(xi_done.sem, xi_done.at(n, 1))
            act.wait_ge(front.sem, front.at(n, 9 + h))
            nc.scalar.activation(umax[:, h, :], FRO[:], ACT.Relu, bias=dtb[:, h:h + 1])
            nc.scalar.activation(soft[:, h, :], FRO[:], ACT.Abs, bias=dtb[:, h:h + 1]).then_inc(u_done.sem, 1)

        def fore(s, n, q):
            if s == 3:
                act.wait_ge(upf.sem, upf.at(n - 2, E0 * FB))
                act.wait_ge(front.sem, front.at(n, 1))
                nc.scalar.copy(xnT[:, q, :], FRO[:]).then_inc(xT_copied.sem, 1)
            elif s == 4:
                act.wait_ge(front.sem, front.at(n, 2))
                nc.scalar.copy(xrT[:], FRO[:]).then_inc(xT_copied.sem, 1)
            elif s == 5 or s == 7:
                b = (s - 5) // 2
                if b == 0:
                    act.wait_ge(delta_done.sem, delta_done.at(n - 1, 1))
                act.wait_ge(front.sem, front.at(n, 3 + 2 * b))
                nc.scalar.activation(xch[:, b, :], FRO[:], ACT.Identity, scale=convw[:, b, 3:4], bias=convb[:, b:b + 1]).then_inc(tap_done.sem, 1)
            elif s == 6 or s == 8:
                b = (s - 6) // 2
                act.wait_ge(front.sem, front.at(n, 4 + 2 * b))
                nc.scalar.activation(tz[:, b, :], FRO[:], ACT.Tanh, scale=0.5).then_inc(tanh_z.sem, 1)
                if b == 1:
                    act.wait_ge(conv_step.sem, conv_step.at(n, 6))
                    nc.scalar.activation(th[:], xch[:], ACT.Tanh).then_inc(tanh_x.sem, 1)
            elif s == 10:
                act.wait_ge(gate_step.sem, gate_step.at(n, 3))
                nc.scalar.activation(pe_[:], lg[:], ACT.Exp).then_inc(gexp.sem, 1)
                act.wait_ge(front.sem, front.at(n, 8))
                act.wait_ge(b_stored.sem, b_stored.at(n - 1, 16))
                nc.scalar.copy(dtB[B_AT:DT_AT + RANK, :], FRO[B_AT:DT_AT + RANK, :]).then_inc(dt_copied.sem, 1)
                nc.scalar.copy(hi[:], FRO[0:3 * S, :]).then_inc(hi_done.sem, 1)
            elif s == 11:
                act.wait_ge(rest_done.sem, rest_done.at(n, 1))
                act.wait_ge(cc_done.sem, cc_done.at(n - 1, 1))
                nc.scalar.copy(mid[:], rest[:]).then_inc(mid_done.sem, 1)
                delta_input(0, n)
            elif s == 12:
                delta_input(1, n)
                act.wait_ge(u_done.sem, u_done.at(n, 2))
                nc.scalar.activation(soft[:], soft[:], ACT.Exp, scale=-1.0).then_inc(sp_done.sem, 1)
                act.wait_ge(sp_done.sem, sp_done.at(n, 1))
                nc.scalar.activation(one_w[:], soft[:], ACT.Identity, bias=1.0).then_inc(sp_done.sem, 1)
            elif s == 14:
                act.wait_ge(outf.sem, outf.at(n - 2, 1))
                act.wait_ge(front.sem, front.at(n, 11))
                nc.scalar.copy(gT[:, q, :], FRO[0:J0 * E0, 0:P]).then_inc(gT_copied.sem, 1)
            elif s == 13:
                act.wait_ge(sp_done.sem, sp_done.at(n, 2))
                nc.scalar.activation(lnw[:], one_w[:], ACT.Ln).then_inc(sp_done.sem, 1)

        pipeline(fore, start, slot, lambda it, par: None, act, between, finish)

    @block.gpsimd
    def _(pool):
        for s in (xn_ready, dbx_ready, y_init, dx_done, rank_step, r_done):
            pool.sem_inc(s.sem, 2 * s.per)
        nc.gpsimd.memset(xproj[:], 0.0)
        nc.gpsimd.memset(H[:, 0, 0, 0:3 * 4 * DH], 0.0)
        nc.gpsimd.memset(b2[:], 0.0).then_inc(zeroed, 1)
        pool.wait_ge(stat_step, 20)
        pool.wait_ge(prep, 1)

        def make_dbx(s, it, par):
            q = par if s < S else 1 - par
            if s == S:
                pool.wait_ge(dx_done.sem, dx_done.at(it + 1, 1))
            k = s // 2
            pool.wait_ge(b_loaded[k % 2].sem, b_loaded[k % 2].at(it, 16 * (k // 2 + 1)))
            pool.wait_ge(scan_done.sem, scan_done.at(it, s - 1))
            nc.gpsimd.tensor_tensor(dBx[:, s % 2], dx[:, q], Bs[:, k % 2, s % 2, :].unsqueeze(1).to_broadcast([P, HALF, T0]),
                                    ALU.mult).then_inc(dbx_ready.sem, 1)

        def slot(s, it, par, first=False, final=False):
            if not (final and s + 1 >= S):
                make_dbx(s + 1, it, par)

        def fore(s, n, q):
            def wide(v):
                return v[:, bass.ds(n * J0, J0)].unsqueeze(2).to_broadcast([P, J0, D])

            xs = X[:, bass.ds(n * J0, J0), :]
            if s == 0:
                if isinstance(n, int) and n == 1:
                    pool.wait_ge(stat_step2, 20)
                pool.wait_ge(front.sem, front.at(n - 1, 2))
                pool.sem_inc(paced, 1)
                nc.gpsimd.tensor_tensor(XR[:], xs, wide(mean), ALU.subtract).then_inc(xn_ready.sem, 1)
                pool.wait_ge(xn_ready.sem, xn_ready.at(n, 1))
                nc.gpsimd.tensor_tensor(XN[:], XR[:], wide(rstd), ALU.mult).then_inc(xn_ready.sem, 1)
            elif s == 1:
                pool.wait_ge(xn_ready.sem, xn_ready.at(n, 2))
                nc.gpsimd.tensor_tensor(XR[:], XN[:], wide(rrms), ALU.mult).then_inc(xn_ready.sem, 1)
            elif s == 2:
                pool.wait_ge(x_done.sem, x_done.at(n - 2, 1))
                pool.sem_inc(paced, 1)
                nc.gpsimd.tensor_tensor(FF[:, q], XN[:], xs, ALU.add).then_inc(xn_ready.sem, 1)
            elif s == 11:
                other = pr[:].unsqueeze(2).to_broadcast([P, J0, E0, E0])
                tri = tri8[:].rearrange("p (e o) -> p e o", o=E0).unsqueeze(1).to_broadcast([P, J0, E0, E0])
                pool.wait_ge(gate_step.sem, gate_step.at(n, 8))
                nc.gpsimd.tensor_tensor(eq[:], eq[:], tri, ALU.mult).then_inc(rank_step.sem, 1)
                pool.wait_ge(rank_step.sem, rank_step.at(n, 1))
                nc.gpsimd.tensor_tensor(gt[:], gt[:], eq[:], ALU.add).then_inc(rank_step.sem, 1)
                pool.wait_ge(rank_step.sem, rank_step.at(n, 2))
                nc.gpsimd.tensor_tensor(eq[:], gt[:], other, ALU.mult).then_inc(rank_step.sem, 1)
            elif s == 10:
                pool.wait_ge(outf.sem, outf.at(n - 2, 1))
                pool.wait_ge(xi_done.sem, xi_done.at(n, 1))
                nc.gpsimd.tensor_tensor(y[:, q], xi[:], Dp[:].unsqueeze(2).to_broadcast([P, HALF, T0]), ALU.mult).then_inc(y_init.sem, 1)
            elif s == 12:
                pool.wait_ge(log_step.sem, log_step.at(n, 1))
                nc.gpsimd.tensor_tensor(umax[:], umax[:], soft[:], ALU.subtract).then_inc(r_done.sem, 1)
            elif s == 13:
                pool.wait_ge(dbx_ready.sem, dbx_ready.at(n - 2, S))
                pool.wait_ge(delta_done.sem, delta_done.at(n, 1))
                nc.gpsimd.tensor_tensor(dx[:, q], delta[:, q], xi[:], ALU.mult).then_inc(dx_done.sem, 1)

        pipeline(fore, lambda: make_dbx(S, -1, 1), slot, lambda it, par: None, pool)

    @block.vector
    def _(dve):
        for s in (conv_step, gate_step, z_done, xi_done, rest_done, cc_done, log_step, delta_done,
                  scan_done, prod_done, add_done, acc_done, yz_done, x_done, restat):
            dve.sem_inc(s.sem, 2 * s.per)

        def norms(tiles, stat_step, root_done):
            token_stats(nc, dve, tiles, stats, mean, rstd, q1, q2, stat_step, root_done)
            r, b = rstd[:, tiles], q2[:, tiles]
            dve.wait_ge(stat_step, 12)
            nc.vector.tensor_tensor(b, b, r, ALU.mult).then_inc(stat_step, 1)
            dve.wait_ge(stat_step, 13)
            nc.vector.tensor_tensor(b, b, r, ALU.mult).then_inc(stat_step, 1)
            dve.wait_ge(stat_step, 14)
            nc.vector.tensor_scalar(b, b, EPS, None, ALU.add).then_inc(stat_step, 1)
            inverse_root(nc, dve, rrms[:, tiles], b, stats[:, tiles, 0], stat_step, root_done, 15, 2)

        dve.wait_ge(xloaded[0], 16)
        for i in range(J0):
            last = nc.vector.bn_stats(stats[:, i, :], X[:, i, :])
        last.then_inc(stat_step, 1)
        norms(FIRST, stat_step, root_done)

        def between(s):
            if s < STATS_END:
                if s % 2 == 0:
                    dve.wait_ge(xloaded[1 + s // 2], 16)
                for i in range(J0 + s * XT // 2, J0 + (s + 1) * XT // 2):
                    last = nc.vector.bn_stats(stats[:, i, :], X[:, i, :])
                if s == STATS_END - 1:
                    last.then_inc(stat_step2, 1)
            elif s == STATS_END:
                norms(OTHERS, stat_step2, root_done2)
            elif s == S - 1:
                dve.wait_ge(wTc, 6)
                nc.vector.memset(dA[:].rearrange("p h (b l) -> p h b l", l=L)[:, :, :, 0:1], 0.0).then_inc(blanked, 1)

        dve.wait_ge(loaded, LOADED)
        nc.vector.tensor_scalar(inproj[:], inproj[:], rmsw[:], None, ALU.mult)
        nc.vector.tensor_scalar(convw[:], convw[:], 0.5, None, ALU.mult)
        nc.vector.tensor_scalar(convb[:], convb[:], 0.5, None, ALU.mult)
        nc.vector.tensor_scalar(outproj[:], outproj[:], 0.5, None, ALU.mult)
        dve.wait_ge(aexp, 1)
        nc.vector.tensor_scalar(A[:], A[:], -1.0, None, ALU.mult).then_inc(prep, 1)
        dve.wait_ge(prep, 1)

        def add(s, it, par):
            if s == 0:
                dve.wait_ge(y_init.sem, y_init.at(it, 1))
            dve.wait_ge(prod_done.sem, prod_done.at(it, s + 1))
            dve.wait_ge(add_done.sem, add_done.at(it, s))
            nc.vector.tensor_tensor(y[:, par], y[:, par], H[:, s % 2], ALU.add).then_inc(add_done.sem, 1)

        def close(it, par):
            add(S - 1, it, par)
            dve.wait_ge(add_done.sem, add_done.at(it, S))
            nc.vector.tensor_tensor(y[:, par], y[:, par], zs[:, par], ALU.mult).then_inc(yz_done.sem, 1)

        def store(it, par):
            dve.wait_ge(outf.sem, outf.at(it, 1))
            dve.wait_ge(acc_done.sem, acc_done.at(it, E0))
            nc.vector.tensor_tensor(X[:, bass.ds(it * J0, J0), :], FRO[:].rearrange("p (j d) -> p j d", d=D), FF[:, par],
                                    ALU.add).then_inc(x_done.sem, 1)

        def restatistic(it):
            dve.wait_ge(x_done.sem, x_done.at(it, 1))
            for j in range(J0):
                last = nc.vector.bn_stats(stats[:, bass.ds(it * J0 + j, 1), :].rearrange("p o s -> p (o s)"),
                                          X[:, bass.ds(it * J0 + j, 1), :].rearrange("p o d -> p (o d)"))
            last.then_inc(restat.sem, 1)

        def accumulate(e, it, par):
            dve.wait_ge(downf.sem, downf.at(it, e + 1))
            dve.wait_ge(acc_done.sem, acc_done.at(it, e))
            if e == 0:
                dve.wait_ge(xn_ready.sem, xn_ready.at(it, 4))
            for j in range(J0):
                last = nc.vector.scalar_tensor_tensor(FF[:, par, j, :], DN[:, j * P:(j + 1) * P], gate[:, par, j, e:e + 1],
                                                      FF[:, par, j, :], ALU.mult, ALU.add)
            last.then_inc(acc_done.sem, 1)

        def slot(s, it, par, first=False, final=False):
            dve.wait_ge(da_ready.sem, da_ready.at(it, 2 * s + 2))
            dve.wait_ge(dbx_ready.sem, dbx_ready.at(it, s + 1))
            dve.wait_ge(add_done.sem, add_done.at(it, s - 1))
            nc.vector.tensor_tensor_scan(H[:, s % 2].rearrange("p h t -> p (h t)"), dA[:].rearrange("p h t -> p (h t)"),
                                         dBx[:, s % 2].rearrange("p h t -> p (h t)"), 0.0, ALU.mult, ALU.add).then_inc(scan_done.sem, 1)
            if s == 0 and not first:
                close(it - 1, 1 - par)
                accumulate(E0 - 1, it - 1, 1 - par)
            if s == 2 and not first:
                store(it - 1, 1 - par)
            if s > 0:
                if s % 2 == 0:
                    accumulate(s // 2 - 1, it, par)
                add(s - 1, it, par)
            dve.wait_ge(scan_done.sem, scan_done.at(it, s + 1))
            dve.wait_ge(cready.sem, cready.at(it, s + 1))
            nc.vector.tensor_tensor(H[:, s % 2], H[:, s % 2], Cp[s % 2][:].unsqueeze(1).to_broadcast([P, HALF, T0]), ALU.mult).then_inc(prod_done.sem, 1)
            if s == 3 and not first:
                restatistic(it - 1)

        def end(it, par):
            accumulate(E0 - 1, it, par)
            close(it, par)
            store(it, par)
            restatistic(it)

        def seqs(ap):
            return ap.rearrange("p (b l) -> p b l", l=L)

        def over(v, n=E0):
            return v.unsqueeze(2).to_broadcast([P, J0, n])

        def fore(s, n, q):
            def gstep(ins, k):
                ins.then_inc(gate_step.sem, 1)
                dve.wait_ge(gate_step.sem, gate_step.at(n, k))

            other = pr[:].unsqueeze(2).to_broadcast([P, J0, E0, E0])
            this = pr[:].unsqueeze(3).to_broadcast([P, J0, E0, E0])
            if s == 5 or s == 7:
                b = (s - 5) // 2
                dve.wait_ge(tap_done.sem, tap_done.at(n, 1 + b))
                src, dst = seqs(FRO[:]), seqs(xch[:, b, :])
                for k in range(1, 4):
                    if k > 1:
                        dve.wait_ge(conv_step.sem, conv_step.at(n, 3 * b + k - 1))
                    nc.vector.scalar_tensor_tensor(dst[:, :, k:], src[:, :, :L - k], convw[:, b, 3 - k:4 - k], dst[:, :, k:],
                                                   ALU.mult, ALU.add).then_inc(conv_step.sem, 1)
            elif s == 6:
                dve.wait_ge(tanh_z.sem, tanh_z.at(n, 1))
                nc.vector.scalar_tensor_tensor(zs[:, q, 0, :], tz[:, 0, :], 1.0, FRO[:], ALU.add, ALU.mult).then_inc(z_done.sem, 1)
            elif s == 8:
                dve.wait_ge(tanh_x.sem, tanh_x.at(n, 1))
                dve.wait_ge(dx_done.sem, dx_done.at(n - 1, 1))
                nc.vector.scalar_tensor_tensor(xi[:], th[:], 1.0, xch[:], ALU.add, ALU.mult).then_inc(xi_done.sem, 1)
                dve.wait_ge(tanh_z.sem, tanh_z.at(n, 2))
                nc.vector.scalar_tensor_tensor(zs[:, q, 1, :], tz[:, 1, :], 1.0, FRO[:], ALU.add, ALU.mult).then_inc(z_done.sem, 1)
            elif s == 9:
                dve.wait_ge(front.sem, front.at(n, 7))
                gstep(nc.vector.tensor_tensor(lg[:], FRO[:, 0:J0 * E0].rearrange("p (j e) -> p j e", e=E0),
                                              br[:].unsqueeze(1).to_broadcast([P, J0, E0]), ALU.add), 1)
                gstep(nc.vector.tensor_reduce(g4[:, 0, :], lg[:], AX.X, ALU.max), 2)
                nc.vector.tensor_tensor(lg[:], lg[:], over(g4[:, 0, :]), ALU.subtract).then_inc(gate_step.sem, 1)
            elif s == 10:
                dve.wait_ge(hi_done.sem, hi_done.at(n, 1))
                nc.vector.scalar_tensor_tensor(rest[:], hi[:], split[0:3 * S, 0:1], FRO[0:3 * S, :], ALU.mult, ALU.add).then_inc(rest_done.sem, 1)
            elif s == 11:
                dve.wait_ge(mid_done.sem, mid_done.at(n, 1))
                dve.wait_ge(cready.sem, cready.at(n - 2, S))
                nc.vector.scalar_tensor_tensor(CC[:, q, :], mid[:], split[0:3 * S, 1:2], rest[:], ALU.mult, ALU.add).then_inc(cc_done.sem, 1)
                dve.wait_ge(gexp.sem, gexp.at(n, 1))
                gstep(nc.vector.tensor_reduce(g4[:, 1, :], pe_[:], AX.X, ALU.add), 4)
                gstep(nc.vector.reciprocal(g4[:, 2, :], g4[:, 1, :]), 5)
                dve.wait_ge(rank_step.sem, rank_step.at(n - 1, 3))
                gstep(nc.vector.tensor_tensor(pr[:], pe_[:], over(g4[:, 2, :]), ALU.mult), 6)
                nc.vector.tensor_tensor(gt[:], other, this, ALU.is_gt).then_inc(gate_step.sem, 1)
                nc.vector.tensor_tensor(eq[:], other, this, ALU.is_equal).then_inc(gate_step.sem, 1)
            elif s == 12:
                dve.wait_ge(rank_step.sem, rank_step.at(n, 3))
                nc.vector.tensor_reduce(cnt[:], gt[:], AX.X, ALU.add)
                gstep(nc.vector.tensor_reduce(cum[:], eq[:], AX.X, ALU.add), 9)
                gstep(nc.vector.tensor_scalar(cum[:], cum[:], TOP_P, None, ALU.is_lt), 10)
                gstep(nc.vector.scalar_tensor_tensor(cum[:], cnt[:], 1.5, cum[:], ALU.is_lt, ALU.max), 11)
                nc.vector.tensor_tensor(gate[:, q], pr[:], cum[:], ALU.mult).then_inc(gate_step.sem, 1)
                dve.wait_ge(sp_done.sem, sp_done.at(n, 2))
                nc.vector.scalar_tensor_tensor(soft[:], one_w[:], -1.0, soft[:], ALU.add, ALU.subtract).then_inc(log_step.sem, 1)
            elif s == 13:
                dve.wait_ge(sp_done.sem, sp_done.at(n, 3))
                nc.vector.scalar_tensor_tensor(lnw[:], one_w[:], 1.0, lnw[:], ALU.is_gt, ALU.mult).then_inc(log_step.sem, 1)
                dve.wait_ge(log_step.sem, log_step.at(n, 2))
                dve.wait_ge(r_done.sem, r_done.at(n, 1))
                dve.wait_ge(da_ready.sem, da_ready.at(n - 2, 2 * S))
                nc.vector.tensor_tensor(delta[:, q], umax[:], lnw[:], ALU.add).then_inc(delta_done.sem, 1)

        pipeline(fore, lambda: None, slot, end, dve, between)
        dve.wait_ge(restat.sem, restat.at(IT0 - 1, 1))


J1 = L // P
NSEQ = NTOK // L
HEADS, LAT, DH = 16, 64, 8
GROUPS = 4
HG = HEADS // GROUPS
TERMS = ((0, 0), (0, 1), (0, 2), (1, 0), (1, 1), (2, 0))
KQ = len(TERMS) * DH
SCALE = 1.0 / float(np.sqrt(DH))
E1, CAP = 128, 32
NSLOT = E1 * CAP


def token_stats(nc, dve, tiles, stats, mean, rstd, q1, q2, stat_step, root_done):
    dve.wait_ge(stat_step, 1)
    me, mo = stats[:, tiles, 1], stats[:, tiles, 4]
    m, r, a, b = mean[:, tiles], rstd[:, tiles], q1[:, tiles], q2[:, tiles]
    nc.vector.tensor_tensor(a, me, mo, ALU.subtract).then_inc(stat_step, 1)
    nc.vector.tensor_tensor(m, me, mo, ALU.add)
    nc.vector.tensor_tensor(r, stats[:, tiles, 2], stats[:, tiles, 5], ALU.add).then_inc(stat_step, 1)
    dve.wait_ge(stat_step, 3)
    nc.vector.tensor_tensor(b, a, a, ALU.mult)
    nc.vector.tensor_scalar(m, m, 0.5, None, ALU.mult).then_inc(stat_step, 1)
    dve.wait_ge(stat_step, 4)
    nc.vector.tensor_scalar(b, b, 0.25, None, ALU.mult).then_inc(stat_step, 1)
    dve.wait_ge(stat_step, 5)
    nc.vector.scalar_tensor_tensor(b, r, 1.0 / D, b, ALU.mult, ALU.add).then_inc(stat_step, 1)
    dve.wait_ge(stat_step, 6)
    nc.vector.tensor_scalar(a, b, EPS, None, ALU.add).then_inc(stat_step, 1)
    inverse_root(nc, dve, r, a, stats[:, tiles, 0], stat_step, root_done, 7, 1)


def inverse_root(nc, dve, out, v, root, stat_step, root_done, k, r):
    dve.wait_ge(root_done, r)
    nc.vector.reciprocal(out, root).then_inc(stat_step, 1)
    dve.wait_ge(stat_step, k + 1)
    nc.vector.tensor_tensor(root, out, out, ALU.mult).then_inc(stat_step, 1)
    dve.wait_ge(stat_step, k + 2)
    nc.vector.tensor_tensor(root, root, v, ALU.mult).then_inc(stat_step, 1)
    dve.wait_ge(stat_step, k + 3)
    nc.vector.tensor_scalar(root, root, -0.5, 1.5, ALU.mult, ALU.add).then_inc(stat_step, 1)
    dve.wait_ge(stat_step, k + 4)
    nc.vector.tensor_tensor(out, out, root, ALU.mult).then_inc(stat_step, 1)


def layer1(nc, ctx, t, dram, scratch):
    def sb(name, shape, dt=F32):
        return ctx.enter_context(nc.sbuf_tensor(name, shape, dt))

    def signal(name, per):
        return Signal(ctx.enter_context(nc.semaphore(name)), per)

    def sem(name):
        return ctx.enter_context(nc.semaphore(name))

    X, ident, identb, WE, carry = t["X"], t["ident"], t["identb"], t["WE"], t["carry"]
    EF, EU, LG, LOC, iota = t["EF"], t["EU"], t["LG"], t["LOC"], t["iota"]
    stats, wq, wk, wqr, wkr, wvg = (t[n] for n in ("stats", "wq", "wk", "wqr", "wkr", "wvg"))
    mean = sb("mean1", [P, NT]); rstd = sb("rstd1", [P, NT])
    q1 = sb("q11", [P, NT]); q2 = sb("q21", [P, NT])
    wc = sb("wc", [P, D])
    cos = sb("cos", [P, L]); sin = sb("sin", [P, L])
    maskq = sb("maskq", [P, HG, P], BF16); maskk = sb("maskk", [P, HG, P], BF16)
    tri = sb("tri", [P, P], BF16); ones = sb("ones", [P, P], BF16)
    XN = sb("XN2", [P, 2, J1, D]); XM = sb("XM2", [P, J1, D]); xnT = sb("xnT2", [P, L])
    t1 = sb("t1", [P, 2, L]); t2 = sb("t2", [P, 2, L]); QK = sb("QK", [P, 2, L]); R1 = sb("R1", [P, 2, L])
    SPL = sb("SPL", [P, 3, 2, L], BF16)
    QS = [sb(f"QS{i}", [64, HEADS, L], BF16) for i in range(2)]
    KS = [sb(f"KS{i}", [64, HEADS, L], BF16) for i in range(2)]
    V = [sb(f"V{i}", [P, J1, HEADS, DH + 1]) for i in range(2)]; VN = sb("VN", [P, 2, J1, HEADS, DH])
    PT = sb("PT", [P, 2, 1536])
    OSB = sb("OSB", [P, GROUPS, L]); rec = sb("rec", [P, HEADS]); YN = sb("YN", [P, J1, HEADS, DH]); yT = sb("yT", [P, L])
    NM = sb("NM", [P, J1, HEADS]); NR = sb("NR", [P, J1, HEADS]); NMS = sb("NMS", [P, J1, P // HEADS, HEADS], BF16)
    NMT = sb("NMT", [3 * HEADS, L], BF16)
    mx = sb("mx", [P, J1, 8]); ix = sb("ix", [P, J1, 8], mybir.dt.uint32); ef = sb("ef", [P, J1, 2])
    MK = sb("MK", [P, J1, 2, P], BF16); cs = sb("cs", [P, 2, P]); loc = sb("loc", [P, J1, 2])
    zeros = sb("zeros", [P, 2 * NTOK * D // (P * NSEQ)])
    SS = [ctx.enter_context(nc.psum_tensor(f"SS{i}", [P, 1536], F32)) for i in range(2)]
    FR = ctx.enter_context(nc.psum_tensor("FR", [P, 512], F32))
    OT = ctx.enter_context(nc.psum_tensor("OT", [P, 2, L], F32))
    FRb = FR[:].bitcast(BF16)

    fr_x = signal("fr_x", 1); fr_vg = signal("fr_vg", 1); fr_qk = signal("fr_qk", 1); fr_rot = signal("fr_rot", 1)
    fr_route = signal("fr_route", 2); fr_nm = signal("fr_nm", 1); fr_o = signal("fr_o", 2); fr_y = signal("fr_y", 1)
    fr_wc = signal("fr_wc", 1); p1 = signal("p1", GROUPS); p2 = signal("p2", GROUPS); pv = signal("pv", GROUPS)
    xT_done = signal("xT_done", 1); v_done = signal("v_done", 1); part_done = signal("part_done", 2)
    nm_copied = signal("nm_copied", 1); exp_done = signal("exp_done", GROUPS); ot_copied = signal("ot_copied", 2)
    yT_done = signal("yT_done", 1)
    top = signal("top", 4); rope = signal("rope", 2); route = signal("route", 13); max_done = signal("max_done", 8)
    nm_step = signal("nm_step", 4); epi = signal("epi", 4); x_upd = signal("x_upd", 1)
    xn_ready = signal("xn_ready1", 2); rest = signal("rest1", 3); v_placed = signal("v_placed", 1)
    xn_stored = signal("xn_stored", 16); parts_out = signal("parts_out", 16); parts_in = [signal(f"parts_in{i}", 16 * 12) for i in range(2)]
    nm_out = signal("nm_out", 16); nm_in = signal("nm_in", 16)
    loaded = sem("loaded1"); stat_step = sem("stat_step1"); root_done = sem("root_done1"); we_loaded = sem("we_loaded")
    yzero = sem("yzero")
    poolset = sem("poolset"); paced = sem("paced"); pool_paced = sem("pool_paced"); offs = sem("offs")
    off, junk = t["off"], sb("junk", [P, 2, P])

    block = ctx.enter_context(nc.Block())
    loads = [(wvg[:, P:], dram["L1_ffn_wg"]), (wc[:], dram["L1_attn_Wc"]), (cos[:], dram["c_cos"]), (sin[:], dram["c_sin"]),
             (maskq[:].rearrange("p a b -> p (a b)"), dram["c_maskq"]), (maskk[:].rearrange("p a b -> p (a b)"), dram["c_maskk"]),
             (tri[:], dram["c_tri"]), (iota[:], dram["c_iota"])]
    LOADED = 16 * len(loads)

    parts_d, nm_d, xn_d, y_d = scratch["parts"], scratch["nm"], scratch["xn"], scratch["y"]

    def schedule(eng, norm=None, front=None, split=None, pass1=None, maxima=None, pass2=None, values=None, epilogue=None):
        def do(piece, *args):
            if piece is not None:
                piece(*args)

        def step(c, par, normed=True, fronted=True, passed1=True, passed2=True, closed=True):
            other = 1 - par

            def both_passes(g, *between):
                if passed1:
                    do(pass1, g, c + 1, other)
                for piece in between:
                    piece()
                if passed2:
                    do(pass2, g, c, par)

            def of_front(piece, k):
                if fronted:
                    do(piece, k, c + 2, par)

            def of_epilogue(k):
                if closed:
                    do(epilogue, k, c - 1, other)

            def values_of(g):
                if passed2:
                    do(values, g, c, par)

            of_front(front, 0)
            if closed:
                do(values, GROUPS - 1, c - 1, other)
            of_front(front, 1)
            both_passes(0)
            of_front(front, 2)
            both_passes(1, lambda: of_front(front, 3))
            of_front(split, 0)
            of_epilogue(0)
            values_of(0)
            of_epilogue(1)
            of_front(split, 1)
            both_passes(2, lambda: of_epilogue(2))
            of_epilogue(3)
            if normed:
                do(norm, c + 3, other)
            of_front(front, 4)
            values_of(1)
            both_passes(3, lambda: of_front(front, 5))
            if passed1:
                do(maxima, c + 1, other)
            values_of(2)

        do(norm, 0, 0)
        step(-2, 0, passed1=False, passed2=False, closed=False)
        step(-1, 1, passed2=False, closed=False)
        step(0, 0, closed=False)
        with eng.Fori(0, NSEQ // 2 - 2) as i:
            for k in range(2):
                step(i * 2 + (1 + k), 1 - k)
        step(NSEQ - 3, 1, normed=False)
        step(NSEQ - 2, 0, normed=False, fronted=False)
        step(NSEQ - 1, 1, normed=False, fronted=False, passed1=False)
        step(NSEQ, 0, normed=False, fronted=False, passed1=False, passed2=False)

    @block.sync
    def _(sp):
        for dst, src in loads:
            sp.dma_start(dst, src, allow_slow_non_contiguous=True).then_inc(loaded, 16)
        sp.wait_ge(poolset, 2)
        sp.wait_ge(stat_step, 1)
        sp.sem_inc(xn_stored.sem, 32)
        sp.sem_inc(parts_out.sem, 32)
        for half in range(2):
            sp.sem_inc(parts_in[half].sem, 2 * 16 * 12)
        sp.sem_inc(nm_out.sem, 32)
        sp.sem_inc(nm_in.sem, 32)

        def norm(c, par):
            sp.wait_ge(xn_ready.sem, xn_ready.at(c, 2))
            sp.dma_start(xn_d.rearrange("(i p) d -> p i d", p=P)[:, bass.ds(c * J1, J1), :], XN[:, par]).then_inc(xn_stored.sem, 16)
            sp.dma_start(WE[:, bass.ds(c * (E1 // NSEQ), E1 // NSEQ), :],
                         dram["L1_ffn_we"].rearrange("e d f -> d e f")[:, bass.ds(c * (E1 // NSEQ), E1 // NSEQ), :]).then_inc(we_loaded, 16)
            sp.dma_start(y_d.rearrange("(p c r) d -> p c (r d)", p=P, c=NSEQ)[:, bass.ds(c, 1), :],
                         zeros[:].unsqueeze(1)).then_inc(yzero, 16)

        def load(half, c, par):
            sp.wait_ge(p2.sem, p2.at(c - 2, 2 * half + 2))
            heads = slice(half * HEADS // 2, (half + 1) * HEADS // 2)
            src = parts_d[par].rearrange("(h d) (r q t) -> d r q h t", d=DH, r=3, q=2)
            for n, term in enumerate(TERMS):
                for q, dst in enumerate((QS, KS)):
                    sp.dma_start(dst[par][DH * n:DH * n + DH, heads, :], src[:, term[q], q, heads, :]).then_inc(parts_in[half].sem, 16)

        def split(k, c, par):
            if k == 1:
                sp.wait_ge(rest.sem, rest.at(c, 3))
                for half in range(2):
                    sp.wait_ge(parts_in[half].sem, parts_in[half].at(c - 2, 16 * 12))
                sp.dma_start(parts_d[par], SPL[:].rearrange("p r q t -> p (r q t)")).then_inc(parts_out.sem, 16)

        def front(k, c, par):
            if k == 4:
                sp.wait_ge(parts_out.sem, parts_out.at(c, 16))
                load(0, c, par)

        def maxima(c, par):
            sp.wait_ge(nm_copied.sem, nm_copied.at(c, 1))
            sp.wait_ge(nm_in.sem, nm_in.at(c - 1, 16))
            sp.dma_start(nm_d[par], NMT[:]).then_inc(nm_out.sem, 16)
            sp.wait_ge(nm_out.sem, nm_out.at(c, 16))
            sp.dma_start(QS[par][KQ:KQ + 3, :, :], nm_d[par].rearrange("(r h) t -> r h t", r=3)).then_inc(nm_in.sem, 16)

        def pass1(g, c, par):
            if g == 0:
                load(1, c, par)

        schedule(sp, norm=norm, front=front, split=split, pass1=pass1, maxima=maxima)
        sp.wait_ge(xn_stored.sem, xn_stored.at(NSEQ - 1, 16))
        sp.wait_ge(nm_in.sem, nm_in.at(NSEQ - 1, 16))
        sp.wait_ge(we_loaded, 16 * NSEQ)
        sp.wait_ge(yzero, 16 * NSEQ)

    @block.tensor
    def _(pe):
        for s in (fr_x, fr_vg, fr_qk, fr_rot, fr_route, fr_nm, fr_o, fr_y, fr_wc, p1, p2, pv):
            pe.sem_inc(s.sem, 2 * s.per)
        pe.wait_ge(loaded, LOADED)
        pe.wait_ge(poolset, 2)
        pe.wait_ge(stat_step, 1)

        def front(k, c, par):
            if k == 0:
                pe.wait_ge(nm_copied.sem, nm_copied.at(c - 2, 1))
                pe.wait_ge(route.sem, route.at(c - 1, 10))
                pe.wait_ge(xn_ready.sem, xn_ready.at(c, 2))
                for j in range(J1):
                    last = nc.tensor.transpose(FR[:, j * P:(j + 1) * P], XN[:, par, j, :], ident[:])
                last.then_inc(fr_x.sem, 1)
            elif k == 1:
                pe.wait_ge(xT_done.sem, xT_done.at(c, 1))
                for j in range(J1):
                    last = nc.tensor.matmul(FR[:, 2 * j * P:2 * (j + 1) * P], xnT[:, j * P:(j + 1) * P], wvg[:], start=True, stop=True)
                last.then_inc(fr_vg.sem, 1)
            elif k == 2:
                pe.wait_ge(v_done.sem, v_done.at(c, 1))
                pe.wait_ge(top.sem, top.at(c, 4))
                for q, w in enumerate((wq, wk)):
                    last = nc.tensor.matmul(FR[:, q * L:(q + 1) * L], w[:], xnT[:], start=True, stop=True)
                last.then_inc(fr_qk.sem, 1)
            elif k == 3:
                pe.wait_ge(rope.sem, rope.at(c, 1))
                for q, w in enumerate((wqr, wkr)):
                    last = nc.tensor.matmul(FR[:, q * L:(q + 1) * L], w[:], xnT[:], start=True, stop=True)
                last.then_inc(fr_rot.sem, 1)
            else:
                j = k - 4
                if j == 0:
                    pe.wait_ge(rope.sem, rope.at(c, 2))
                    pe.wait_ge(x_upd.sem, x_upd.at(c - 3, 1))
                    pe.wait_ge(route.sem, route.at(c, 4))
                else:
                    pe.wait_ge(route.sem, route.at(c, 6))
                rhs = MK[:, j, :, :].rearrange("p c e -> p (c e)")
                nc.tensor.matmul(FR[:, 0:2 * P], tri[:], rhs, start=True, stop=True)
                nc.tensor.matmul(FR[:, 2 * P:4 * P], ones[:], rhs, start=True, stop=True).then_inc(fr_route.sem, 1)

        def pass1(g, c, par):
            S_ = SS[1]
            if g % 2 == 0:
                pe.wait_ge(parts_in[g // 2].sem, parts_in[g // 2].at(c, 16 * 12))
            pe.wait_ge(max_done.sem, max_done.at(c, 2 * g))
            nc.tensor.matmul(S_[:, 0:512], identb[:], maskq[:].rearrange("p a b -> p (a b)"), start=True, stop=False)
            for j in range(HG):
                h = HG * g + j
                nc.tensor.matmul(S_[:, j * P:(j + 1) * P], QS[par][0:KQ, h, 0:P], KS[par][0:KQ, h, 0:P], start=False, stop=(j == HG - 1))
            for b in range(2):
                bank = S_[:, 512 * (b + 1):512 * (b + 2)]
                for j in range(2):
                    h = HG * g + 2 * b + j
                    nc.tensor.matmul(bank[:, j * L:(j + 1) * L], QS[par][0:KQ, h, P:L], KS[par][0:KQ, h, :], start=(j == 0), stop=False)
                last = nc.tensor.matmul(bank.rearrange("p (j k) -> p j k", j=2)[:, :, P:L], identb[:], maskq[:, 0:2, :], start=False, stop=True)
            last.then_inc(p1.sem, 1)

        def maxima(c, par):
            pe.wait_ge(nm_step.sem, nm_step.at(c, 4))
            if isinstance(c, int) and c == NSEQ - 1:
                pe.wait_ge(x_upd.sem, x_upd.at(c - 2, 1))
            else:
                pe.wait_ge(route.sem, route.at(c + 1, 10))
            for j in range(J1):
                last = nc.tensor.transpose(FRb[:, j * P:(j + 1) * P], NMS[:, j, :, :].rearrange("p r h -> p (r h)"), identb[:])
            last.then_inc(fr_nm.sem, 1)

        def values(g, c, par):
            pe.wait_ge(exp_done.sem, exp_done.at(c, g + 1))
            if g == 0:
                pe.wait_ge(v_placed.sem, v_placed.at(c, 1))
                pe.wait_ge(ot_copied.sem, ot_copied.at(c - 1, 2))
            if g == 2:
                pe.wait_ge(ot_copied.sem, ot_copied.at(c, 1))
            for j in range(HG):
                h, rows = HG * g + j, slice(32 * j, 32 * j + DH + 1)
                nc.tensor.matmul(OT[rows, g % 2, :], V[par][:, 0, h, :], PT[:, g % 2, j * L:(j + 1) * L],
                                 start=True, stop=False, tile_position=(0, 32 * j))
                last = nc.tensor.matmul(OT[rows, g % 2, P:L], V[par][:, 1, h, :], PT[:, g % 2, 1024 + j * P:1024 + (j + 1) * P],
                                        start=False, stop=True, tile_position=(0, 32 * j))
            last.then_inc(pv.sem, 1)

        def pass2(g, c, par):
            S_ = SS[0]
            if g == 0:
                pe.wait_ge(nm_in.sem, nm_in.at(c, 16))
            pe.wait_ge(exp_done.sem, exp_done.at(c, g))
            for b in range(2):
                bank = S_[:, 512 * b:512 * (b + 1)]
                for j in range(2):
                    h = HG * g + 2 * b + j
                    nc.tensor.matmul(bank[:, j * L:(j + 1) * L], KS[par][0:KQ + 3, h, 0:P], QS[par][0:KQ + 3, h, :], start=(j == 0), stop=False)
                nc.tensor.matmul(bank.rearrange("p (j q) -> p j q", j=2)[:, :, 0:P], identb[:], maskk[:, 0:2, :], start=False, stop=True)
            nc.tensor.matmul(S_[:, 1024:1536], identb[:], maskk[:].rearrange("p a b -> p (a b)"), start=True, stop=False)
            for j in range(HG):
                h = HG * g + j
                last = nc.tensor.matmul(S_[:, 1024 + j * P:1024 + (j + 1) * P], KS[par][0:KQ + 3, h, P:L], QS[par][0:KQ + 3, h, P:L],
                                        start=False, stop=(j == HG - 1))
            last.then_inc(p2.sem, 1)

        def epilogue(k, c, par):
            if k < J1:
                if k == 0:
                    pe.wait_ge(ot_copied.sem, ot_copied.at(c, 2))
                    if not isinstance(c, int) or c < NSEQ - 3:
                        pe.wait_ge(rope.sem, rope.at(c + 3, 2))
                    elif c < NSEQ - 1:
                        pe.wait_ge(nm_copied.sem, nm_copied.at(c + 1, 1))
                    else:
                        pe.wait_ge(x_upd.sem, x_upd.at(c - 1, 1))
                else:
                    pe.wait_ge(epi.sem, epi.at(c, 2))
                for g in range(GROUPS):
                    last = nc.tensor.transpose(FR[:, g * P:(g + 1) * P], OSB[:, g, k * P:(k + 1) * P], ident[:])
                last.then_inc(fr_o.sem, 1)
            elif k == J1:
                pe.wait_ge(epi.sem, epi.at(c, 4))
                for j in range(J1):
                    last = nc.tensor.transpose(FR[:, j * P:(j + 1) * P], YN[:, j, :, :].rearrange("p h d -> p (h d)"), ident[:])
                last.then_inc(fr_y.sem, 1)
            else:
                pe.wait_ge(yT_done.sem, yT_done.at(c, 1))
                for j in range(J1):
                    last = nc.tensor.matmul(FR[:, j * P:(j + 1) * P], yT[:, j * P:(j + 1) * P], wc[:], start=True, stop=True)
                last.then_inc(fr_wc.sem, 1)

        schedule(pe, front=front, pass1=pass1, maxima=maxima, pass2=pass2, values=values, epilogue=epilogue)

    @block.scalar
    def _(act):
        for s in (xT_done, v_done, part_done, nm_copied, exp_done, ot_copied, yT_done):
            act.sem_inc(s.sem, 2 * s.per)
        act.wait_ge(poolset, 2)
        act.wait_ge(stat_step, 7)
        nc.scalar.activation(stats[:, :, 0], q1[:], ACT.Sqrt).then_inc(root_done, 1)

        def front(k, c, par):
            if k == 0:
                act.wait_ge(fr_x.sem, fr_x.at(c, 1))
                act.wait_ge(fr_rot.sem, fr_rot.at(c - 1, 1))
                nc.scalar.copy(xnT[:], FR[:, 0:L]).then_inc(xT_done.sem, 1)
            elif k == 1:
                act.wait_ge(fr_vg.sem, fr_vg.at(c, 1))
                act.wait_ge(v_placed.sem, v_placed.at(c - 2, 1))
                vg = FR[:].rearrange("p (j v h d) -> p j v h d", j=J1, v=2, d=DH)
                nc.scalar.copy(VN[:, par], vg[:, :, 0, :, :]).then_inc(v_done.sem, 1)

        def split(k, c, par):
            act.wait_ge(rest.sem, rest.at(c, 1 + k))
            if k == 0:
                act.wait_ge(parts_out.sem, parts_out.at(c - 1, 16))
            nc.scalar.copy(SPL[:, k], (QK if k == 0 else R1)[:]).then_inc(part_done.sem, 1)

        def maxima(c, par):
            act.wait_ge(fr_nm.sem, fr_nm.at(c, 1))
            act.wait_ge(nm_out.sem, nm_out.at(c - 1, 16))
            nc.scalar.copy(NMT[:], FRb[0:3 * HEADS, 0:L]).then_inc(nm_copied.sem, 1)

        def pass2(g, c, par):
            act.wait_ge(p2.sem, p2.at(c, g + 1))
            act.wait_ge(pv.sem, pv.at(c, g - 1))
            nc.scalar.activation(PT[:, g % 2, :], SS[0][:], ACT.Exp, scale=SCALE).then_inc(exp_done.sem, 1)

        def values(g, c, par):
            if g % 2 == 1:
                k = g // 2
                act.wait_ge(pv.sem, pv.at(c, 2 * k + 2))
                act.wait_ge(fr_o.sem, fr_o.at(c - 1, 2))
                nc.scalar.copy(OSB[:, 2 * k:2 * k + 2, :], OT[:]).then_inc(ot_copied.sem, 1)

        def epilogue(k, c, par):
            if k == 2:
                act.wait_ge(fr_y.sem, fr_y.at(c, 1))
                act.wait_ge(fr_wc.sem, fr_wc.at(c - 1, 1))
                nc.scalar.copy(yT[:], FR[:, 0:L]).then_inc(yT_done.sem, 1)

        schedule(act, front=front, split=split, maxima=maxima, pass2=pass2, values=values, epilogue=epilogue)

    @block.gpsimd
    def _(pool):
        pool.sem_inc(xn_ready.sem, 2 * xn_ready.per)
        pool.sem_inc(rest.sem, 2 * rest.per)
        pool.sem_inc(v_placed.sem, 2)
        nc.gpsimd.memset(zeros[:], 0.0)
        nc.gpsimd.memset(ones[:], 1.0)
        nc.gpsimd.memset(carry[:], 0.0)
        for i in range(2):
            nc.gpsimd.memset(V[i][:], 1.0).then_inc(poolset, 1)
        pool.wait_ge(stat_step, 12)

        def norm(c, par):
            def wide(v):
                return v[:, bass.ds(c * J1, J1)].unsqueeze(2).to_broadcast([P, J1, D])

            pool.wait_ge(fr_x.sem, fr_x.at(c - 2, 1))
            pool.wait_ge(xn_stored.sem, xn_stored.at(c - 2, 16))
            nc.gpsimd.tensor_tensor(XM[:], X[:, bass.ds(c * J1, J1), :], wide(mean), ALU.subtract).then_inc(xn_ready.sem, 1)
            pool.wait_ge(xn_ready.sem, xn_ready.at(c, 1))
            nc.gpsimd.tensor_tensor(XN[:, par], XM[:], wide(rstd), ALU.mult).then_inc(xn_ready.sem, 1)

        def split(k, c, par):
            if k == 0:
                pool.wait_ge(rope.sem, rope.at(c, 2))
                nc.gpsimd.tensor_tensor(QK[:], t1[:], t2[:], ALU.add).then_inc(rest.sem, 1)
                pool.wait_ge(part_done.sem, part_done.at(c, 1))
                nc.gpsimd.tensor_tensor(R1[:], QK[:], SPL[:, 0], ALU.subtract).then_inc(rest.sem, 1)
            else:
                pool.wait_ge(part_done.sem, part_done.at(c, 2))
                nc.gpsimd.tensor_tensor(SPL[:, 2], R1[:], SPL[:, 1], ALU.subtract).then_inc(rest.sem, 1)

        def pass2(g, c, par):
            if g == 0:
                pool.wait_ge(v_done.sem, v_done.at(c, 1))
                pool.wait_ge(pv.sem, pv.at(c - 2, GROUPS))
                pool.sem_inc(pool_paced, 1)
                nc.gpsimd.tensor_copy(V[par][:, :, :, 0:DH], VN[:, par]).then_inc(v_placed.sem, 1)

        schedule(pool, norm=norm, split=split, pass2=pass2)

    @block.vector
    def _(dve):
        for s in (top, rope, route, max_done, nm_step, epi, x_upd):
            dve.sem_inc(s.sem, 2 * s.per)
        nc.vector.memset(OT[:], 0.0)
        nc.vector.memset(NMS[:], 0.0)
        for i in range(2):
            nc.vector.memset(KS[i][32:64], 1.0)
        dve.sem_inc(stat_step, 1)
        token_stats(nc, dve, slice(0, NT), stats, mean, rstd, q1, q2, stat_step, root_done)
        dve.wait_ge(poolset, 2)

        def step(ins, c, k):
            ins.then_inc(route.sem, 1)
            dve.wait_ge(route.sem, route.at(c, k))

        def front(k, c, par):
            fr = FR[:].rearrange("p (q t) -> p q t", q=2)
            tiles = bass.ds(c * J1, J1)
            wide = lambda v: v[:].unsqueeze(1).to_broadcast([P, 2, L])
            if k == 1:
                dve.wait_ge(fr_vg.sem, fr_vg.at(c, 1))
                dve.wait_ge(v_done.sem, v_done.at(c, 1))
                dve.wait_ge(route.sem, route.at(c - 1, 13))
                dve.sem_inc(paced, 1)
                for j in range(J1):
                    nc.vector.max(mx[:, j, :], FR[:, (2 * j + 1) * P:(2 * j + 2) * P]).then_inc(top.sem, 1)
                dve.wait_ge(top.sem, top.at(c, J1))
                dve.sem_inc(paced, 1)
                for j in range(J1):
                    nc.vector.max_index(ix[:, j, :], mx[:, j, :], FR[:, (2 * j + 1) * P:(2 * j + 2) * P]).then_inc(top.sem, 1)
            elif k == 2:
                dve.wait_ge(fr_qk.sem, fr_qk.at(c, 1))
                dve.wait_ge(rest.sem, rest.at(c - 1, 1))
                nc.vector.tensor_tensor(t1[:], fr, wide(cos), ALU.mult).then_inc(rope.sem, 1)
            elif k == 3:
                dve.wait_ge(fr_rot.sem, fr_rot.at(c, 1))
                nc.vector.tensor_tensor(t2[:], fr, wide(sin), ALU.mult).then_inc(rope.sem, 1)
                dve.wait_ge(top.sem, top.at(c, 2 * J1))
                step(nc.vector.tensor_copy(ef[:], ix[:, :, 0:2]), c, 1)
                step(nc.vector.tensor_copy(EF[:, tiles, :], ef[:]), c, 2)
                step(nc.vector.tensor_copy(EU[:, tiles, :], ix[:, :, 0:2]), c, 3)
                nc.vector.tensor_tensor(MK[:], iota[:].unsqueeze(1).unsqueeze(1).to_broadcast([P, J1, 2, P]),
                                        ef[:].unsqueeze(3).to_broadcast([P, J1, 2, P]), ALU.is_equal).then_inc(route.sem, 1)
            elif k >= 4:
                j = k - 4
                dve.wait_ge(fr_route.sem, fr_route.at(c, j + 1))
                fv = FR[:].rearrange("p (s e) -> p s e", e=P)
                n = 4 + 4 * j
                step(nc.vector.tensor_tensor(cs[:], fv[:, 0:2, :], carry[:], ALU.add), c, n + 1)
                step(nc.vector.tensor_tensor(carry[:], fv[:, 2:4, :], carry[:], ALU.add), c, n + 2)
                step(nc.vector.tensor_tensor(cs[:], cs[:], MK[:, j, :, :], ALU.mult), c, n + 3)
                step(nc.vector.tensor_reduce(loc[:, j, :], cs[:], AX.X, ALU.add), c, n + 4)
                if j == J1 - 1:
                    nc.vector.tensor_copy(LG[:, tiles, :], mx[:, :, 0:2])
                    nc.vector.tensor_copy(LOC[:, tiles, :], loc[:]).then_inc(route.sem, 1)

        def pass1(g, c, par):
            dve.wait_ge(p1.sem, p1.at(c, g + 1))
            if g == 0:
                dve.wait_ge(nm_step.sem, nm_step.at(c - 1, 4))
            nc.vector.tensor_reduce(NM[:, 0, HG * g:HG * g + HG], SS[1][:, 0:512].rearrange("p (h k) -> p h k", h=HG),
                                    AX.X, ALU.max, negate=True).then_inc(max_done.sem, 1)
            nc.vector.tensor_reduce(NM[:, 1, HG * g:HG * g + HG], SS[1][:, 512:1536].rearrange("p (h k) -> p h k", h=HG),
                                    AX.X, ALU.max, negate=True).then_inc(max_done.sem, 1)
            if g == GROUPS - 1:
                dve.wait_ge(max_done.sem, max_done.at(c, 8))
                dve.wait_ge(fr_nm.sem, fr_nm.at(c - 1, 1))
                nc.vector.tensor_copy(NMS[:, :, 0, :], NM[:]).then_inc(nm_step.sem, 1)
                dve.wait_ge(nm_step.sem, nm_step.at(c, 1))
                nc.vector.tensor_tensor(NR[:], NM[:], NMS[:, :, 0, :], ALU.subtract).then_inc(nm_step.sem, 1)
                dve.wait_ge(nm_step.sem, nm_step.at(c, 2))
                nc.vector.tensor_copy(NMS[:, :, 1, :], NR[:]).then_inc(nm_step.sem, 1)
                dve.wait_ge(nm_step.sem, nm_step.at(c, 3))
                nc.vector.tensor_tensor(NMS[:, :, 2, :], NR[:], NMS[:, :, 1, :], ALU.subtract).then_inc(nm_step.sem, 1)

        def offsets(n):
            if n == 0:
                dve.wait_ge(route.sem, route.at(NSEQ - 1, 13))
            for i in range(n * NT // 8, (n + 1) * NT // 8):
                if i >= 2:
                    dve.wait_ge(offs, i - 1)
                nc.vector.scalar_tensor_tensor(junk[:, i % 2, :], iota[:], EF[:, i, 1:2], carry[:, 0, :], ALU.is_equal, ALU.mult,
                                               accum_out=off[:, i:i + 1]).then_inc(offs, 1)

        def epilogue(k, c, par):
            if isinstance(c, int) and c >= NSEQ - 3 and k != 2 and not (c == NSEQ - 3 and k == 0):
                offsets(3 * (c - NSEQ + 3) + min(k, 2) - 1)
            if k < J1:
                dve.wait_ge(fr_o.sem, fr_o.at(c, k + 1))
                if k == 0:
                    dve.wait_ge(fr_y.sem, fr_y.at(c - 1, 1))
                else:
                    dve.wait_ge(epi.sem, epi.at(c, 2))
                o = FR[:].rearrange("p (h w) -> p h w", w=32)
                nc.vector.reciprocal(rec[:], o[:, :, DH]).then_inc(epi.sem, 1)
                dve.wait_ge(epi.sem, epi.at(c, 2 * k + 1))
                nc.vector.tensor_tensor(YN[:, k, :, :], o[:, :, 0:DH], rec[:].unsqueeze(2).to_broadcast([P, HEADS, DH]),
                                        ALU.mult).then_inc(epi.sem, 1)
            elif k == J1 + 1:
                dve.wait_ge(fr_wc.sem, fr_wc.at(c, 1))
                xs = X[:, bass.ds(c * J1, J1), :]
                nc.vector.tensor_tensor(xs, FR[:, 0:L].rearrange("p (j d) -> p j d", j=J1), xs, ALU.add).then_inc(x_upd.sem, 1)

        schedule(dve, front=front, pass1=pass1, epilogue=epilogue)
        dve.wait_ge(offs, NT)


def experts1(nc, ctx, t, dram, scratch, out):
    def sb(name, shape, dt=F32):
        return ctx.enter_context(nc.sbuf_tensor(name, shape, dt))

    def sem(name):
        return ctx.enter_context(nc.semaphore(name))

    X, ident, WE, carry, iota = t["X"], t["ident"], t["WE"], t["carry"], t["iota"]
    EF, EU, LG, LOC = t["EF"], t["EU"], t["LG"], t["LOC"]
    xn_d, y_d = scratch["xn"], scratch["y"]
    U32 = mybir.dt.uint32
    NG = NSLOT // P
    NV = 2
    FAR = float(1 << 20)
    off = t["off"]
    W = sb("W", [P, NT, 2]); wd = sb("wd", [P, NT])
    VAL = sb("VAL", [P, NT, 2, NV], BF16)
    lo_u = sb("lo_u", [P, NT, 2], U32); hi_u = sb("hi_u", [P, NT, 2], U32)
    lo_e = sb("lo_e", [P, NT, 2]); hi_e = sb("hi_e", [P, NT, 2]); ok = sb("ok", [P, NT, 2])
    A = sb("A1", [P, 2, 2, 2, P], BF16); G = sb("G1", [P, 2, 4, NG], BF16); R = sb("R1c", [P, 2, 4, NV, NG], BF16)
    mhi = sb("mhi", [P, NG]); mlo = sb("mlo", [P, NG]); m1 = sb("m1", [P, NG]); m2 = sb("m2", [P, NG])
    gi = sb("gi", [P, NG], U32); si = sb("si", [P, NG], U32)
    XG = sb("XG", [P, NG, D]); XGT = sb("XGT", [P, 2, 4, P]); YB = sb("YB", [P, 2, 4, D])
    YC = sb("YC", [P, 2, 2, 8, D])
    MAP = ctx.enter_context(nc.psum_tensor("MAP", [P, 512], F32))
    TR = [ctx.enter_context(nc.psum_tensor(f"TR{i}", [P, 512], F32)) for i in range(2)]
    EO = [ctx.enter_context(nc.psum_tensor(f"EO{i}", [P, 512], F32)) for i in range(2)]

    val_loaded = sem("val_loaded"); bulk = sem("bulk"); gexp = sem("gexp1"); onehot = sem("onehot")
    told = sem("told"); mapped = sem("mapped"); decoded = sem("decoded"); gathered = [sem(f"gathered{i}") for i in range(8)]
    blank = sem("blank"); transposed = sem("transposed"); tr_copied = sem("tr_copied"); applied = sem("applied"); copied = sem("copied")
    scattered = [sem(f"scattered{i}") for i in range(2)]; y_loaded = [sem(f"y_loaded{i}") for i in range(2)]; half_added = sem("half_added"); added = sem("added")
    stored = sem("stored")

    block = ctx.enter_context(nc.Block())

    @block.sync
    def _(sp):
        sp.dma_start(VAL[:].rearrange("p i c v -> p (i c v)"), dram["c_rowval"]).then_inc(val_loaded, 16)
        yv, ov = y_d.rearrange("(c i p) d -> p c i d", c=2, p=P), out.rearrange("(i p) d -> p i d", p=P)
        for i in range(2):
            sp.wait_ge(scattered[i], 16 * NG // 2)
        for g in range(8):
            if g >= 2:
                sp.wait_ge(added, g - 1)
            for c in range(2):
                sp.dma_start(YC[:, g % 2, c, :, :], yv[:, c, 8 * g:8 * g + 8, :]).then_inc(y_loaded[g % 2], 16)
            if g:
                sp.wait_ge(added, g)
                sp.dma_start(ov[:, 8 * g - 8:8 * g, :], X[:, 8 * g - 8:8 * g, :]).then_inc(stored, 16)
        sp.wait_ge(added, 8)
        sp.dma_start(ov[:, 56:64, :], X[:, 56:64, :]).then_inc(stored, 16)
        sp.wait_ge(stored, 16 * 8)

    @block.tensor
    def _(pe):
        for i in range(NT // 2):
            pe.wait_ge(told, i + 1)
            for k in range(4):
                last = nc.tensor.matmul(MAP[:, 0:NV * NG], A[:, i % 2, k // 2, k % 2, :], R[:, i % 2, k, :, :].rearrange("p v g -> p (v g)"),
                                        start=(i == 0 and k == 0), stop=(i == NT // 2 - 1 and k == 3))
            last.then_inc(mapped, 1)
        for b in range(8):
            pe.wait_ge(gathered[b], 64)
            if b >= 2:
                pe.wait_ge(tr_copied, b - 1)
            for k in range(4):
                last = nc.tensor.transpose(TR[b % 2][:, k * P:(k + 1) * P], XG[:, 4 * b + k, :], ident[:])
            last.then_inc(transposed, 1)
            pe.wait_ge(tr_copied, b + 1)
            if b >= 2:
                pe.wait_ge(copied, b - 1)
            for k in range(4):
                for j in range(4):
                    e = 4 * (4 * b + k) + j
                    last = nc.tensor.matmul(EO[b % 2][32 * j:32 * j + 32, k * P:(k + 1) * P], XGT[:, b % 2, k, 32 * j:32 * j + 32], WE[:, e, :],
                                            start=True, stop=True, tile_position=(0, 32 * j))
            last.then_inc(applied, 1)

    @block.scalar
    def _(act):
        act.wait_ge(bulk, 1)
        nc.scalar.activation(wd[:], wd[:], ACT.Exp).then_inc(gexp, 1)
        for b in range(8):
            act.wait_ge(transposed, b + 1)
            if b >= 2:
                act.wait_ge(applied, b - 1)
            nc.scalar.copy(XGT[:, b % 2].rearrange("p k q -> p (k q)"), TR[b % 2][:]).then_inc(tr_copied, 1)

    @block.gpsimd
    def _(pool):
        pool.wait_ge(val_loaded, 16)
        for i in range(NT // 2):
            if i == 2:
                nc.gpsimd.memset(XG[:], 0.0).then_inc(blank, 1)
            pool.wait_ge(onehot, 2 * i + 2)
            if i >= 2:
                pool.wait_ge(mapped, i - 1)
            val = VAL[:, 2 * i:2 * i + 2, :, :].rearrange("p i c v -> p (i c) v")
            nc.gpsimd.tensor_tensor(R[:, i % 2], G[:, i % 2].unsqueeze(2).to_broadcast([P, 4, NV, NG]),
                                    val.unsqueeze(3).to_broadcast([P, 4, NV, NG]), ALU.mult).then_inc(told, 1)
        pool.wait_ge(decoded, 8)
        pool.wait_ge(blank, 1)
        for b in range(8):
            for k in range(4):
                g = 4 * b + k
                nc.gpsimd.indirect_dma_start(out=XG[:, g, :], out_offset=None, in_=xn_d, in_offset=bass.IndirectOffsetOnAxis(ap=gi[:, g:g + 1], axis=0),
                                             bounds_check=NTOK - 1, oob_is_err=False).then_inc(gathered[b], 16)
        for b in range(8):
            pool.wait_ge(copied, b + 1)
            for k in range(4):
                g = 4 * b + k
                nc.gpsimd.indirect_dma_start(out=y_d, out_offset=bass.IndirectOffsetOnAxis(ap=si[:, g:g + 1], axis=0), in_=YB[:, b % 2, k, :], in_offset=None,
                                             bounds_check=2 * NTOK - 1, oob_is_err=False).then_inc(scattered[b % 2], 16)

    @block.vector
    def _(dve):
        nc.vector.tensor_tensor(wd[:], LG[:, :, 1], LG[:, :, 0], ALU.subtract).then_inc(bulk, 1)
        n = [1]

        def step(ins):
            ins.then_inc(bulk, 1)
            n[0] += 1
            dve.wait_ge(bulk, n[0])

        step(nc.vector.tensor_tensor(LOC[:, :, 1], LOC[:, :, 1], off[:], ALU.add))
        step(nc.vector.tensor_scalar(ok[:], LOC[:], float(CAP) + 0.5, None, ALU.is_lt))
        step(nc.vector.tensor_single_scalar(lo_u[:], EU[:], 3, ALU.bitwise_and))
        step(nc.vector.tensor_single_scalar(hi_u[:], EU[:], 2, ALU.logical_shift_right))
        step(nc.vector.tensor_copy(lo_e[:], lo_u[:]))
        step(nc.vector.tensor_copy(hi_e[:], hi_u[:]))
        step(nc.vector.scalar_tensor_tensor(lo_e[:], lo_e[:], float(CAP), LOC[:], ALU.mult, ALU.add))
        step(nc.vector.tensor_tensor(lo_e[:], lo_e[:], ok[:], ALU.mult))
        step(nc.vector.tensor_scalar(lo_e[:], lo_e[:], -1.0, None, ALU.add))
        for i in range(NT // 2):
            if i >= 2:
                dve.wait_ge(mapped, i - 1)
                dve.wait_ge(told, i - 1)
            def wide(v, m):
                return v[:, 2 * i:2 * i + 2, :].rearrange("p i c -> p (i c)").unsqueeze(2).to_broadcast([P, 4, m])
            nc.vector.tensor_tensor(A[:, i % 2].rearrange("p i c q -> p (i c) q"), iota[:].unsqueeze(1).to_broadcast([P, 4, P]), wide(lo_e, P),
                                    ALU.is_equal).then_inc(onehot, 1)
            nc.vector.tensor_tensor(G[:, i % 2], iota[:, 0:NG].unsqueeze(1).to_broadcast([P, 4, NG]), wide(hi_e, NG), ALU.is_equal).then_inc(onehot, 1)
        dve.wait_ge(mapped, NT // 2)
        m = [0]

        def dstep(ins):
            ins.then_inc(decoded, 1)
            m[0] += 1
            dve.wait_ge(decoded, m[0])

        mv = MAP[:, 0:NV * NG].rearrange("p (v g) -> p v g", v=NV)
        dstep(nc.vector.tensor_scalar(mhi[:], mv[:, 0, :], -1.0, float(P), ALU.add, ALU.mult))
        dstep(nc.vector.tensor_tensor(mlo[:], mhi[:], mv[:, 1, :], ALU.add))
        dstep(nc.vector.tensor_scalar(m1[:], mv[:, 0, :], 0.5, FAR, ALU.is_lt, ALU.mult))
        dstep(nc.vector.tensor_tensor(mlo[:], mlo[:], m1[:], ALU.add))
        dstep(nc.vector.tensor_copy(si[:], mlo[:]))
        dstep(nc.vector.tensor_scalar(m2[:], mv[:, 0, :], NT + 0.5, -float(NTOK), ALU.is_gt, ALU.mult))
        dstep(nc.vector.tensor_tensor(mlo[:], mlo[:], m2[:], ALU.add))
        dstep(nc.vector.tensor_copy(gi[:], mlo[:]))
        dve.wait_ge(gexp, 1)
        step(nc.vector.tensor_scalar(W[:, :, 0], wd[:], 1.0, None, ALU.add))
        step(nc.vector.reciprocal(W[:, :, 0], W[:, :, 0]))
        step(nc.vector.tensor_tensor(W[:, :, 1], wd[:], W[:, :, 0], ALU.mult))
        for b in range(8):
            dve.wait_ge(applied, b + 1)
            if b >= 2:
                dve.wait_ge(scattered[b % 2], 64 * (b // 2))
            nc.vector.tensor_copy(YB[:, b % 2], EO[b % 2][:].rearrange("p (k d) -> p k d", k=4)).then_inc(copied, 1)
        for g in range(8):
            dve.wait_ge(y_loaded[g % 2], 32 * (g // 2 + 1))
            for c in range(2):
                if c:
                    dve.wait_ge(half_added, g + 1)
                for i in range(8):
                    x = X[:, 8 * g + i, :]
                    last = nc.vector.scalar_tensor_tensor(x, YC[:, g % 2, c, i, :], W[:, 8 * g + i, c:c + 1], x, ALU.mult, ALU.add)
                last.then_inc(added if c else half_added, 1)


def constants():
    bf16 = np.dtype("bfloat16")
    c = {}
    c["c_ident"] = np.eye(P, dtype=np.float32)
    c["c_identb"] = np.eye(P).astype(bf16)
    sel = np.zeros((3 * S, S, P), np.float32)
    for r in range(3):
        for n in range(S):
            sel[S * r + n, n, :] = 1
    c["c_sel"] = sel.reshape(3 * S, -1).astype(bf16)
    c["c_tri8"] = np.tile(np.tril(np.ones((E0, E0), np.float32)).reshape(1, -1), (P, 1))
    split = np.zeros((P, 2), np.float32)
    split[S:3 * S, 0] = -1
    split[2 * S:3 * S, 1] = -1
    c["c_split"] = split
    dim = DH // 2
    inv = (1.0 / np.float32(10000.0) ** (np.arange(0, dim, 2, dtype=np.float32) / np.float32(dim))).astype(np.float32)
    freqs = np.arange(L, dtype=np.float32)[:, None] * inv[None, :]
    emb = np.concatenate((freqs, freqs), axis=-1)
    cos, sin = np.ones((HEADS, DH, L), np.float32), np.zeros((HEADS, DH, L), np.float32)
    cos[:, dim:, :] = np.cos(emb).T
    sin[:, dim:, :] = (np.sin(emb) * np.array([-1, 1] * (dim // 2), np.float32)).T
    c["c_cos"], c["c_sin"] = cos.reshape(P, L), sin.reshape(P, L)
    q = np.where(np.arange(P)[None, :] <= np.arange(P)[:, None], 0, -1e30).astype(np.float32)
    c["c_maskq"], c["c_maskk"] = np.tile(q, (1, HG)).astype(bf16), np.tile(q.T, (1, HG)).astype(bf16)
    c["c_tri"] = np.triu(np.ones((P, P), np.float32)).astype(bf16)
    c["c_iota"] = np.tile(np.arange(P, dtype=np.float32), (P, 1))
    row = np.zeros((P, NT, 2, 2), np.float32)
    row[:, :, :, 0] = np.arange(NT)[None, :, None] + NT * np.arange(2)[None, None, :] + 1
    row[:, :, :, 1] = np.arange(P)[:, None, None]
    c["c_rowval"] = row.reshape(P, -1).astype(bf16)
    return c


def build(nc, dram, out):
    def scr(name, shape, dt):
        return nc.dram_tensor(name, shape, dt, kind="Internal").ap()

    scratch = {
        "xn": scr("s_xn", [NTOK, D], F32), "y": scr("s_y", [2 * NTOK, D], F32),
        "parts": [scr(f"s_parts{i}", [P, 3 * 2 * L], BF16) for i in range(2)],
        "b": [scr(f"s_b{i}", [S, T0], F32) for i in range(2)],
        "nm": [scr(f"s_nm{i}", [3 * HEADS, L], BF16) for i in range(2)],
    }
    with ExitStack() as ctx:
        def sb(name, shape, dt=F32):
            return ctx.enter_context(nc.sbuf_tensor(name, shape, dt))

        U32 = mybir.dt.uint32
        t = {"X": sb("X", [P, NT, D]), "ident": sb("ident", [P, P]), "identb": sb("identb", [P, P], BF16),
             "stats": sb("stats", [P, NT, 6]), "wvg": sb("wvg", [P, 2 * P])}
        for name in ("wq", "wk", "wqr", "wkr"):
            t[name] = sb(name, [P, P])
        with ExitStack() as c0:
            layer0(nc, c0, t, dram, scratch["b"])
        t.update(WE=sb("WE", [P, E1, D]), carry=sb("carry", [P, 2, P]), EF=sb("EF", [P, NT, 2]), EU=sb("EU", [P, NT, 2], U32),
                 LG=sb("LG", [P, NT, 2]), LOC=sb("LOC", [P, NT, 2]), off=sb("off", [P, NT]), iota=sb("iota", [P, P]))
        with ExitStack() as c1:
            layer1(nc, c1, t, dram, scratch)
        with ExitStack() as c2:
            experts1(nc, c2, t, dram, scratch, out)


_INS = ['L0_attn_x', 'L0_attn_rms_w', 'L0_attn_in_proj', 'L0_attn_conv_w', 'L0_attn_conv_b', 'L0_attn_x_proj', 'L0_attn_dt_w',
        'L0_attn_dt_b', 'L0_attn_A_log', 'L0_attn_D', 'L0_attn_out_proj', 'L0_ffn_Wr', 'L0_ffn_br', 'L0_ffn_W1', 'L0_ffn_b1',
        'L0_ffn_W2', 'L0_ffn_b2', 'L1_attn_Wq_down', 'L1_attn_Wk_down', 'L1_attn_Wv_down', 'L1_attn_Wq_up_c', 'L1_attn_Wq_up_e',
        'L1_attn_Wk_up_c', 'L1_attn_Wk_up_e', 'L1_attn_Wv_up', 'L1_attn_Wc', 'L1_ffn_wg', 'L1_ffn_we']


def kernel(**inputs):
    import concourse.bacc as bacc
    from concourse.bass_utils import run_bass_kernel_spmd

    nc = bacc.Bacc("TRN2", target_bir_lowering=False, num_devices=1)
    given = {name: np.ascontiguousarray(inputs[name]) for name in _INS}
    given.update(constants())
    arrays, dram = {}, {}
    for name, a in given.items():
        arrays[f"in_{name}"] = a
        dram[name] = nc.dram_tensor(f"in_{name}", a.shape, mybir.dt.from_np(a.dtype), kind="ExternalInput").ap()
    out = nc.dram_tensor("out_0", (NTOK, D), F32, kind="ExternalOutput").ap()
    build(nc, dram, out)
    r = run_bass_kernel_spmd(nc, [arrays], core_ids=[0])
    return r.results[0]["out_0"].reshape(NTOK // L, L, D)
```
